# Optimizing a Trainium2 kernel written in Bass

```python
import numpy as np
import jax
import jax.numpy as jnp

def _softmax(x, axis=-1):
    return jax.nn.softmax(x, axis=axis)

def _gelu(x):
    return jax.nn.gelu(x, approximate=True)

def _silu(x):
    return jax.nn.silu(x)

def _sigmoid(x):
    return jax.nn.sigmoid(x)

def _layernorm(x, axis=-1, eps=1e-05):
    m = jnp.mean(x, axis=axis, keepdims=True)
    v = jnp.var(x, axis=axis, keepdims=True)
    return (x - m) / jnp.sqrt(v + eps)

def _scatter_add(tgt, idx, src, axis=0):
    return tgt.at[idx].add(src)

def _segment_sum(src, seg, n):
    return jax.ops.segment_sum(src, seg, n)
kernel_name = 'mk_adaln_d1_jaxref_r2_d6423a'

def setup_inputs(seed: int=0):
    np.random.seed(seed)
    _w = jnp.asarray

    def _L0_attn_setup():
        import jax, jax.numpy as jnp
        import numpy as np
        EMBED = 512
        EXPAND = 128
        B, T = (4, 1024)
        PI = 3.141592653589793
        EPS = 1e-05

        def _gla_scan(q, k, v, g):
            Bq, Tq, H, Dk = q.shape
            Dv = v.shape[-1]
            scale = Dk ** (-0.5)

            def step(S, inp):
                qt, kt, vt, gt = inp
                S = S * jnp.exp(gt)[..., None] + kt[..., None] * vt[..., None, :]
                o = jnp.einsum('bhk,bhkv->bhv', qt * scale, S)
                return (S, o)
            S0 = jnp.zeros((Bq, H, Dk, Dv), q.dtype)
            seq = tuple((jnp.moveaxis(a, 1, 0) for a in (q, k, v, g)))
            _, out = jax.lax.scan(step, S0, seq)
            return jnp.moveaxis(out, 0, 1)
        key = jax.random.key(seed)
        ks = jax.random.split(key, 8)
        std = 0.02
        return {'x': jax.random.normal(ks[0], (B, T, EMBED), jnp.float32), 'wq': jax.random.normal(ks[1], (EMBED, EMBED), jnp.float32) * std, 'wk': jax.random.normal(ks[2], (EMBED, EMBED), jnp.float32) * std, 'wv': jax.random.normal(ks[3], (EMBED, EMBED), jnp.float32) * std, 'wo': jax.random.normal(ks[4], (EMBED, EMBED), jnp.float32) * std, 'wg1': jax.random.normal(ks[5], (EMBED, EXPAND), jnp.float32) * std, 'wg2': jax.random.normal(ks[6], (EXPAND, EMBED), jnp.float32) * std, 'norm_w': jnp.ones((EMBED,), jnp.float32)}
    _L0_attn_in = _L0_attn_setup()

    def _L0_ffn_setup():
        import jax, jax.numpy as jnp
        import numpy as np
        DIM = 512

        def _reference_tuple_inner(x, W_r, W_k, W_v, mu_r, mu_k):
            B, T, C = x.shape
            x_prev = jnp.concatenate([jnp.zeros((B, 1, C), x.dtype), x[:, :-1, :]], axis=1)
            xr = mu_r * x + (1.0 - mu_r) * x_prev
            xk = mu_k * x + (1.0 - mu_k) * x_prev
            r = jax.nn.sigmoid(jnp.einsum('btc,dc->btd', xr, W_r))
            k = jnp.einsum('btc,dc->btd', xk, W_k)
            k_act = jnp.square(jax.nn.relu(k))
            out = r * jnp.einsum('btc,dc->btd', k_act, W_v)
            new_state = x[:, -1, :]
            return (out, new_state)
        key = jax.random.key(seed)
        ks = jax.random.split(key, 6)
        B, T, C = (8, 1024, DIM)
        x = jax.random.normal(ks[0], (B, T, C), dtype=jnp.float32)
        s = 1.0 / np.sqrt(C)
        W_r = jax.random.uniform(ks[1], (C, C), jnp.float32, -s, s)
        W_k = jax.random.uniform(ks[2], (C, C), jnp.float32, -s, s)
        W_v = jax.random.uniform(ks[3], (C, C), jnp.float32, -s, s)
        mu_r = jax.random.uniform(ks[4], (C,), jnp.float32)
        mu_k = jax.random.uniform(ks[5], (C,), jnp.float32)
        return {'x': x, 'W_r': W_r, 'W_k': W_k, 'W_v': W_v, 'mu_r': mu_r, 'mu_k': mu_k}
    _L0_ffn_in = _L0_ffn_setup()
    _L0_c = _w((lambda *s: np.random.randn(*s).astype(np.float32) * 0.05)(2, 512))
    _L0_wmod = _w((lambda *s: np.random.randn(*s).astype(np.float32) * 0.05)(512, 6 * 512) * 512 ** (-0.5))
    _d = {'L0_attn_x': _L0_attn_in['x'], 'L0_attn_wq': _L0_attn_in['wq'], 'L0_attn_wk': _L0_attn_in['wk'], 'L0_attn_wv': _L0_attn_in['wv'], 'L0_attn_wo': _L0_attn_in['wo'], 'L0_attn_wg1': _L0_attn_in['wg1'], 'L0_attn_wg2': _L0_attn_in['wg2'], 'L0_attn_norm_w': _L0_attn_in['norm_w'], 'L0_ffn_W_r': _L0_ffn_in['W_r'], 'L0_ffn_W_k': _L0_ffn_in['W_k'], 'L0_ffn_W_v': _L0_ffn_in['W_v'], 'L0_ffn_mu_r': _L0_ffn_in['mu_r'], 'L0_ffn_mu_k': _L0_ffn_in['mu_k'], 'L0_c': _L0_c, 'L0_wmod': _L0_wmod}
    _x0 = _d['L0_attn_x']
    _d['L0_attn_x'] = jax.random.normal(jax.random.fold_in(jax.random.key(seed), 1), (2, 4096, 512), dtype=_x0.dtype)
    del _x0
    return _d

def reference(L0_attn_x, L0_attn_wq, L0_attn_wk, L0_attn_wv, L0_attn_wo, L0_attn_wg1, L0_attn_wg2, L0_attn_norm_w, L0_ffn_W_r, L0_ffn_W_k, L0_ffn_W_v, L0_ffn_mu_r, L0_ffn_mu_k, L0_c, L0_wmod):

    def _L0_attn_ref(x, wq, wk, wv, wo, wg1, wg2, norm_w):
        import jax, jax.numpy as jnp
        import numpy as np
        EMBED = 512
        EXPAND = 128
        B, T = (4, 1024)
        PI = 3.141592653589793
        EPS = 1e-05

        def _gla_scan(q, k, v, g):
            Bq, Tq, H, Dk = q.shape
            Dv = v.shape[-1]
            scale = Dk ** (-0.5)

            def step(S, inp):
                qt, kt, vt, gt = inp
                S = S * jnp.exp(gt)[..., None] + kt[..., None] * vt[..., None, :]
                o = jnp.einsum('bhk,bhkv->bhv', qt * scale, S)
                return (S, o)
            S0 = jnp.zeros((Bq, H, Dk, Dv), q.dtype)
            seq = tuple((jnp.moveaxis(a, 1, 0) for a in (q, k, v, g)))
            _, out = jax.lax.scan(step, S0, seq)
            return jnp.moveaxis(out, 0, 1)
        Bx, Tx, E = x.shape
        d = EXPAND
        H = E // d
        q = jax.nn.silu(x @ wq)
        k = jax.nn.sigmoid(x @ wk)
        v = x @ wv
        f = 1.0 - k
        log_f = jnp.log(f)
        q4 = q.reshape(Bx, Tx, H, d)
        k4 = k.reshape(Bx, Tx, H, d)
        v4 = v.reshape(Bx, Tx, H, d)
        f4 = f.reshape(Bx, Tx, H, d)
        g4 = log_f.reshape(Bx, Tx, H, d)
        sign_f = jnp.sign(f4 - 0.5)
        theta = jnp.cumsum(sign_f, axis=1) * PI
        sin, cos = (jnp.sin(theta), jnp.cos(theta))
        qr = jnp.concatenate([q4 * cos, q4 * sin], axis=-1)
        kr = jnp.concatenate([k4 * cos, k4 * sin], axis=-1)
        g = jnp.concatenate([g4, g4], axis=-1)
        out = _gla_scan(qr, kr, v4, g)
        out = out.reshape(Bx, Tx, E)
        gate = jax.nn.sigmoid(x @ wg1 @ wg2)
        out = out * gate
        mu = jnp.mean(out, axis=-1, keepdims=True)
        var = jnp.mean(jnp.square(out - mu), axis=-1, keepdims=True)
        out = (out - mu) * jax.lax.rsqrt(var + EPS) * norm_w
        return out @ wo

    def _L0_ffn_ref(x, W_r, W_k, W_v, mu_r, mu_k):
        import jax, jax.numpy as jnp
        import numpy as np
        DIM = 512

        def _reference_tuple_inner(x, W_r, W_k, W_v, mu_r, mu_k):
            B, T, C = x.shape
            x_prev = jnp.concatenate([jnp.zeros((B, 1, C), x.dtype), x[:, :-1, :]], axis=1)
            xr = mu_r * x + (1.0 - mu_r) * x_prev
            xk = mu_k * x + (1.0 - mu_k) * x_prev
            r = jax.nn.sigmoid(jnp.einsum('btc,dc->btd', xr, W_r))
            k = jnp.einsum('btc,dc->btd', xk, W_k)
            k_act = jnp.square(jax.nn.relu(k))
            out = r * jnp.einsum('btc,dc->btd', k_act, W_v)
            new_state = x[:, -1, :]
            return (out, new_state)
        return _reference_tuple_inner(x, W_r, W_k, W_v, mu_r, mu_k)[0]
    x = L0_attn_x
    mod = (_silu(L0_c) @ L0_wmod).reshape(L0_c.shape[0], 6, 1, -1)
    sa, ca, ga, sb, cb, gb = (mod[:, 0], mod[:, 1], mod[:, 2], mod[:, 3], mod[:, 4], mod[:, 5])
    ga = (2 * (ga >= 0) - 1) * jnp.maximum(jnp.abs(ga), 0.25)
    gb = (2 * (gb >= 0) - 1) * jnp.maximum(jnp.abs(gb), 0.25)
    h = _layernorm(x, axis=-1) * (1 + ca) + sa
    x = x + ga * _L0_attn_ref(h, L0_attn_wq, L0_attn_wk, L0_attn_wv, L0_attn_wo, L0_attn_wg1, L0_attn_wg2, L0_attn_norm_w)
    h = _layernorm(x, axis=-1) * (1 + cb) + sb
    x = x + gb * _L0_ffn_ref(h, L0_ffn_W_r, L0_ffn_W_k, L0_ffn_W_v, L0_ffn_mu_r, L0_ffn_mu_k)
    return x

_drawn_inputs = setup_inputs


def setup_inputs(seed=0):
    import zlib

    import numpy as np

    out = dict(_drawn_inputs(seed))
    spreads = {'L0_attn_norm_w': (1.0, 0.6)}
    factors = {'L0_attn_wk': 4.746,
     'L0_attn_wg1': 8.0,
     'L0_attn_wg2': 8.0,
     'L0_ffn_W_r': 8.0,
     'L0_ffn_W_k': 3.065,
     'L0_ffn_W_v': 2.79,
     'L0_ffn_mu_r': 8.0,
     'L0_ffn_mu_k': 5.051}
    for name, (base, spread) in spreads.items():
        noise = np.random.default_rng([zlib.crc32(name.encode()), seed]).standard_normal(out[name].shape)
        drawn = base * np.exp(spread * noise) if base else spread * noise
        out[name] = jnp.asarray(drawn.astype(out[name].dtype))
    for name, factor in factors.items():
        out[name] = (out[name] * factor).astype(out[name].dtype)
    return out
```

```python
import concourse.bass as bass
from concourse import mybir
from contextlib import ExitStack

F32 = mybir.dt.float32
F32R = mybir.dt.float32r
I32 = mybir.dt.int32
ALU = mybir.AluOpType
ACT = mybir.ActivationFunctionType

P = 128
B, T, E = 2, 4096, 512
H = 4
KT = E // P
TB = 256
NC = TB // P
NB = B * T // TB
BPB = NB // B
G = H * NC
LEVELS = [1, 2, 4, 8, 16, 32, 64]
NL = len(LEVELS) + 1
EPS = 1e-5
FLOOR = 0.25
QSCALE = float(2 * P) ** -0.5
XS = 4


def adaln_kernel(nc, x, wq, wk, wv, wo, wg1, wg2, norm_w, W_r, W_k, W_v, mu_r, mu_k, c, wmod, out):
    xf = x.rearrange("b t e -> (b t) e")
    of = out.rearrange("b t e -> (b t) e")
    x2d = nc.dram_tensor("x2_scratch", (B * T, E), F32, kind="Internal").ap()

    def sb(ctx, name, shape, dt=F32):
        return ctx.enter_context(nc.sbuf_tensor(name, shape, dt))

    def sem(ctx, name):
        return ctx.enter_context(nc.semaphore(name))

    def wait(eng, s, value):
        if not isinstance(value, int) or value > 0:
            eng.wait_ge(s, value)

    with ExitStack() as top:
        bank = [top.enter_context(nc.psum_tensor(f"bank{n}", [P, 512], F32)) for n in range(6)]
        lvl2 = top.enter_context(nc.psum_tensor("lvl2", [P, 1024], F32))
        lbank = [lvl2[:, 0:512], lvl2[:, 512:1024]]

        ident = sb(top, "ident", [P, P])
        flags = sb(top, "flags", [P, NB + 1])
        mhalf = sb(top, "mhalf", [P, NC])
        scl = [sb(top, f"scl{n}", [P, NB, KT]) for n in range(2)]
        sft = [sb(top, f"sft{n}", [P, NB, KT]) for n in range(2)]
        gab = sb(top, "gab", [P, 2 * B, E])
        vec = sb(top, "vec", [P, (B + 3) * KT])
        ffn_raw = [sb(top, f"ffn_raw{n}", [P, KT, E]) for n in range(2)]
        w_in = sem(top, "w_in")

        attn = ExitStack()
        W = {}
        for name, kt, n in (("q", KT, E), ("k", KT, E), ("v", KT, E), ("o", KT, E), ("g1", KT, P), ("g2", 1, E)):
            W[name] = [sb(attn, f"w{name}_{part}", [P, kt, n], F32R) for part in ("hi", "lo")]
        masks = sb(attn, "masks", [P, 5, 64], I32)
        diag = ident

        setup(nc, sb, sem, locals())
        attend(nc, sb, sem, wait, locals())
        attn.close()
        ffn(nc, sb, sem, wait, locals())


def setup(nc, sb, sem, env):
    bank, ident, flags, mhalf, masks = (env[n] for n in ("bank", "ident", "flags", "mhalf", "masks"))
    scl, sft, gab, W = env["scl"], env["sft"], env["gab"], env["W"]
    wmod, c = env["wmod"], env["c"]
    with ExitStack() as ctx:
        mod_raw = sb(ctx, "mod_raw", [P, 6, KT, E])
        raw = {n: sb(ctx, f"raw_{n}", [P, KT, E]) for n in "qkvo"}
        raw["g1"] = sb(ctx, "raw_g1", [P, KT, P])
        raw["g2"] = sb(ctx, "raw_g2", [P, 1, E])
        csig = sb(ctx, "csig", [P, B * KT])
        csil = sb(ctx, "csil", [P, B, KT])
        cbc = sb(ctx, "cbc", [P, B * KT, P])
        vrows = sb(ctx, "vrows", [(B + 3) * KT, P])
        cT, nw = env["vec"][:, 0:B * KT], env["vec"][:, B * KT:(B + 1) * KT]
        mean_m = sb(ctx, "mean_m", [P, P])
        mcol = sb(ctx, "mcol", [P, 4, KT, B])
        gmag = sb(ctx, "gmag", [P, 2 * B, E])
        maskf = sb(ctx, "maskf", [P, 5, 64])

        small_in, vec_turned, vec_sb, mod_in = sem(ctx, "small_in"), sem(ctx, "vec_turned"), sem(ctx, "vec_sb"), [sem(ctx, f"mod_in{n}") for n in range(6)]
        raw_in = {n: sem(ctx, f"raw_in_{n}") for n in ("q", "k", "v", "o", "g1", "g2")}
        sig_ready, silu_ready, cols_ready, gates_raw = (sem(ctx, n) for n in ("sig_ready", "silu_ready", "cols_ready", "gates_raw"))
        const_set, step_pool = sem(ctx, "const_set"), sem(ctx, "step_pool")
        gcopy, mcopy, mag, hi_done, wo_scaled, mean_ready, wo_centred = (
            sem(ctx, n) for n in ("gcopy", "mcopy", "mag", "hi_done", "wo_scaled", "mean_ready", "wo_centred"))
        order = ["q", "k", "v", "g1", "g2", "o"]
        VECS = [1, 0, 4, 3]

        with nc.Block() as block:
            @block.sync
            def _(sp):
                sp.dma_start(vrows[0:B * KT, :], c.rearrange("b (k p) -> (b k) p", p=P)).then_inc(small_in, 16)
                for n, src in enumerate((env["norm_w"], env["mu_r"], env["mu_k"])):
                    sp.dma_start(vrows[(B + n) * KT:(B + n + 1) * KT, :], src.rearrange("(k p) -> k p", p=P)).then_inc(small_in, 16)
                for v in (0, 1, 2, 3, 4, 5):
                    sp.dma_start(mod_raw[:, v, :, :], wmod[:, v * E:(v + 1) * E].rearrange("(k p) n -> p k n", p=P)
                                 ).then_inc(mod_in[v], 16)

            @block.scalar
            def _(act):
                for n, src in (("q", env["wq"]), ("k", env["wk"]), ("v", env["wv"]), ("o", env["wo"]),
                               ("g1", env["wg1"]), ("g2", env["wg2"])):
                    act.dma_start(raw[n][:, :, :], src.rearrange("(k p) n -> p k n", p=P)).then_inc(raw_in[n], 16)
                act.wait_ge(vec_sb, 1)
                act.activation(csig[:, :], cT, ACT.Sigmoid).then_inc(sig_ready, 1)

            @block.gpsimd
            def _(pool):
                pool.memset(ident[:, :], 0.0).then_inc(step_pool, 1)
                pool.memset(maskf[:, :, :], 1.0).then_inc(step_pool, 1)
                pool.memset(flags[:, :], 1.0).then_inc(step_pool, 1)
                pool.memset(mhalf[:, :], -0.5)
                pool.memset(mean_m[:, :], 1.0 / E).then_inc(const_set, 1)
                pool.wait_ge(step_pool, 3)
                for b in range(B):
                    pool.memset(flags[:, b * BPB:b * BPB + 1], 0.0)
                pool.affine_select(out=ident[:, :], in_=ident[:, :], compare_op=ALU.not_equal, fill=1.0,
                                   base=0, pattern=[[-1, P]], channel_multiplier=1).then_inc(const_set, 1)
                for n, m in enumerate(LEVELS[:5]):
                    nb = 64 // m
                    view = maskf[:, n, :].rearrange("p (n m) -> p n m", m=m)
                    pool.affine_select(out=view, in_=view, compare_op=ALU.is_ge, fill=0.0, base=0,
                                       pattern=[[-2 * m, nb], [0, m]], channel_multiplier=1).then_inc(step_pool, 1)
                    pool.wait_ge(step_pool, 4 + 2 * n)
                    pool.affine_select(out=view, in_=view, compare_op=ALU.is_ge, fill=0.0, base=m - 1,
                                       pattern=[[2 * m, nb], [0, m]], channel_multiplier=-1).then_inc(step_pool, 1)

            @block.vector
            def _(dve):
                dve.wait_ge(vec_turned, 1)
                dve.tensor_copy(env["vec"][:, :], bank[5][:, 0:(B + 3) * KT]).then_inc(vec_sb, 1)
                dve.wait_ge(sig_ready, 1)
                dve.tensor_tensor(out=csil[:, :, :].rearrange("p b k -> p (b k)"), in0=cT, in1=csig[:, :], op=ALU.mult).then_inc(silu_ready, 1)
                dve.wait_ge(silu_ready, 1)
                dve.tensor_copy(cbc[:, :, :], csil[:, :, :].rearrange("p b k -> p (b k)").unsqueeze(2)
                                .to_broadcast([P, B * KT, P])).then_inc(silu_ready, 1)
                def split(name, src):
                    hi, lo = W[name]
                    dve.tensor_copy(hi[:, :, :], src[:, :, :]).then_inc(hi_done, 1)
                    dve.wait_ge(hi_done, order.index(name) + 1)
                    dve.tensor_tensor(out=lo[:, :, :], in0=src[:, :, :], in1=hi[:, :, :].bitcast(F32), op=ALU.subtract)
                for name in order[:-1]:
                    dve.wait_ge(raw_in[name], 16)
                    split(name, raw[name])
                dve.wait_ge(raw_in["o"], 16)
                for k in range(KT):
                    last = dve.tensor_scalar(raw["o"][:, k, :], raw["o"][:, k, :], nw[:, k:k + 1], None, ALU.mult)
                last.then_inc(wo_scaled, 1)
                dve.wait_ge(mean_ready, 1)
                dve.tensor_copy(gmag[:, 0, :], bank[5][:, :]).then_inc(wo_scaled, 1)
                dve.wait_ge(wo_scaled, 2)
                dve.tensor_tensor(out=raw["o"][:, :, :], in0=raw["o"][:, :, :],
                                  in1=gmag[:, 0:1, :].to_broadcast([P, KT, E]), op=ALU.subtract).then_inc(wo_centred, 1)
                dve.wait_ge(wo_centred, 1)
                split("o", raw["o"])
                dve.wait_ge(cols_ready, 1)
                dve.tensor_copy(mcol[:, :, :, :].rearrange("p v k b -> p (v k b)"), bank[0][:, 0:4 * KT * B]).then_inc(mcopy, 1)
                dve.wait_ge(mcopy, 1)
                for n in range(2):
                    for b in range(B):
                        rows = slice(b * BPB, (b + 1) * BPB)
                        dve.tensor_scalar(scl[n][:, rows, :], mcol[:, 2 * n:2 * n + 1, :, b].to_broadcast([P, BPB, KT]),
                                          1.0, None, ALU.add)
                        dve.tensor_copy(sft[n][:, rows, :], mcol[:, 2 * n + 1:2 * n + 2, :, b].to_broadcast([P, BPB, KT]))
                dve.wait_ge(gates_raw, 2 * B)
                for n in range(2 * B):
                    last = dve.tensor_copy(gab[:, n, :], bank[1 + n][:, :])
                last.then_inc(gcopy, 1)
                dve.wait_ge(gcopy, 1)
                dve.scalar_tensor_tensor(out=gmag[:, :, :], in0=gab[:, :, :], scalar=-1.0, in1=gab[:, :, :],
                                         op0=ALU.mult, op1=ALU.max).then_inc(mag, 1)
                dve.wait_ge(mag, 1)
                dve.tensor_scalar(gmag[:, :, :], gmag[:, :, :], FLOOR, None, ALU.max).then_inc(mag, 1)
                dve.tensor_scalar(gab[:, :, :], gab[:, :, :], 0.0, 2.0, ALU.is_ge, ALU.mult).then_inc(mag, 1)
                dve.wait_ge(mag, 3)
                dve.scalar_tensor_tensor(out=gab[:, :, :], in0=gab[:, :, :], scalar=-1.0, in1=gmag[:, :, :],
                                         op0=ALU.add, op1=ALU.mult)
                dve.wait_ge(step_pool, 3 + 2 * 5)
                dve.tensor_copy(masks[:, :, :], maskf[:, :, :])

            @block.tensor
            def _(pe):
                pe.wait_ge(const_set, 2)
                pe.wait_ge(small_in, 64)
                rows = (B + 3) * KT
                pe.transpose(bank[5][:, 0:rows], vrows[:, :], ident[0:rows, 0:rows]).then_inc(vec_turned, 1)
                pe.wait_ge(silu_ready, 2)
                for v in range(6):
                    pe.wait_ge(mod_in[v], 16)
                for n, v in enumerate(VECS):
                    for t in range(KT):
                        col = (n * KT + t) * B
                        for k in range(KT):
                            last = pe.matmul(bank[0][:, col:col + B], mod_raw[:, v, k, t * P:(t + 1) * P], csil[:, :, k],
                                             start=(k == 0), stop=(k == KT - 1))
                last.then_inc(cols_ready, 1)
                for n, v in enumerate((2, 5)):
                    for b in range(B):
                        for k in range(KT):
                            last = pe.matmul(bank[1 + n * B + b][:, :], cbc[:, b * KT + k, :], mod_raw[:, v, k, :],
                                             start=(k == 0), stop=(k == KT - 1))
                        last.then_inc(gates_raw, 1)
                pe.wait_ge(wo_scaled, 1)
                for k in range(KT):
                    last = pe.matmul(bank[5][:, :], mean_m[:, :], raw["o"][:, k, :], start=(k == 0), stop=(k == KT - 1))
                last.then_inc(mean_ready, 1)


def attend(nc, sb, sem, wait, env):
    bank, lvl2, lbank, ident, flags, mhalf, masks = (env[n] for n in ("bank", "lvl2", "lbank", "ident", "flags", "mhalf", "masks"))
    W, gab, scl, sft, xf, x2d = (env[n] for n in ("W", "gab", "scl", "sft", "xf", "x2d"))
    ffn_raw, w_in = env["ffn_raw"], env["w_in"]
    with ExitStack() as ctx:
        xs = sb(ctx, "xs", [P, XS, NC * E])
        tick = sb(ctx, "tick", [P, 1])
        ticked = sem(ctx, "ticked")
        xn = sb(ctx, "xn", [P, NC, E])
        hF = sb(ctx, "hF", [P, KT, TB])
        hT = [sb(ctx, f"hT_{part}", [P, KT, TB], F32R) for part in ("hi", "lo")]
        Q = [sb(ctx, f"Q{n}", [P, G, P]) for n in range(2)]
        K = [sb(ctx, f"K{n}", [P, G, P]) for n in range(2)]
        f = [sb(ctx, "f", [P, G, P])] * 2
        V = [sb(ctx, f"V{n}", [P, NC, E]) for n in range(2)]
        og = [sb(ctx, f"og{n}", [P, NC, E]) for n in range(2)]
        g1 = [sb(ctx, f"g1_{part}", [P, TB], F32R) for part in ("hi", "lo")]
        eq = sb(ctx, "eq", [P, E])
        Tot = sb(ctx, "Tot", [P, G * P])
        A = sb(ctx, "A", [P, G, P])
        Kt = sb(ctx, "Kt", [P, NC, H, P])
        S = [sb(ctx, f"S{n}", [P, H, P]) for n in range(NC)]
        ogT = [sb(ctx, f"ogT_{part}", [P, NC, KT, P], F32R) for part in ("hi", "lo")]
        y = sb(ctx, "y", [P, NC, E])
        st1 = sb(ctx, "st1", [P, NC, 6])
        mv1 = sb(ctx, "mv1", [P, NC, 2])
        ve1 = sb(ctx, "ve1", [P, NC])
        rs1 = sb(ctx, "rs1", [P, NC])
        sto = sb(ctx, "sto", [P, NC, 6])
        mvo = sb(ctx, "mvo", [P, NC, 2])
        veo = sb(ctx, "veo", [P, NC])
        rso = sb(ctx, "rso", [P, NC])

        x_in = [sem(ctx, f"x_in{n}") for n in range(2)]
        x_out = [sem(ctx, f"x_out{n}") for n in range(2)]
        mm = {n: sem(ctx, f"mm_{n}") for n in ("t1", "q", "k", "v", "g1", "gate", "lvl", "kt", "o", "ds", "t2", "wo")}
        h_full, q_sig, k_f, v_sb, g1_hi, gate_sb, kt_sb, ogt_hi, merged_act = (
            sem(ctx, n) for n in ("h_full", "q_sig", "k_f", "v_sb", "g1_hi", "gate_sb", "kt_sb", "ogt_hi", "merged_act"))
        h_hi, q_sb, f_eq, f_sb, level, merged, g1_lo, ogt_lo, stat1, var1, xn_sb, s_mid, s_new, og_sb, sto_s, varo, y_sb, s_flag = (
            sem(ctx, n) for n in ("h_hi", "q_sb", "f_eq", "f_sb", "level", "merged", "g1_lo", "ogt_lo", "stat1", "var1", "xn_sb",
                                  "s_mid", "s_new", "og_sb", "sto_s", "varo", "y_sb", "s_flag"))
        ve_1, rstd1, ve_o, rstdo, h_lo, x2_sb = (sem(ctx, n) for n in ("ve_1", "rstd1", "ve_o", "rstdo", "h_lo", "x2_sb"))

        def run(eng, start, body):
            start()
            body(0, 0, True, True, False)
            body(0, 1, True, True, True)
            with eng.Fori(1, NB // 2 - 1) as half:
                body(half, 0, True, True, True)
                body(half, 1, True, True, True)
            body(NB // 2 - 1, 0, True, False, True)
            body(NB // 2 - 1, 1, False, False, True)

        def slot(n):
            return bass.ds(n % XS, 1)

        def rows(n):
            return bass.ds(n * TB, TB)

        with nc.Block() as block:
            @block.sync
            def _(sp):
                def load(n, half, par):
                    wait(sp, stat1, n - 1)
                    sp.dma_start(xs[:, slot(n), :].rearrange("p a (c e) -> p (a c) e", c=NC),
                                 xf[rows(n), :].rearrange("(c p) e -> p c e", p=P)).then_inc(x_in[par], 16)

                def start():
                    for n in range(2):
                        load(n, 0, n)

                def store(n, half, par):
                    wait(sp, x2_sb, 2 * (n + 1))
                    sp.dma_start(x2d[rows(n), :].rearrange("(c p) e -> p c e", p=P),
                                 xs[:, slot(n), :].rearrange("p a (c e) -> p (a c) e", c=NC)).then_inc(x_out[par], 16)

                def body(half, par, has_next, has_next2, has_prev):
                    n = 2 * half + par
                    if has_next2:
                        wait(sp, x_out[par], 16 * half)
                        load(n + 2, None, par)
                    if has_prev:
                        store(n - 1, None, 1 - par)

                run(sp, start, body)
                store(NB - 1, None, (NB - 1) % 2)
                for q in range(2):
                    sp.wait_ge(x_out[q], 16 * (NB // 2))

            @block.gpsimd
            def _(pool):
                def carry(ticks):
                    wait(pool, ticked, ticks)
                    pool.tensor_tensor(out=tick[:, :], in0=mhalf[:, 0:1], in1=mhalf[:, 0:1], op=ALU.mult).then_inc(ticked, 1)

                def rstd(ve, ve_s, rs, rstd_s, n):
                    pool.wait_ge(ve_s, n + 1)
                    pool.tensor_tensor(out=rs[:, :], in0=ve[:, :], in1=mhalf[:, :], op=ALU.pow).then_inc(rstd_s, 1)

                def h_low(n):
                    wait(pool, h_hi, n + 1)
                    pool.tensor_tensor(out=hT[1][:, :, :], in0=hF[:, :, :], in1=hT[0][:, :, :].bitcast(F32),
                                       op=ALU.subtract).then_inc(h_lo, 1)

                def add(n, ch):
                    wait(pool, y_sb, 2 * n + ch + 1)
                    carry(2 * n + ch)
                    dst = xs[:, slot(n), ch * E:(ch + 1) * E].rearrange("p a e -> p (a e)")
                    pool.tensor_tensor(out=dst, in0=dst, in1=y[:, ch, :], op=ALU.add).then_inc(x2_sb, 1)

                def start():
                    for n in range(2):
                        rstd(ve1, ve_1, rs1, rstd1, n)
                        h_low(n)

                def body(half, par, has_next, has_next2, has_prev):
                    n = 2 * half + par
                    if has_prev:
                        rstd(veo, ve_o, rso, rstdo, n - 1)
                    if has_next2:
                        rstd(ve1, ve_1, rs1, rstd1, n + 2)
                    if has_prev:
                        add(n - 1, 0)
                    if has_next2:
                        h_low(n + 2)
                    if has_prev:
                        add(n - 1, 1)

                run(pool, start, body)
                rstd(veo, ve_o, rso, rstdo, NB - 1)
                add(NB - 1, 0)
                add(NB - 1, 1)

            @block.scalar
            def _(act):
                def h_affine(n):
                    wait(act, h_lo, n)
                    for k in range(KT):
                        if k % 2 == 0:
                            act.wait_ge(mm["t1"], 2 * n + k // 2 + 1)
                        src = bank[5 - 5 * (k // 2)][:, (k % 2) * TB:(k % 2 + 1) * TB]
                        act.activation(hF[:, k, :], src, ACT.Identity, scale=scl[0][:, bass.ds(n, 1), k],
                                       bias=sft[0][:, bass.ds(n, 1), k]).then_inc(h_full, 1)

                def q_gate(n, par, pair):
                    act.wait_ge(mm["q"], 2 * n + pair + 1)
                    act.activation(Q[par][:, 4 * pair:4 * pair + 4, :].rearrange("p g t -> p (g t)"), bank[2 + pair][:, :],
                                   ACT.Sigmoid).then_inc(q_sig, 1)

                def k_and_f(n, par, pair):
                    act.wait_ge(mm["k"], 2 * n + pair + 1)
                    act.activation(K[par][:, 4 * pair:4 * pair + 4, :].rearrange("p g t -> p (g t)"), bank[4 + pair][:, :], ACT.Sigmoid)
                    act.activation(f[par][:, 4 * pair:4 * pair + 4, :].rearrange("p g t -> p (g t)"), bank[4 + pair][:, :],
                                   ACT.Sigmoid, scale=-1.0).then_inc(k_f, 1)

                def v_copy(n, par, ch):
                    act.wait_ge(mm["v"], 2 * n + ch + 1)
                    act.copy(V[par][:, ch, :], bank[ch][:, :]).then_inc(v_sb, 1)

                def g1_high(n):
                    act.wait_ge(mm["g1"], n + 1)
                    act.copy(g1[0][:, :], bank[2][:, 0:TB]).then_inc(g1_hi, 1)

                def gate(n, par, ch):
                    wait(act, sto_s, 2 * (n - 1))
                    act.wait_ge(mm["gate"], 2 * n + ch + 1)
                    act.activation(og[par][:, ch, :], bank[ch][:, :], ACT.Sigmoid).then_inc(gate_sb, 1)

                def start():
                    for n, src in enumerate((env["W_r"], env["W_k"])):
                        act.dma_start(ffn_raw[n][:, :, :], src.rearrange("(k p) n -> p k n", p=P)).then_inc(w_in, 16)
                    h_affine(0)
                    for pair in range(2):
                        q_gate(0, 0, pair)
                    for pair in range(2):
                        k_and_f(0, 0, pair)
                    for ch in range(NC):
                        v_copy(0, 0, ch)
                    g1_high(0)
                    for ch in range(NC):
                        gate(0, 0, ch)
                    h_affine(1)

                def body(half, par, has_next, has_next2, has_prev):
                    n = 2 * half + par
                    if has_prev:
                        for ch in range(NC):
                            act.wait_ge(mm["t2"], 2 * (n - 1) + ch + 1)
                            act.copy(ogT[0][:, ch, :, :].rearrange("p k t -> p (k t)"), bank[ch][:, :]).then_inc(ogt_hi, 1)
                    if has_next:
                        for pair in range(2):
                            q_gate(n + 1, 1 - par, pair)
                        for pair in range(2):
                            k_and_f(n + 1, 1 - par, pair)
                        v_copy(n + 1, 1 - par, 0)
                    act.wait_ge(mm["lvl"], NL * n + 7)
                    act.wait_ge(merged, 6 * n + 6)
                    src = lbank[1].rearrange("p (g t) -> p g t", g=G)
                    for q in range(2):
                        last = act.copy(A[64 * q:64 * q + 32, :, 64 * q + 32:64 * q + 64],
                                        src[64 * q:64 * q + 32, :, 32 * q:32 * q + 32])
                    last.then_inc(merged_act, 1)
                    if has_next:
                        v_copy(n + 1, 1 - par, 1)
                    act.wait_ge(mm["lvl"], NL * n + 8)
                    act.copy(A[0:64, :, 64:128], lbank[0].rearrange("p (g t) -> p g t", g=G)[0:64, :, :]).then_inc(merged_act, 1)
                    if has_next:
                        g1_high(n + 1)
                    for ch in range(NC):
                        act.wait_ge(mm["kt"], 2 * n + ch + 1)
                        act.copy(Kt[:, ch, :, :].rearrange("p h t -> p (h t)"), bank[4 + ch][:, :]).then_inc(kt_sb, 1)
                    if has_next:
                        for ch in range(NC):
                            gate(n + 1, 1 - par, ch)
                    if has_next2:
                        h_affine(n + 2)

                run(act, start, body)
                for ch in range(NC):
                    act.wait_ge(mm["t2"], 2 * (NB - 1) + ch + 1)
                    act.copy(ogT[0][:, ch, :, :].rearrange("p k t -> p (k t)"), bank[ch][:, :]).then_inc(ogt_hi, 1)

            @block.vector
            def _(dve):
                def ln_stats(n, half, par):
                    dve.wait_ge(x_in[par], 16 * (half + 1))
                    for ch in range(NC):
                        last = dve.bn_stats(st1[:, ch, :], xs[:, slot(n), ch * E:(ch + 1) * E].rearrange("p a e -> p (a e)"))
                    last.then_inc(stat1, 1)

                def ln_var(n):
                    for ch in range(NC):
                        last = dve.bn_aggr(mv1[:, ch, :], st1[:, ch, :])
                    last.then_inc(var1, 1)
                    dve.wait_ge(var1, n + 1)
                    dve.tensor_scalar(ve1[:, :], mv1[:, :, 1], EPS, None, ALU.add).then_inc(ve_1, 1)

                def ln_apply(n):
                    dve.wait_ge(rstd1, n + 1)
                    wait(dve, mm["t1"], 2 * n)
                    for ch in range(NC):
                        last = dve.tensor_scalar(xn[:, ch, :], xs[:, slot(n), ch * E:(ch + 1) * E].rearrange("p a e -> p (a e)"),
                                                 mv1[:, ch, 0:1], rs1[:, ch:ch + 1], ALU.subtract, ALU.mult)
                    last.then_inc(xn_sb, 1)

                def h_high(n):
                    dve.wait_ge(h_full, 4 * (n + 1))
                    dve.tensor_copy(hT[0][:, :, :], hF[:, :, :]).then_inc(h_hi, 1)

                def q_silu(n, par, pair):
                    dve.wait_ge(q_sig, 2 * n + pair + 1)
                    dst = Q[par][:, 4 * pair:4 * pair + 4, :].rearrange("p g t -> p (g t)")
                    dve.scalar_tensor_tensor(out=dst, in0=bank[2 + pair][:, :], scalar=QSCALE, in1=dst,
                                             op0=ALU.mult, op1=ALU.mult).then_inc(q_sb, 1)

                def f_signed(n, par, pair):
                    dve.wait_ge(k_f, 2 * n + pair + 1)
                    dst = f[par][:, 4 * pair:4 * pair + 4, :].rearrange("p g t -> p (g t)")
                    wait(dve, f_sb, 2 * n + pair)
                    dve.tensor_scalar(eq[:, :], dst, 0.5, 2.0, ALU.is_equal, ALU.mult).then_inc(f_eq, 1)
                    dve.wait_ge(f_eq, 2 * n + pair + 1)
                    dve.scalar_tensor_tensor(out=dst, in0=eq[:, :], scalar=-1.0, in1=dst,
                                             op0=ALU.add, op1=ALU.mult).then_inc(f_sb, 1)

                def g1_low(n):
                    dve.wait_ge(g1_hi, n + 1)
                    dve.tensor_tensor(out=g1[1][:, :], in0=bank[2][:, 0:TB], in1=g1[0][:, :].bitcast(F32),
                                      op=ALU.subtract).then_inc(g1_lo, 1)

                def ogt_low(n, ch):
                    dve.wait_ge(ogt_hi, 2 * n + ch + 1)
                    dve.tensor_tensor(out=ogT[1][:, ch, :, :].rearrange("p k t -> p (k t)"), in0=bank[ch][:, :],
                                      in1=ogT[0][:, ch, :, :].rearrange("p k t -> p (k t)").bitcast(F32),
                                      op=ALU.subtract).then_inc(ogt_lo, 1)

                def wo_scale(n, ch, b):
                    dve.wait_ge(mm["wo"], 2 * n + ch + 1)
                    dve.wait_ge(rstdo, n + 1)
                    wait(dve, x2_sb, 2 * (n - 1) + ch + 1)
                    dve.scalar_tensor_tensor(out=y[:, ch, :], in0=bank[3 - 2 * ch][:, :], scalar=rso[:, ch:ch + 1],
                                             in1=gab[:, bass.ds(b, 1), :].rearrange("p a e -> p (a e)"),
                                             op0=ALU.mult, op1=ALU.mult).then_inc(y_sb, 1)

                def tots(par, m):
                    cnt = G * P // m
                    off = G * P - 2 * cnt
                    t = f[par][:, :, :].rearrange("p g t -> p (g t)") if m == 1 else Tot[:, off:off + cnt]
                    return t.rearrange("p (n two) -> p n two", two=2)

                def level_update(n, par, m, idx, has_next2):
                    nb = G * P // (2 * m)
                    t = tots(par, m)
                    cnt2 = G * P // (2 * m)
                    off2 = G * P - 2 * cnt2
                    dve.wait_ge(mm["lvl"], NL * n + idx + 1)
                    dve.wait_ge(level, NL * n + idx)
                    if idx <= 5:
                        dve.wait_ge(merged, 6 * n + idx)
                    if m == 32 and has_next2:
                        dve.wait_ge(stat1, n + 3)
                    dve.tensor_tensor(out=Tot[:, off2:off2 + cnt2], in0=t[:, :, 0], in1=t[:, :, 1], op=ALU.mult)
                    q = Q[par][:, :, :].rearrange("p g t -> p (g t)").rearrange("p (n two m) -> p n two m", two=2, m=m)[:, :, 1, :]
                    k = K[par][:, :, :].rearrange("p g t -> p (g t)").rearrange("p (n two m) -> p n two m", two=2, m=m)[:, :, 0, :]
                    dve.tensor_tensor(out=q, in0=q, in1=t[:, :, 0:1].to_broadcast([P, nb, m]), op=ALU.mult)
                    dve.tensor_tensor(out=k, in0=k, in1=t[:, :, 1:2].to_broadcast([P, nb, m]), op=ALU.mult).then_inc(level, 1)

                def level_merge(n, m, idx):
                    nb = 64 // m
                    dst = A[:, :, :].rearrange("p g (n two m) -> p g n two m", two=2, m=m)[:, :, :, 1, :]
                    src = lbank[(idx - 1) % 2].rearrange("p (g n m) -> p g n m", g=G, m=m)
                    msk = masks[:, idx - 1, :].rearrange("p (n m) -> p n m", m=m).unsqueeze(1).to_broadcast([P, G, nb, m])
                    dve.copy_predicated(dst, msk, src).then_inc(merged, 1)

                def gated_var(n):
                    for ch in range(NC):
                        last = dve.bn_aggr(mvo[:, ch, :], sto[:, ch, :])
                    last.then_inc(varo, 1)
                    dve.wait_ge(varo, n + 1)
                    dve.tensor_scalar(veo[:, :], mvo[:, :, 1], EPS, None, ALU.add).then_inc(ve_o, 1)

                def start():
                    dve.memset(S[0][:, :, :], 0.0)
                    for n in range(2):
                        ln_stats(n, 0, n)
                        dve.wait_ge(stat1, n + 1)
                        ln_var(n)
                        ln_apply(n)
                        h_high(n)
                        if n == 0:
                            for pair in range(2):
                                q_silu(0, 0, pair)
                            for pair in range(2):
                                f_signed(0, 0, pair)
                            g1_low(0)

                def body(half, par, has_next, has_next2, has_prev):
                    n = 2 * half + par
                    prev_b = (n - 1) // BPB if has_prev else 0
                    dve.wait_ge(mm["lvl"], NL * n + 1)
                    dve.wait_ge(f_sb, 2 * (n + 1))
                    dve.wait_ge(q_sb, 2 * (n + 1))
                    wait(dve, sto_s, 2 * n)
                    dve.tensor_tensor(out=Q[par][:, :, :], in0=Q[par][:, :, :], in1=f[par][:, :, :], op=ALU.mult).then_inc(level, 1)
                    wait(dve, mm["o"], 2 * n)
                    wait(dve, merged_act, 2 * n)
                    dve.tensor_tensor(out=A[:, :, :], in0=lvl2[:, :].rearrange("p (g t) -> p g t", g=G),
                                      in1=ident[:, :].unsqueeze(1).to_broadcast([P, G, P]), op=ALU.mult).then_inc(merged, 1)
                    if has_prev:
                        gated_var(n - 1)
                        ogt_low(n - 1, 0)
                    for idx, m in enumerate(LEVELS, 1):
                        level_update(n, par, m, idx, has_next2)
                        if m <= 16:
                            level_merge(n, m, idx)
                        if m == 1 and has_prev:
                            ogt_low(n - 1, 1)
                        if has_next and m in (2, 4):
                            q_silu(n + 1, 1 - par, m // 4)
                        if has_next and m in (8, 16):
                            f_signed(n + 1, 1 - par, m // 16)
                        if has_next2 and m == 16:
                            ln_stats(n + 2, half + 1, par)
                        if has_next2 and m == 32:
                            ln_var(n + 2)
                    if has_next2:
                        ln_apply(n + 2)
                    if has_next:
                        g1_low(n + 1)
                    if has_prev:
                        wo_scale(n - 1, 0, prev_b)
                    def gated(ch):
                        dve.wait_ge(mm["o"], 2 * n + ch + 1)
                        dve.wait_ge(gate_sb, 2 * n + ch + 1)
                        bk = bank[2]
                        dve.tensor_tensor(out=og[par][:, ch, :], in0=bk[:, :], in1=og[par][:, ch, :], op=ALU.mult).then_inc(og_sb, 1)

                    def gated_stats(ch):
                        dve.wait_ge(og_sb, 2 * n + ch + 1)
                        dve.bn_stats(sto[:, ch, :], og[par][:, ch, :]).then_inc(sto_s, 1)

                    gated(0)
                    dve.wait_ge(mm["ds"], 2 * n + 1)
                    dve.wait_ge(level, NL * (n + 1))
                    wait(dve, s_flag, n)
                    tot = Tot[:, G * P - 2 * G:G * P - G].rearrange("p (h c) -> p h c", c=NC)
                    for h in range(H):
                        last = dve.scalar_tensor_tensor(out=S[1][:, h, :], in0=S[0][:, h, :], scalar=tot[:, h, 0:1],
                                                        in1=bank[3][:, h * P:(h + 1) * P], op0=ALU.mult, op1=ALU.add)
                    last.then_inc(s_mid, 1)
                    dve.wait_ge(mm["ds"], 2 * n + 2)
                    dve.wait_ge(s_mid, n + 1)
                    for h in range(H):
                        last = dve.scalar_tensor_tensor(out=S[0][:, h, :], in0=S[1][:, h, :], scalar=tot[:, h, 1:2],
                                                        in1=bank[4][:, h * P:(h + 1) * P], op0=ALU.mult, op1=ALU.add)
                    last.then_inc(s_new, 1)
                    dve.wait_ge(s_new, n + 1)
                    dve.tensor_scalar(S[0][:, :, :], S[0][:, :, :], flags[:, bass.ds(n + 1, 1)], None, ALU.mult).then_inc(s_flag, 1)
                    gated_stats(0)
                    if has_next2:
                        h_high(n + 2)
                    if has_prev:
                        wo_scale(n - 1, 1, prev_b)
                    gated(1)
                    gated_stats(1)

                run(dve, start, body)
                dve.wait_ge(sto_s, 2 * NB)
                gated_var(NB - 1)
                for ch in range(NC):
                    ogt_low(NB - 1, ch)
                for ch in range(NC):
                    wo_scale(NB - 1, ch, B - 1)

            @block.tensor
            def _(pe):
                def product(dst, lhs, rhs, steps):
                    terms = [(a, b, s) for s in range(steps) for a, b in ((0, 0), (0, 1), (1, 0))]
                    for t, (a, b, s) in enumerate(terms):
                        last = pe.matmul(dst, lhs(a, s), rhs(b, s), start=(t == 0), stop=(t == len(terms) - 1))
                    return last

                def t1(n):
                    pe.wait_ge(xn_sb, n + 1)
                    for k in range(KT):
                        for ch in range(NC):
                            col = (k % 2) * TB + ch * P
                            last = pe.transpose(bank[5 - 5 * (k // 2)][:, col:col + P], xn[:, ch, k * P:(k + 1) * P], ident[:, :])
                        if k % 2:
                            last.then_inc(mm["t1"], 1)

                def rows_of(name, pair, first, key):
                    for o in range(2):
                        h = 2 * pair + o
                        last = product(bank[first + pair][:, o * TB:(o + 1) * TB],
                                       lambda a, s: W[name][a][:, s, h * P:(h + 1) * P], lambda b, s: hT[b][:, s, :], KT)
                    last.then_inc(mm[key], 1)

                def v_rows(ch):
                    product(bank[ch][:, :], lambda a, s: hT[a][:, s, ch * P:(ch + 1) * P],
                            lambda b, s: W["v"][b][:, s, :], KT).then_inc(mm["v"], 1)

                def g1_rows():
                    product(bank[2][:, 0:TB], lambda a, s: W["g1"][a][:, s, :], lambda b, s: hT[b][:, s, :], KT).then_inc(mm["g1"], 1)

                def gate_rows(ch):
                    product(bank[ch][:, :], lambda a, s: g1[a][:, ch * P:(ch + 1) * P],
                            lambda b, s: W["g2"][b][:, s, :], 1).then_inc(mm["gate"], 1)

                def t2(n, par, ch):
                    pe.wait_ge(og_sb, 2 * n + ch + 1)
                    for k in range(KT):
                        last = pe.transpose(bank[ch][:, k * P:(k + 1) * P], og[par][:, ch, k * P:(k + 1) * P], ident[:, :])
                    last.then_inc(mm["t2"], 1)

                def wo_rows(n, ch):
                    pe.wait_ge(ogt_lo, 2 * n + ch + 1)
                    product(bank[3 - 2 * ch][:, :], lambda a, s: ogT[a][:, ch, s, :],
                            lambda b, s: W["o"][b][:, s, :], KT).then_inc(mm["wo"], 1)

                def start():
                    t1(0)
                    pe.wait_ge(h_lo, 1)
                    for pair in range(2):
                        rows_of("q", pair, 2, "q")
                    pe.wait_ge(h_full, 4)
                    for pair in range(2):
                        rows_of("k", pair, 4, "k")
                    for ch in range(NC):
                        v_rows(ch)
                    pe.wait_ge(q_sb, 1)
                    g1_rows()
                    pe.wait_ge(g1_lo, 1)
                    pe.wait_ge(v_sb, 2)
                    for ch in range(NC):
                        gate_rows(ch)
                    pe.wait_ge(k_f, 2)
                    pe.wait_ge(gate_sb, 1)
                    t1(1)

                def body(half, par, has_next, has_next2, has_prev):
                    n = 2 * half + par
                    q, k = Q[par], K[par]

                    def level_product(idx):
                        m = LEVELS[idx - 1]
                        pe.wait_ge(level, NL * n + idx)
                        wait(pe, merged, 6 * n + min(max(1, idx - 2), 6) if idx < 8 else 6 * n + 6)
                        for g in range(G):
                            rhs = q[:, g, :].rearrange("p (n two m) -> p n two m", two=2, m=m)[:, :, 1, :]
                            last = pe.matmul(lbank[(idx - 1) % 2][:, g * 64:(g + 1) * 64].rearrange("p (n m) -> p n m", m=m),
                                             k[:, g, :], rhs, start=True, stop=True)
                        last.then_inc(mm["lvl"], 1)

                    pe.wait_ge(q_sb, 2 * (n + 1))
                    pe.wait_ge(k_f, 2 * (n + 1))
                    wait(pe, merged_act, 2 * n)
                    for g in range(G):
                        last = pe.matmul(lvl2[:, g * P:(g + 1) * P], k[:, g, :], q[:, g, :], start=True, stop=True)
                    last.then_inc(mm["lvl"], 1)
                    if has_prev:
                        if has_next:
                            pe.wait_ge(h_full, 4 * (n + 2))
                        t2(n - 1, 1 - par, 0)
                    level_product(1)
                    if has_prev:
                        wait(pe, y_sb, 2 * (n - 1))
                        t2(n - 1, 1 - par, 1)
                    if has_next:
                        pe.wait_ge(h_lo, n + 2)
                        wait(pe, og_sb, 2 * n)
                        rows_of("q", 0, 2, "q")
                    level_product(2)
                    if has_next:
                        wait(pe, s_mid, n)
                        rows_of("q", 1, 2, "q")
                    level_product(3)
                    if has_next:
                        wait(pe, s_new, n)
                        rows_of("k", 0, 4, "k")
                    level_product(4)
                    if has_next:
                        pe.wait_ge(h_full, 4 * (n + 2))
                        rows_of("k", 1, 4, "k")
                    level_product(5)
                    if has_next:
                        pe.wait_ge(gate_sb, 2 * (n + 1))
                        wait(pe, ogt_lo, 2 * n)
                        v_rows(0)
                    level_product(6)
                    if has_next:
                        v_rows(1)
                    level_product(7)
                    if has_next:
                        pe.wait_ge(q_sb, 2 * (n + 2))
                        g1_rows()
                    if has_prev:
                        wait(pe, s_mid, n)
                        wo_rows(n - 1, 0)
                    pe.wait_ge(level, NL * (n + 1))
                    if has_next:
                        pe.wait_ge(k_f, 2 * (n + 2))
                    for ch in range(NC):
                        for h in range(H):
                            last = pe.transpose(bank[4 + ch][:, h * P:(h + 1) * P], k[:, h * NC + ch, :], ident[:, :])
                        last.then_inc(mm["kt"], 1)
                    if has_next:
                        pe.wait_ge(g1_lo, n + 2)
                        for ch in range(NC):
                            pe.wait_ge(v_sb, 2 * (n + 1) + ch + 1)
                            gate_rows(ch)

                    def output(ch):
                        for h in range(H):
                            g = h * NC + ch
                            pe.matmul(bank[2][:, h * P:(h + 1) * P], q[:, g, :], S[ch][:, h, :], start=True, stop=False)
                            last = pe.matmul(bank[2][:, h * P:(h + 1) * P], A[:, g, :], V[par][:, ch, h * P:(h + 1) * P],
                                             start=False, stop=True)
                        last.then_inc(mm["o"], 1)

                    pe.wait_ge(merged_act, 2 * (n + 1))
                    wait(pe, s_flag, n)
                    pe.wait_ge(v_sb, 2 * (n + 1))
                    if has_next:
                        pe.wait_ge(g1_lo, n + 2)
                    output(0)
                    if has_prev:
                        pe.wait_ge(y_sb, 2 * (n - 1) + 1)
                    elif has_next:
                        pe.wait_ge(q_sb, 2 * (n + 2))
                    for ch in range(NC):
                        pe.wait_ge(kt_sb, 2 * n + ch + 1)
                        if ch == 1:
                            pe.wait_ge(kt_sb, 2 * n + 1)
                        for h in range(H):
                            last = pe.matmul(bank[3 + ch][:, h * P:(h + 1) * P], Kt[:, ch, h, :], V[par][:, ch, h * P:(h + 1) * P],
                                             start=True, stop=True)
                        last.then_inc(mm["ds"], 1)
                    if has_next2:
                        pe.wait_ge(kt_sb, 2 * (n + 1))
                        pe.wait_ge(gate_sb, 2 * (n + 1) + 1)
                        t1(n + 2)
                    if has_prev:
                        if has_next:
                            pe.wait_ge(gate_sb, 2 * (n + 2))
                        wo_rows(n - 1, 1)
                    pe.wait_ge(s_mid, n + 1)
                    pe.wait_ge(og_sb, 2 * n + 1)
                    output(1)

                run(pe, start, body)
                pe.wait_ge(y_sb, 2 * (NB - 1))
                for ch in range(NC):
                    t2(NB - 1, (NB - 1) % 2, ch)
                for ch in range(NC):
                    pe.wait_ge(s_mid, NB)
                    if ch == 1:
                        pe.wait_ge(ogt_lo, 2 * NB)
                    wo_rows(NB - 1, ch)


def ffn(nc, sb, sem, wait, env):
    ident, flags, mhalf = (env[n] for n in ("ident", "flags", "mhalf"))
    gab, scl, sft, x2d, of = (env[n] for n in ("gab", "scl", "sft", "x2d", "of"))
    bank8 = env["bank"] + env["lbank"]
    ffn_raw, w_in = env["ffn_raw"], env["w_in"]
    mur, muk = (env["vec"][:, (B + n) * KT:(B + n + 1) * KT] for n in (1, 2))
    KK, TT, RR, FV = bank8[0:2], bank8[2:4], bank8[4:6], bank8[6:8]
    with ExitStack() as ctx:
        W = {n: [sb(ctx, f"f{n}_{part}", [P, KT, E], F32R) for part in ("hi", "lo")] for n in "rkv"}
        ffn_raw = ffn_raw + [sb(ctx, "ffn_raw2", [P, KT, E])]
        xs = sb(ctx, "fxs", [P, XS, NC * E])
        tick = sb(ctx, "ftick", [P, 1])
        ticked = sem(ctx, "fticked")
        xn = sb(ctx, "fxn", [P, NC, E])
        h2 = sb(ctx, "h2", [P, KT, TB + 1])
        dd = sb(ctx, "dd", [P, KT, TB])
        xk32 = sb(ctx, "xk32", [P, KT, TB])
        xr32 = sb(ctx, "xr32", [P, KT, TB])
        xk = [sb(ctx, f"xk_{part}", [P, KT, TB], F32R) for part in ("hi", "lo")]
        xr = [sb(ctx, f"xr_{part}", [P, KT, TB], F32R) for part in ("hi", "lo")]
        rl = sb(ctx, "rl", [P, KT, TB])
        ka = [sb(ctx, f"ka_{part}", [P, KT, TB], F32R) for part in ("hi", "lo")]
        r = sb(ctx, "r", [P, NC, E])
        st = sb(ctx, "fst", [P, NC, 6])
        mv = sb(ctx, "fmv", [P, NC, 2])
        ve = sb(ctx, "fve", [P, NC])
        rs = sb(ctx, "frs", [P, NC])
        x_in = [sem(ctx, f"fx_in{n}") for n in range(2)]
        x_out = [sem(ctx, f"fx_out{n}") for n in range(2)]
        wt, wt_hi, wt_lo = sem(ctx, "wt"), sem(ctx, "wt_hi"), sem(ctx, "wt_lo")
        mm = {n: sem(ctx, f"fmm_{n}") for n in ("t", "k", "r", "v")}
        relu, ka_hi, h_sb, r_sig, xk_hi, xr_hi = (sem(ctx, n) for n in ("relu", "ka_hi", "h_sb", "r_sig", "xk_hi", "xr_hi"))
        halo, diff, xk_f, xr_f, xk_lo, xr_lo, sq, ka_lo, stat, var, xn_sb, rv = (
            sem(ctx, n) for n in ("halo", "diff", "xk_f", "xr_f", "xk_lo", "xr_lo", "sq", "ka_lo", "fstat", "fvar", "fxn_sb", "rv"))
        ve_s, rstd, r_gb, x3 = (sem(ctx, n) for n in ("fve_s", "frstd", "r_gb", "x3"))

        def run(eng, start, body):
            start()
            body(0, 0, True, True, False)
            body(0, 1, True, True, True)
            with eng.Fori(1, NB // 2 - 1) as half:
                body(half, 0, True, True, True)
                body(half, 1, True, True, True)
            body(NB // 2 - 1, 0, True, False, True)
            body(NB // 2 - 1, 1, False, False, True)

        def slot(n):
            return bass.ds(n % XS, 1)

        def rows(n):
            return bass.ds(n * TB, TB)

        def chunk(n, ch):
            return xs[:, slot(n), ch * E:(ch + 1) * E].rearrange("p a e -> p (a e)")

        with nc.Block() as block:
            @block.sync
            def _(sp):
                def load(n, par):
                    wait(sp, stat, n - 1)
                    sp.dma_start(xs[:, slot(n), :].rearrange("p a (c e) -> p (a c) e", c=NC),
                                 x2d[rows(n), :].rearrange("(c p) e -> p c e", p=P)).then_inc(x_in[par], 16)

                def store(n, par):
                    wait(sp, x3, 2 * (n + 1))
                    sp.dma_start(of[rows(n), :].rearrange("(c p) e -> p c e", p=P),
                                 xs[:, slot(n), :].rearrange("p a (c e) -> p (a c) e", c=NC)).then_inc(x_out[par], 16)

                def start():
                    for n in range(2):
                        load(n, n)

                def body(half, par, has_next, has_next2, has_prev):
                    n = 2 * half + par
                    if has_next2:
                        wait(sp, x_out[par], 16 * half)
                        load(n + 2, par)
                    if has_prev:
                        store(n - 1, 1 - par)

                run(sp, start, body)
                store(NB - 1, (NB - 1) % 2)
                for q in range(2):
                    sp.wait_ge(x_out[q], 16 * (NB // 2))

            @block.gpsimd
            def _(pool):
                def carry(ticks):
                    wait(pool, ticked, ticks)
                    pool.tensor_tensor(out=tick[:, :], in0=mhalf[:, 0:1], in1=mhalf[:, 0:1], op=ALU.mult).then_inc(ticked, 1)

                def rstd_of(n):
                    pool.wait_ge(ve_s, n + 1)
                    pool.tensor_tensor(out=rs[:, :], in0=ve[:, :], in1=mhalf[:, :], op=ALU.pow).then_inc(rstd, 1)

                def start():
                    rstd_of(0)
                    rstd_of(1)

                def body(half, par, has_next, has_next2, has_prev):
                    n = 2 * half + par
                    if has_next2:
                        rstd_of(n + 2)
                    for ch in range(NC):
                        pool.wait_ge(r_sig, 2 * n + ch + 1)
                        carry(4 * n + ch)
                        pool.tensor_tensor(out=r[:, ch, :], in0=r[:, ch, :],
                                           in1=gab[:, bass.ds(n // BPB + B, 1), :].rearrange("p a e -> p (a e)"),
                                           op=ALU.mult).then_inc(r_gb, 1)
                    for ch in range(NC):
                        pool.wait_ge(rv, 2 * n + ch + 1)
                        carry(4 * n + 2 + ch)
                        pool.tensor_tensor(out=chunk(n, ch), in0=chunk(n, ch), in1=r[:, ch, :], op=ALU.add).then_inc(x3, 1)

                run(pool, start, body)

            @block.scalar
            def _(act):
                def h_affine(n):
                    wait(act, halo, n + 1)
                    for k in range(KT):
                        if k % 2 == 0:
                            act.wait_ge(mm["t"], 2 * n + k // 2 + 1)
                        last = act.activation(h2[:, k, 1:TB + 1], TT[k // 2][:, (k % 2) * TB:(k % 2 + 1) * TB], ACT.Identity,
                                              scale=scl[1][:, bass.ds(n, 1), k], bias=sft[1][:, bass.ds(n, 1), k])
                    last.then_inc(h_sb, 1)

                def highs(n):
                    act.wait_ge(xk_f, n + 1)
                    wait(act, mm["k"], 2 * n)
                    act.copy(xk[0][:, :, :], xk32[:, :, :]).then_inc(xk_hi, 1)
                    act.wait_ge(xr_f, n + 1)
                    wait(act, mm["r"], 2 * n)
                    act.copy(xr[0][:, :, :], xr32[:, :, :]).then_inc(xr_hi, 1)

                def start():
                    act.dma_start(ffn_raw[2][:, :, :], env["W_v"].rearrange("(k p) n -> p k n", p=P)).then_inc(w_in, 16)
                    for u in range(3 * KT):
                        act.wait_ge(wt, u + 1)
                        act.copy(W["rkv"[u // KT]][0][:, u % KT, :], bank8[u % 8][:, :]).then_inc(wt_hi, 1)
                    h_affine(0)
                    highs(0)

                def body(half, par, has_next, has_next2, has_prev):
                    n = 2 * half + par
                    for pair in range(2):
                        act.wait_ge(mm["k"], 2 * n + pair + 1)
                        wait(act, ka_lo, 2 * n)
                        act.activation(rl[:, 2 * pair:2 * pair + 2, :].rearrange("p k t -> p (k t)"), KK[pair][:, :],
                                       ACT.Relu).then_inc(relu, 1)
                    for pair in range(2):
                        act.wait_ge(sq, 2 * n + pair + 1)
                        wait(act, mm["v"], 2 * n)
                        act.copy(ka[0][:, 2 * pair:2 * pair + 2, :], rl[:, 2 * pair:2 * pair + 2, :]).then_inc(ka_hi, 1)
                    if has_next:
                        h_affine(n + 1)
                    for ch in range(NC):
                        act.wait_ge(mm["r"], 2 * n + ch + 1)
                        wait(act, x3, 2 * n)
                        act.activation(r[:, ch, :], RR[ch][:, :], ACT.Sigmoid).then_inc(r_sig, 1)
                    if has_next:
                        highs(n + 1)

                run(act, start, body)

            @block.vector
            def _(dve):
                def ln_stats(n, half, par):
                    dve.wait_ge(x_in[par], 16 * (half + 1))
                    for ch in range(NC):
                        last = dve.bn_stats(st[:, ch, :], chunk(n, ch))
                    last.then_inc(stat, 1)

                def ln_var(n):
                    for ch in range(NC):
                        last = dve.bn_aggr(mv[:, ch, :], st[:, ch, :])
                    last.then_inc(var, 1)
                    dve.wait_ge(var, n + 1)
                    dve.tensor_scalar(ve[:, :], mv[:, :, 1], EPS, None, ALU.add).then_inc(ve_s, 1)

                def ln_apply(n):
                    dve.wait_ge(rstd, n + 1)
                    wait(dve, mm["t"], 2 * n)
                    for ch in range(NC):
                        last = dve.tensor_scalar(xn[:, ch, :], chunk(n, ch), mv[:, ch, 0:1], rs[:, ch:ch + 1],
                                                 ALU.subtract, ALU.mult)
                    last.then_inc(xn_sb, 1)

                def shift(n):
                    dve.wait_ge(h_sb, n + 1)
                    prev = h2[:, :, 0:TB]
                    dve.tensor_tensor(out=dd[:, :, :], in0=h2[:, :, 1:TB + 1], in1=prev, op=ALU.subtract).then_inc(diff, 1)
                    dve.wait_ge(diff, n + 1)
                    for dst, mu, s in ((xk32, muk, xk_f), (xr32, mur, xr_f)):
                        for k in range(KT):
                            last = dve.scalar_tensor_tensor(out=dst[:, k, :], in0=dd[:, k, :], scalar=mu[:, k:k + 1],
                                                            in1=h2[:, k, 0:TB], op0=ALU.mult, op1=ALU.add)
                        last.then_inc(s, 1)
                    dve.wait_ge(xr_f, n + 1)
                    dve.tensor_scalar(h2[:, :, 0:1], h2[:, :, TB:TB + 1], flags[:, bass.ds(n + 1, 1)], None,
                                      ALU.mult).then_inc(halo, 1)

                def lows(n):
                    for part, full, hi_s, lo_s in ((xk, xk32, xk_hi, xk_lo), (xr, xr32, xr_hi, xr_lo)):
                        dve.wait_ge(hi_s, n + 1)
                        dve.tensor_tensor(out=part[1][:, :, :], in0=full[:, :, :], in1=part[0][:, :, :].bitcast(F32),
                                          op=ALU.subtract).then_inc(lo_s, 1)

                def start():
                    dve.memset(h2[:, :, 0:1], 0.0).then_inc(halo, 1)
                    ln_stats(0, 0, 0)
                    dve.wait_ge(stat, 1)
                    ln_var(0)
                    ln_apply(0)
                    for u in range(3 * KT):
                        dve.wait_ge(wt_hi, u + 1)
                        w = W["rkv"[u // KT]]
                        dve.tensor_tensor(out=w[1][:, u % KT, :], in0=bank8[u % 8][:, :], in1=w[0][:, u % KT, :].bitcast(F32),
                                          op=ALU.subtract).then_inc(wt_lo, 1)
                    shift(0)
                    lows(0)
                    ln_stats(1, 0, 1)
                    dve.wait_ge(stat, 2)
                    ln_var(1)
                    ln_apply(1)

                def body(half, par, has_next, has_next2, has_prev):
                    n = 2 * half + par
                    for pair in range(2):
                        part = rl[:, 2 * pair:2 * pair + 2, :]
                        dve.wait_ge(relu, 2 * n + pair + 1)
                        dve.tensor_tensor(out=part, in0=part, in1=part, op=ALU.mult).then_inc(sq, 1)
                    for pair in range(2):
                        part = rl[:, 2 * pair:2 * pair + 2, :]
                        dve.wait_ge(ka_hi, 2 * n + pair + 1)
                        dve.tensor_tensor(out=ka[1][:, 2 * pair:2 * pair + 2, :], in0=part,
                                          in1=ka[0][:, 2 * pair:2 * pair + 2, :].bitcast(F32), op=ALU.subtract).then_inc(ka_lo, 1)
                    if has_next2:
                        ln_stats(n + 2, half + 1, par)
                    if has_next:
                        if has_next2:
                            dve.wait_ge(stat, n + 3)
                        shift(n + 1)
                        if has_next2:
                            ln_var(n + 2)
                        lows(n + 1)
                    if has_next2:
                        ln_apply(n + 2)
                    for ch in range(NC):
                        dve.wait_ge(mm["v"], 2 * n + ch + 1)
                        dve.wait_ge(r_gb, 2 * n + ch + 1)
                        dve.tensor_tensor(out=r[:, ch, :], in0=FV[ch][:, :], in1=r[:, ch, :], op=ALU.mult).then_inc(rv, 1)

                run(dve, start, body)

            @block.tensor
            def _(pe):
                def product(dst, lhs, rhs, steps):
                    terms = [(a, b, s) for s in range(steps) for a, b in ((0, 0), (0, 1), (1, 0))]
                    for t, (a, b, s) in enumerate(terms):
                        last = pe.matmul(dst, lhs(a, s), rhs(b, s), start=(t == 0), stop=(t == len(terms) - 1))
                    return last

                def transposes(n):
                    pe.wait_ge(xn_sb, n + 1)
                    wait(pe, h_sb, n)
                    for k in range(KT):
                        for ch in range(NC):
                            col = (k % 2) * TB + ch * P
                            last = pe.transpose(TT[k // 2][:, col:col + P], xn[:, ch, k * P:(k + 1) * P], ident[:, :])
                        if k % 2:
                            last.then_inc(mm["t"], 1)

                def start():
                    pe.wait_ge(w_in, 48)
                    for u in range(3 * KT):
                        wait(pe, wt_lo, u - 7)
                        for d in range(KT):
                            last = pe.transpose(bank8[u % 8][:, d * P:(d + 1) * P],
                                                ffn_raw[u // KT][:, d, (u % KT) * P:(u % KT + 1) * P], ident[:, :])
                        last.then_inc(wt, 1)
                    pe.wait_ge(wt_lo, 3 * KT)
                    transposes(0)

                def body(half, par, has_next, has_next2, has_prev):
                    n = 2 * half + par
                    pe.wait_ge(xk_lo, n + 1)
                    for d in range(KT):
                        if d % 2 == 0:
                            wait(pe, relu, 2 * (n - 1) + d // 2 + 1)
                        last = product(KK[d // 2][:, (d % 2) * TB:(d % 2 + 1) * TB],
                                       lambda a, s: W["k"][a][:, s, d * P:(d + 1) * P], lambda b, s: xk[b][:, s, :], KT)
                        if d % 2:
                            last.then_inc(mm["k"], 1)
                    if has_next:
                        transposes(n + 1)
                    pe.wait_ge(xr_lo, n + 1)
                    for ch in range(NC):
                        wait(pe, r_sig, 2 * (n - 1) + ch + 1)
                        product(RR[ch][:, :], lambda a, s: xr[a][:, s, ch * P:(ch + 1) * P],
                                lambda b, s: W["r"][b][:, s, :], KT).then_inc(mm["r"], 1)
                    pe.wait_ge(ka_lo, 2 * (n + 1))
                    for ch in range(NC):
                        wait(pe, rv, 2 * (n - 1) + ch + 1)
                        product(FV[ch][:, :], lambda a, s: ka[a][:, s, ch * P:(ch + 1) * P],
                                lambda b, s: W["v"][b][:, s, :], KT).then_inc(mm["v"], 1)

                run(pe, start, body)


_INS = ['L0_attn_x', 'L0_attn_wq', 'L0_attn_wk', 'L0_attn_wv', 'L0_attn_wo', 'L0_attn_wg1', 'L0_attn_wg2', 'L0_attn_norm_w',
        'L0_ffn_W_r', 'L0_ffn_W_k', 'L0_ffn_W_v', 'L0_ffn_mu_r', 'L0_ffn_mu_k', 'L0_c', 'L0_wmod']


def kernel(**inputs):
    import numpy as _np
    import concourse.bacc as _bacc
    from concourse import mybir as _mybir
    from concourse.bass_utils import run_bass_kernel_spmd as _run

    nc = _bacc.Bacc("TRN2", target_bir_lowering=False, num_devices=1)
    arrays, args = {}, []
    for name in _INS:
        a = _np.ascontiguousarray(inputs[name])
        arrays[f"in_{name}"] = a
        args.append(nc.dram_tensor(f"in_{name}", a.shape, _mybir.dt.from_np(a.dtype), kind="ExternalInput").ap())
    args.append(nc.dram_tensor("out_0", (B, T, E), _mybir.dt.float32, kind="ExternalOutput").ap())
    adaln_kernel(nc, *args)
    r = _run(nc, [arrays], core_ids=[0])
    return r.results[0]["out_0"]
```

```python
import concourse.bass as bass
from concourse import mybir
from contextlib import ExitStack

F32 = mybir.dt.float32
F32R = mybir.dt.float32r
I32 = mybir.dt.int32
ALU = mybir.AluOpType
ACT = mybir.ActivationFunctionType

P = 128
B, T, E = 2, 4096, 512
H = 4
KT = E // P
TB = 256
NC = TB // P
NB = B * T // TB
BPB = NB // B
G = H * NC
LEVELS = [1, 2, 4, 8, 16, 32, 64]
NL = len(LEVELS) + 1
NU = len(LEVELS)
EPS = 1e-5
FLOOR = 0.25
QSCALE = float(2 * P) ** -0.5
XS = 4


def adaln_kernel(nc, x, wq, wk, wv, wo, wg1, wg2, norm_w, W_r, W_k, W_v, mu_r, mu_k, c, wmod, out):
    xf = x.rearrange("b t e -> (b t) e")
    of = out.rearrange("b t e -> (b t) e")
    x2d = nc.dram_tensor("x2_scratch", (B * T, E), F32, kind="Internal").ap()

    def sb(ctx, name, shape, dt=F32):
        return ctx.enter_context(nc.sbuf_tensor(name, shape, dt))

    def sem(ctx, name):
        return ctx.enter_context(nc.semaphore(name))

    def wait(eng, s, value):
        if not isinstance(value, int) or value > 0:
            eng.wait_ge(s, value)

    with ExitStack() as top:
        bank = [top.enter_context(nc.psum_tensor(f"bank{n}", [P, 512], F32)) for n in range(6)]
        lvl2 = top.enter_context(nc.psum_tensor("lvl2", [P, 1024], F32))
        lbank = [lvl2[:, 0:512], lvl2[:, 512:1024]]

        ident = sb(top, "ident", [P, P])
        flags = sb(top, "flags", [P, NB + 1])
        mhalf = sb(top, "mhalf", [P, NC])
        scl = [sb(top, f"scl{n}", [P, NB, KT]) for n in range(2)]
        sft = [sb(top, f"sft{n}", [P, NB, KT]) for n in range(2)]
        gab = sb(top, "gab", [P, 2 * B, E])
        vec = sb(top, "vec", [P, (B + 3) * KT])
        ffn_raw = [sb(top, f"ffn_raw{n}", [P, KT, E]) for n in range(2)]
        w_in = sem(top, "w_in")

        attn = ExitStack()
        W = {}
        for name, kt, n in (("q", KT, E), ("k", KT, E), ("v", KT, E), ("o", KT, E), ("g1", KT, P), ("g2", 1, E)):
            W[name] = [sb(attn, f"w{name}_{part}", [P, kt, n], F32R) for part in ("hi", "lo")]
        masks = sb(attn, "masks", [P, 5, 64], I32)
        ln1 = ln_state(attn, sb, sem, "ln1")
        setup(nc, sb, sem, wait, locals())
        attend(nc, sb, sem, wait, locals())
        attn.close()
        ffn(nc, sb, sem, wait, locals())


def ln_state(ctx, sb, sem, name):
    return {
        "xs": sb(ctx, f"{name}_xs", [P, XS, NC * E]), "xn": sb(ctx, f"{name}_xn", [P, NC, E]),
        "st": sb(ctx, f"{name}_st", [P, NC, 6]), "mv": sb(ctx, f"{name}_mv", [P, NC, 2]),
        "ve": sb(ctx, f"{name}_ve", [P, NC]), "rs": sb(ctx, f"{name}_rs", [P, NC]),
        "x_in": [sem(ctx, f"{name}_x_in{n}") for n in range(2)],
        "stat": sem(ctx, f"{name}_stat"), "var": sem(ctx, f"{name}_var"), "ve_ready": sem(ctx, f"{name}_ve_ready"),
        "rstd": sem(ctx, f"{name}_rstd"), "xn_ready": sem(ctx, f"{name}_xn_ready"),
    }


def slot(n):
    return bass.ds(n % XS, 1)


def rows(n):
    return bass.ds(n * TB, TB)


def chunk(ln, n, ch):
    return ln["xs"][:, slot(n), ch * E:(ch + 1) * E].rearrange("p a e -> p (a e)")


def ln_load(sp, ln, src, n, par):
    sp.dma_start(ln["xs"][:, slot(n), :].rearrange("p a (c e) -> p (a c) e", c=NC),
                 src[rows(n), :].rearrange("(c p) e -> p c e", p=P)).then_inc(ln["x_in"][par], 16)


def ln_stats(dve, ln, n, half, par):
    dve.wait_ge(ln["x_in"][par], 16 * (half + 1))
    for ch in range(NC):
        last = dve.bn_stats(ln["st"][:, ch, :], chunk(ln, n, ch))
    last.then_inc(ln["stat"], 1)


def ln_var(dve, ln, n):
    for ch in range(NC):
        last = dve.bn_aggr(ln["mv"][:, ch, :], ln["st"][:, ch, :])
    last.then_inc(ln["var"], 1)
    dve.wait_ge(ln["var"], n + 1)
    dve.tensor_scalar(ln["ve"][:, :], ln["mv"][:, :, 1], EPS, None, ALU.add).then_inc(ln["ve_ready"], 1)


def ln_rstd(pool, ln, mhalf, n):
    pool.wait_ge(ln["ve_ready"], n + 1)
    pool.tensor_tensor(out=ln["rs"][:, :], in0=ln["ve"][:, :], in1=mhalf[:, :], op=ALU.pow).then_inc(ln["rstd"], 1)


def ln_apply(dve, ln, n):
    dve.wait_ge(ln["rstd"], n + 1)
    for ch in range(NC):
        last = dve.tensor_scalar(ln["xn"][:, ch, :], chunk(ln, n, ch), ln["mv"][:, ch, 0:1], ln["rs"][:, ch:ch + 1],
                                 ALU.subtract, ALU.mult)
    last.then_inc(ln["xn_ready"], 1)


def setup(nc, sb, sem, wait, env):
    bank, lvl2, ident, flags, mhalf, masks = (env[n] for n in ("bank", "lvl2", "ident", "flags", "mhalf", "masks"))
    scl, sft, gab, W, ln = (env[n] for n in ("scl", "sft", "gab", "W", "ln1"))
    wmod, c = env["wmod"], env["c"]
    GATES = (2, 5)
    COLS = (1, 0, 4, 3)
    ORDER = (1, 0, 2, 4, 3, 5)
    with ExitStack() as ctx:
        mod_raw = [sb(ctx, f"mod_raw{n}", [P, KT, E]) for n in range(3)] + env["ffn_raw"]
        mod_raw.append(mod_raw[0])
        raw = {n: sb(ctx, f"raw_{n}", [P, KT, E]) for n in "qkvo"}
        raw["g1"] = sb(ctx, "raw_g1", [P, KT, P])
        raw["g2"] = sb(ctx, "raw_g2", [P, 1, E])
        vrows = sb(ctx, "vrows", [(B + 3) * KT, P])
        cT, nw = env["vec"][:, 0:B * KT], env["vec"][:, B * KT:(B + 1) * KT]
        csig = sb(ctx, "csig", [P, B * KT])
        csil = sb(ctx, "csil", [P, B, KT])
        mean_m = sb(ctx, "mean_m", [P, P])
        mean_sb = sb(ctx, "mean_sb", [P, 1, E])
        sel = sb(ctx, "sel", [B, B, P])
        mrow = sb(ctx, "mrow", [B, 6, E])
        gmag = sb(ctx, "gmag", [B, 2, E])
        gsgn = sb(ctx, "gsgn", [B, 2, E])
        mcol = sb(ctx, "mcol", [P, 4, KT, B])
        maskf = sb(ctx, "maskf", [P, 5, 64])

        small_in, vec_turned, vec_sb = (sem(ctx, n) for n in ("small_in", "vec_turned", "vec_sb"))
        mod_in = [sem(ctx, f"mod_in{n}") for n in range(6)]
        raw_in = {n: sem(ctx, f"raw_in_{n}") for n in ("q", "k", "v", "o", "g1", "g2")}
        sig_ready, silu_ready, mod_ready, row_sb, cols_ready, gate_rows, gates_spread = (
            sem(ctx, n) for n in ("sig_ready", "silu_ready", "mod_ready", "row_sb", "cols_ready", "gate_rows", "gates_spread"))
        const_set, step_pool = sem(ctx, "const_set"), sem(ctx, "step_pool")
        mcopy, mag, hi_done, wo_scaled, mean_ready, mean_copied, wo_centred = (
            sem(ctx, n) for n in ("mcopy", "mag", "hi_done", "wo_scaled", "mean_ready", "mean_copied", "wo_centred"))
        order = ["q", "k", "o", "v", "g1", "g2"]

        with nc.Block() as block:
            @block.sync
            def _(sp):
                sp.dma_start(vrows[0:B * KT, :], c.rearrange("b (k p) -> (b k) p", p=P)).then_inc(small_in, 16)
                for n, src in enumerate((env["norm_w"], env["mu_r"], env["mu_k"])):
                    sp.dma_start(vrows[(B + n) * KT:(B + n + 1) * KT, :], src.rearrange("(k p) -> k p", p=P)).then_inc(small_in, 16)
                ln_load(sp, ln, env["xf"], 0, 0)
                for n, v in enumerate(ORDER):
                    if n == 5:
                        sp.wait_ge(mod_ready, 1)
                    sp.dma_start(mod_raw[n][:, :, :], wmod[:, v * E:(v + 1) * E].rearrange("(k p) n -> p k n", p=P)
                                 ).then_inc(mod_in[v], 16)
                ln_load(sp, ln, env["xf"], 1, 1)

            @block.scalar
            def _(act):
                for n in order:
                    act.dma_start(raw[n][:, :, :], env["w" + n].rearrange("(k p) n -> p k n", p=P)).then_inc(raw_in[n], 16)
                act.wait_ge(vec_sb, 1)
                act.activation(csig[:, :], cT, ACT.Sigmoid).then_inc(sig_ready, 1)

                def mod_row(n):
                    act.wait_ge(mod_ready, n + 1)
                    act.copy(mrow[:, ORDER[n], :], bank[n][0:B, :]).then_inc(row_sb, 1)

                def high(name):
                    if name == "o":
                        act.wait_ge(wo_centred, 1)
                    else:
                        act.wait_ge(raw_in[name], 16)
                    act.copy(W[name][0][:, :, :], raw[name][:, :, :]).then_inc(hi_done, 1)
                high("q")
                mod_row(0)
                mod_row(1)
                high("k")
                act.wait_ge(mean_ready, 1)
                act.copy(mean_sb[:, 0, :], lvl2[:, 512:1024]).then_inc(mean_copied, 1)
                mod_row(2)
                high("v")
                high("g1")
                high("g2")
                for n in range(3, 6):
                    mod_row(n)
                high("o")
                for n in range(2 * B):
                    act.wait_ge(gates_spread, n + 1)
                    act.copy(gab[:, n, :], bank[n][:, :])

            @block.gpsimd
            def _(pool):
                pool.memset(ident[:, :], 0.0).then_inc(step_pool, 1)
                pool.memset(maskf[:, :, :], 1.0).then_inc(step_pool, 1)
                pool.memset(flags[:, :], 1.0).then_inc(step_pool, 1)
                pool.memset(sel[:, :, :], 1.0).then_inc(step_pool, 1)
                pool.memset(mhalf[:, :], -0.5).then_inc(step_pool, 1)
                pool.memset(mean_m[:, :], 1.0 / E).then_inc(const_set, 1)
                pool.wait_ge(step_pool, 5)
                pool.affine_select(out=ident[:, :], in_=ident[:, :], compare_op=ALU.not_equal, fill=1.0,
                                   base=0, pattern=[[-1, P]], channel_multiplier=1).then_inc(const_set, 1)
                pool.affine_select(out=sel[:, :, :], in_=sel[:, :, :], compare_op=ALU.is_equal, fill=0.0,
                                   base=0, pattern=[[-1, B], [0, P]], channel_multiplier=1).then_inc(const_set, 1)
                for b in range(B):
                    pool.memset(flags[:, b * BPB:b * BPB + 1], 0.0)
                ln_rstd(pool, ln, mhalf, 0)
                for n, m in enumerate(LEVELS[:5]):
                    nb = 64 // m
                    view = maskf[:, n, :].rearrange("p (n m) -> p n m", m=m)
                    pool.affine_select(out=view, in_=view, compare_op=ALU.is_ge, fill=0.0, base=0,
                                       pattern=[[-2 * m, nb], [0, m]], channel_multiplier=1).then_inc(step_pool, 1)
                    pool.wait_ge(step_pool, 6 + 2 * n)
                    pool.affine_select(out=view, in_=view, compare_op=ALU.is_ge, fill=0.0, base=m - 1,
                                       pattern=[[2 * m, nb], [0, m]], channel_multiplier=-1).then_inc(step_pool, 1)

            @block.vector
            def _(dve):
                dve.wait_ge(vec_turned, 1)
                dve.tensor_copy(env["vec"][:, :], bank[5][:, 0:(B + 3) * KT]).then_inc(vec_sb, 1)
                dve.wait_ge(sig_ready, 1)
                dve.tensor_tensor(out=csil[:, :, :].rearrange("p b k -> p (b k)"), in0=cT, in1=csig[:, :], op=ALU.mult).then_inc(silu_ready, 1)
                ln_stats(dve, ln, 0, 0, 0)
                dve.wait_ge(ln["stat"], 1)
                ln_var(dve, ln, 0)
                ln_apply(dve, ln, 0)

                def low(name, n):
                    dve.wait_ge(hi_done, n)
                    hi, lo = W[name]
                    dve.tensor_tensor(out=lo[:, :, :], in0=raw[name][:, :, :], in1=hi[:, :, :].bitcast(F32), op=ALU.subtract)

                def cols(n):
                    dve.wait_ge(cols_ready, n + 1)
                    half = mcol[:, 2 * n:2 * n + 2, :, :]
                    dve.tensor_copy(half.rearrange("p v k b -> p (v k b)"), lvl2[:, n * 2 * KT * B:(n + 1) * 2 * KT * B]).then_inc(mcopy, 1)
                    dve.wait_ge(mcopy, n + 1)
                    for b in range(B):
                        blocks = slice(b * BPB, (b + 1) * BPB)
                        dve.tensor_scalar(scl[n][:, blocks, :], mcol[:, 2 * n:2 * n + 1, :, b].to_broadcast([P, BPB, KT]),
                                          1.0, None, ALU.add)
                        dve.tensor_copy(sft[n][:, blocks, :], mcol[:, 2 * n + 1:2 * n + 2, :, b].to_broadcast([P, BPB, KT]))

                low("q", 1)
                dve.wait_ge(raw_in["o"], 16)
                for k in range(KT):
                    last = dve.tensor_scalar(raw["o"][:, k, :], raw["o"][:, k, :], nw[:, k:k + 1], None, ALU.mult)
                last.then_inc(wo_scaled, 1)
                low("k", 2)
                cols(0)
                dve.wait_ge(mean_copied, 1)
                dve.tensor_tensor(out=raw["o"][:, :, :], in0=raw["o"][:, :, :],
                                  in1=mean_sb[:, :, :].to_broadcast([P, KT, E]), op=ALU.subtract).then_inc(wo_centred, 1)
                for n, name in enumerate(("v", "g1", "g2"), 3):
                    low(name, n)
                low("o", 6)
                dve.wait_ge(row_sb, 6)
                for n, v in enumerate(GATES):
                    dve.scalar_tensor_tensor(out=gmag[:, n, :], in0=mrow[:, v, :], scalar=-1.0, in1=mrow[:, v, :],
                                             op0=ALU.mult, op1=ALU.max)
                    last = dve.tensor_scalar(gsgn[:, n, :], mrow[:, v, :], 0.0, 2.0, ALU.is_ge, ALU.mult)
                last.then_inc(mag, 1)
                dve.wait_ge(mag, 1)
                dve.tensor_scalar(gmag[:, :, :], gmag[:, :, :], FLOOR, None, ALU.max).then_inc(mag, 1)
                dve.wait_ge(mag, 2)
                dve.scalar_tensor_tensor(out=gmag[:, :, :], in0=gsgn[:, :, :], scalar=-1.0, in1=gmag[:, :, :],
                                         op0=ALU.add, op1=ALU.mult).then_inc(gate_rows, 1)
                cols(1)
                dve.wait_ge(step_pool, 5 + 2 * 5)
                dve.tensor_copy(masks[:, :, :], maskf[:, :, :])

            @block.tensor
            def _(pe):
                pe.wait_ge(const_set, 3)
                pe.wait_ge(small_in, 64)
                n = (B + 3) * KT
                pe.transpose(bank[5][:, 0:n], vrows[:, :], ident[0:n, 0:n]).then_inc(vec_turned, 1)
                pe.wait_ge(silu_ready, 1)

                def mod_rows(n):
                    v = ORDER[n]
                    pe.wait_ge(mod_in[v], 16)
                    for k in range(KT):
                        last = pe.matmul(bank[n][0:B, :], csil[:, :, k], mod_raw[n][:, k, :], start=(k == 0), stop=(k == KT - 1))
                    last.then_inc(mod_ready, 1)

                def mod_cols(n):
                    pe.wait_ge(row_sb, 2 if n == 0 else 5)
                    wait(pe, mcopy, n)
                    for q in range(2):
                        for t in range(KT):
                            col = ((2 * n + q) * KT + t) * B
                            last = pe.transpose(lvl2[:, col:col + B], mrow[:, COLS[2 * n + q], t * P:(t + 1) * P], ident[0:B, 0:B])
                    last.then_inc(cols_ready, 1)

                mod_rows(0)
                mod_rows(1)
                pe.wait_ge(wo_scaled, 1)
                for k in range(KT):
                    last = pe.matmul(lvl2[:, 512:1024], mean_m[:, :], raw["o"][:, k, :], start=(k == 0), stop=(k == KT - 1))
                last.then_inc(mean_ready, 1)
                mod_cols(0)
                for n in range(2, 6):
                    mod_rows(n)
                mod_cols(1)
                pe.wait_ge(gate_rows, 1)
                for n in range(2):
                    for b in range(B):
                        pe.matmul(bank[n * B + b][:, :], sel[:, b, :], gmag[:, n, :], start=True, stop=True).then_inc(gates_spread, 1)


def attend(nc, sb, sem, wait, env):
    bank, lvl2, lbank, ident, flags, mhalf, masks = (env[n] for n in ("bank", "lvl2", "lbank", "ident", "flags", "mhalf", "masks"))
    W, gab, scl, sft, xf, x2d = (env[n] for n in ("W", "gab", "scl", "sft", "xf", "x2d"))
    ffn_raw, w_in, ln = env["ffn_raw"], env["w_in"], env["ln1"]
    xs, xn = ln["xs"], ln["xn"]
    with ExitStack() as ctx:
        tick = sb(ctx, "tick", [P, 1])
        ticked = sem(ctx, "ticked")
        hF = sb(ctx, "hF", [P, KT, TB])
        hT = [sb(ctx, f"hT_{part}", [P, KT, TB], F32R) for part in ("hi", "lo")]
        Q = [sb(ctx, f"Q{n}", [P, G, P]) for n in range(2)]
        K = [sb(ctx, f"K{n}", [P, G, P]) for n in range(2)]
        f = sb(ctx, "f", [P, G, P])
        Qo = sb(ctx, "Qo", [P, G, P // 2])
        V = [sb(ctx, f"V{n}", [P, NC, E]) for n in range(2)]
        og = [sb(ctx, f"og{n}", [P, NC, E]) for n in range(2)]
        g1 = [sb(ctx, f"g1_{part}", [P, TB], F32R) for part in ("hi", "lo")]
        eq = sb(ctx, "eq", [P, E])
        Tot = sb(ctx, "Tot", [P, G * P])
        A = sb(ctx, "A", [P, G, P])
        Kt = sb(ctx, "Kt", [P, NC, H, P])
        S = [sb(ctx, f"S{n}", [P, H, P]) for n in range(NC)]
        ogT = [sb(ctx, f"ogT_{part}", [P, NC, KT, P], F32R) for part in ("hi", "lo")]
        y = sb(ctx, "y", [P, NC, E])
        sto = sb(ctx, "sto", [P, NC, 6])
        mvo = sb(ctx, "mvo", [P, NC, 2])
        veo = sb(ctx, "veo", [P, NC])
        rso = sb(ctx, "rso", [P, NC])

        x_out = [sem(ctx, f"x_out{n}") for n in range(2)]
        mm = {n: sem(ctx, f"mm_{n}") for n in ("t1", "q", "k", "v", "g1", "gate", "lvl", "kt", "o", "ds", "t2", "wo")}
        h_full, q_sig, k_f, v_sb, g1_hi, gate_sb, kt_sb, ogt_hi, merged_act = (
            sem(ctx, n) for n in ("h_full", "q_sig", "k_f", "v_sb", "g1_hi", "gate_sb", "kt_sb", "ogt_hi", "merged_act"))
        h_hi, q_sb, qodd, f_eq, f_sb, level, merged, g1_lo, ogt_lo, s_mid, s_new, og_sb, sto_s, varo, ve_o, y_sb, s_flag = (
            sem(ctx, n) for n in ("h_hi", "q_sb", "qodd", "f_eq", "f_sb", "level", "merged", "g1_lo", "ogt_lo",
                                  "s_mid", "s_new", "og_sb", "sto_s", "varo", "ve_o", "y_sb", "s_flag"))
        rstdo, h_lo, x2_sb = (sem(ctx, n) for n in ("rstdo", "h_lo", "x2_sb"))

        def run(eng, start, body):
            start()
            body(0, 0, True, True, False)
            body(0, 1, True, True, True)
            with eng.Fori(1, NB // 2 - 1) as half:
                body(half, 0, True, True, True)
                body(half, 1, True, True, True)
            body(NB // 2 - 1, 0, True, False, True)
            body(NB // 2 - 1, 1, False, False, True)

        def level_bank(idx):
            return bank[3][:, :] if idx == 1 else lbank[idx % 2]

        with nc.Block() as block:
            @block.sync
            def _(sp):
                def store(n, half, par):
                    wait(sp, x2_sb, 2 * (n + 1))
                    sp.dma_start(x2d[rows(n), :].rearrange("(c p) e -> p c e", p=P),
                                 xs[:, slot(n), :].rearrange("p a (c e) -> p (a c) e", c=NC)).then_inc(x_out[par], 16)

                def body(half, par, has_next, has_next2, has_prev):
                    n = 2 * half + par
                    if has_next2:
                        wait(sp, x_out[par], 16 * half)
                        sp.wait_ge(ln["stat"], n + 1)
                        ln_load(sp, ln, xf, n + 2, par)
                    if has_prev:
                        store(n - 1, None, 1 - par)

                run(sp, lambda: None, body)
                store(NB - 1, None, (NB - 1) % 2)
                for q in range(2):
                    sp.wait_ge(x_out[q], 16 * (NB // 2))

            @block.gpsimd
            def _(pool):
                def carry(ticks):
                    wait(pool, ticked, ticks)
                    pool.tensor_tensor(out=tick[:, :], in0=mhalf[:, 0:1], in1=mhalf[:, 0:1], op=ALU.mult).then_inc(ticked, 1)

                def rstd_o(n):
                    pool.wait_ge(ve_o, n + 1)
                    pool.tensor_tensor(out=rso[:, :], in0=veo[:, :], in1=mhalf[:, :], op=ALU.pow).then_inc(rstdo, 1)

                def h_low(n):
                    wait(pool, h_hi, n + 1)
                    pool.tensor_tensor(out=hT[1][:, :, :], in0=hF[:, :, :], in1=hT[0][:, :, :].bitcast(F32),
                                       op=ALU.subtract).then_inc(h_lo, 1)

                def add(n, ch):
                    wait(pool, y_sb, 2 * n + ch + 1)
                    carry(2 * n + ch)
                    dst = xs[:, slot(n), ch * E:(ch + 1) * E].rearrange("p a e -> p (a e)")
                    pool.tensor_tensor(out=dst, in0=dst, in1=y[:, ch, :], op=ALU.add).then_inc(x2_sb, 1)

                def start():
                    h_low(0)
                    ln_rstd(pool, ln, mhalf, 1)
                    h_low(1)

                def body(half, par, has_next, has_next2, has_prev):
                    n = 2 * half + par
                    if has_prev:
                        rstd_o(n - 1)
                    if has_next2:
                        ln_rstd(pool, ln, mhalf, n + 2)
                    if has_prev:
                        add(n - 1, 0)
                    if has_next2:
                        h_low(n + 2)
                    if has_prev:
                        add(n - 1, 1)

                run(pool, start, body)
                rstd_o(NB - 1)
                add(NB - 1, 0)
                add(NB - 1, 1)

            @block.scalar
            def _(act):
                def h_affine(n):
                    wait(act, h_lo, n)
                    for k in range(KT):
                        if k % 2 == 0:
                            act.wait_ge(mm["t1"], 2 * n + k // 2 + 1)
                        src = bank[5 - 5 * (k // 2)][:, (k % 2) * TB:(k % 2 + 1) * TB]
                        act.activation(hF[:, k, :], src, ACT.Identity, scale=scl[0][:, bass.ds(n, 1), k],
                                       bias=sft[0][:, bass.ds(n, 1), k]).then_inc(h_full, 1)

                def q_gate(n, par, pair):
                    act.wait_ge(mm["q"], 2 * n + pair + 1)
                    act.activation(Q[par][:, 4 * pair:4 * pair + 4, :].rearrange("p g t -> p (g t)"), bank[2 + pair][:, :],
                                   ACT.Sigmoid).then_inc(q_sig, 1)

                def k_and_f(n, par, pair):
                    act.wait_ge(mm["k"], 2 * n + pair + 1)
                    act.activation(K[par][:, 4 * pair:4 * pair + 4, :].rearrange("p g t -> p (g t)"), bank[4 + pair][:, :], ACT.Sigmoid)
                    act.activation(f[:, 4 * pair:4 * pair + 4, :].rearrange("p g t -> p (g t)"), bank[4 + pair][:, :],
                                   ACT.Sigmoid, scale=-1.0).then_inc(k_f, 1)

                def v_copy(n, par, ch):
                    act.wait_ge(mm["v"], 2 * n + ch + 1)
                    act.copy(V[par][:, ch, :], bank[ch][:, :]).then_inc(v_sb, 1)

                def g1_high(n):
                    act.wait_ge(mm["g1"], n + 1)
                    act.copy(g1[0][:, :], bank[2][:, 0:TB]).then_inc(g1_hi, 1)

                def gate(n, par, ch):
                    wait(act, sto_s, 2 * (n - 1))
                    act.wait_ge(mm["gate"], 2 * n + ch + 1)
                    act.activation(og[par][:, ch, :], bank[ch][:, :], ACT.Sigmoid).then_inc(gate_sb, 1)

                def start():
                    for n, src in enumerate((env["W_r"], env["W_k"])):
                        act.dma_start(ffn_raw[n][:, :, :], src.rearrange("(k p) n -> p k n", p=P)).then_inc(w_in, 16)
                    h_affine(0)
                    for pair in range(2):
                        q_gate(0, 0, pair)
                    for pair in range(2):
                        k_and_f(0, 0, pair)
                    for ch in range(NC):
                        v_copy(0, 0, ch)
                    g1_high(0)
                    for ch in range(NC):
                        gate(0, 0, ch)
                    h_affine(1)

                def body(half, par, has_next, has_next2, has_prev):
                    n = 2 * half + par
                    if has_prev:
                        for ch in range(NC):
                            act.wait_ge(mm["t2"], 2 * (n - 1) + ch + 1)
                            act.copy(ogT[0][:, ch, :, :].rearrange("p k t -> p (k t)"), bank[ch][:, :]).then_inc(ogt_hi, 1)
                    if has_next:
                        for pair in range(2):
                            q_gate(n + 1, 1 - par, pair)
                        for pair in range(2):
                            k_and_f(n + 1, 1 - par, pair)
                        v_copy(n + 1, 1 - par, 0)
                    act.wait_ge(mm["lvl"], NL * n + 7)
                    act.wait_ge(merged, 6 * n + 6)
                    src = level_bank(6).rearrange("p (g t) -> p g t", g=G)
                    for q in range(2):
                        last = act.copy(A[64 * q:64 * q + 32, :, 64 * q + 32:64 * q + 64],
                                        src[64 * q:64 * q + 32, :, 32 * q:32 * q + 32])
                    last.then_inc(merged_act, 1)
                    if has_next:
                        v_copy(n + 1, 1 - par, 1)
                    act.wait_ge(mm["lvl"], NL * n + 8)
                    act.copy(A[0:64, :, 64:128], level_bank(7).rearrange("p (g t) -> p g t", g=G)[0:64, :, :]).then_inc(merged_act, 1)
                    if has_next:
                        g1_high(n + 1)
                    for ch in range(NC):
                        act.wait_ge(mm["kt"], 2 * n + ch + 1)
                        act.copy(Kt[:, ch, :, :].rearrange("p h t -> p (h t)"), bank[4 + ch][:, :]).then_inc(kt_sb, 1)
                    if has_next:
                        for ch in range(NC):
                            gate(n + 1, 1 - par, ch)
                    if has_next2:
                        h_affine(n + 2)

                run(act, start, body)
                for ch in range(NC):
                    act.wait_ge(mm["t2"], 2 * (NB - 1) + ch + 1)
                    act.copy(ogT[0][:, ch, :, :].rearrange("p k t -> p (k t)"), bank[ch][:, :]).then_inc(ogt_hi, 1)

            @block.vector
            def _(dve):
                def h_high(n):
                    dve.wait_ge(h_full, 4 * (n + 1))
                    dve.tensor_copy(hT[0][:, :, :], hF[:, :, :]).then_inc(h_hi, 1)

                def q_silu(n, par, pair):
                    dve.wait_ge(q_sig, 2 * n + pair + 1)
                    dst = Q[par][:, 4 * pair:4 * pair + 4, :].rearrange("p g t -> p (g t)")
                    dve.scalar_tensor_tensor(out=dst, in0=bank[2 + pair][:, :], scalar=QSCALE, in1=dst,
                                             op0=ALU.mult, op1=ALU.mult).then_inc(q_sb, 1)

                def f_signed(n, par, pair):
                    dve.wait_ge(k_f, 2 * n + pair + 1)
                    dst = f[:, 4 * pair:4 * pair + 4, :].rearrange("p g t -> p (g t)")
                    wait(dve, f_sb, 2 * n + pair)
                    dve.tensor_scalar(eq[:, :], dst, 0.5, 2.0, ALU.is_equal, ALU.mult).then_inc(f_eq, 1)
                    dve.wait_ge(f_eq, 2 * n + pair + 1)
                    dve.scalar_tensor_tensor(out=dst, in0=eq[:, :], scalar=-1.0, in1=dst,
                                             op0=ALU.add, op1=ALU.mult).then_inc(f_sb, 1)

                def q_odd(n, par):
                    dve.wait_ge(f_sb, 2 * (n + 1))
                    dve.wait_ge(q_sb, 2 * (n + 1))
                    dve.tensor_tensor(out=Qo[:, :, :], in0=Q[par][:, :, 1::2], in1=f[:, :, 1::2], op=ALU.mult).then_inc(qodd, 1)

                def g1_low(n):
                    dve.wait_ge(g1_hi, n + 1)
                    dve.tensor_tensor(out=g1[1][:, :], in0=bank[2][:, 0:TB], in1=g1[0][:, :].bitcast(F32),
                                      op=ALU.subtract).then_inc(g1_lo, 1)

                def ogt_low(n, ch):
                    dve.wait_ge(ogt_hi, 2 * n + ch + 1)
                    dve.tensor_tensor(out=ogT[1][:, ch, :, :].rearrange("p k t -> p (k t)"), in0=bank[ch][:, :],
                                      in1=ogT[0][:, ch, :, :].rearrange("p k t -> p (k t)").bitcast(F32),
                                      op=ALU.subtract).then_inc(ogt_lo, 1)

                def wo_scale(n, ch, b):
                    dve.wait_ge(mm["wo"], 2 * n + ch + 1)
                    dve.wait_ge(rstdo, n + 1)
                    wait(dve, x2_sb, 2 * (n - 1) + ch + 1)
                    dve.scalar_tensor_tensor(out=y[:, ch, :], in0=bank[3 - 2 * ch][:, :], scalar=rso[:, ch:ch + 1],
                                             in1=gab[:, bass.ds(b, 1), :].rearrange("p a e -> p (a e)"),
                                             op0=ALU.mult, op1=ALU.mult).then_inc(y_sb, 1)

                def tots(par, m):
                    cnt = G * P // m
                    off = G * P - 2 * cnt
                    t = f[:, :, :].rearrange("p g t -> p (g t)") if m == 1 else Tot[:, off:off + cnt]
                    return t.rearrange("p (n two) -> p n two", two=2)

                def level_update(n, par, m, idx, has_next2):
                    nb = G * P // (2 * m)
                    t = tots(par, m)
                    if m == 1:
                        dve.wait_ge(mm["lvl"], NL * n + 2)
                        dve.wait_ge(qodd, n + 1)
                        dve.wait_ge(merged, 6 * n + 1)
                        tq, tk = Q[par][:, :, :].rearrange("p g (n two) -> p g n two", two=2), K[par][:, :, 0::2]
                        fe = f[:, :, 0::2]
                        dve.tensor_tensor(out=tq[:, :, :, 1], in0=Qo[:, :, :], in1=fe, op=ALU.mult)
                        dve.tensor_tensor(out=tq[:, :, :, 0], in0=tq[:, :, :, 0], in1=fe, op=ALU.mult)
                        dve.tensor_tensor(out=Tot[:, 0:G * P // 2].rearrange("p (g n) -> p g n", g=G), in0=fe, in1=f[:, :, 1::2], op=ALU.mult)
                        dve.tensor_tensor(out=tk, in0=tk, in1=f[:, :, 1::2], op=ALU.mult).then_inc(level, 1)
                        return
                    cnt2 = G * P // (2 * m)
                    off2 = G * P - 2 * cnt2
                    dve.wait_ge(mm["lvl"], NL * n + idx + 1)
                    dve.wait_ge(level, NU * n + idx - 1)
                    if idx <= 5:
                        dve.wait_ge(merged, 6 * n + idx)
                    if m == 32 and has_next2:
                        dve.wait_ge(ln["stat"], n + 3)
                    dve.tensor_tensor(out=Tot[:, off2:off2 + cnt2], in0=t[:, :, 0], in1=t[:, :, 1], op=ALU.mult)
                    q = Q[par][:, :, :].rearrange("p g t -> p (g t)").rearrange("p (n two m) -> p n two m", two=2, m=m)[:, :, 1, :]
                    k = K[par][:, :, :].rearrange("p g t -> p (g t)").rearrange("p (n two m) -> p n two m", two=2, m=m)[:, :, 0, :]
                    dve.tensor_tensor(out=q, in0=q, in1=t[:, :, 0:1].to_broadcast([P, nb, m]), op=ALU.mult)
                    dve.tensor_tensor(out=k, in0=k, in1=t[:, :, 1:2].to_broadcast([P, nb, m]), op=ALU.mult).then_inc(level, 1)

                def level_merge(n, m, idx):
                    nb = 64 // m
                    dst = A[:, :, :].rearrange("p g (n two m) -> p g n two m", two=2, m=m)[:, :, :, 1, :]
                    src = level_bank(idx).rearrange("p (g n m) -> p g n m", g=G, m=m)
                    msk = masks[:, idx - 1, :].rearrange("p (n m) -> p n m", m=m).unsqueeze(1).to_broadcast([P, G, nb, m])
                    dve.copy_predicated(dst, msk, src).then_inc(merged, 1)

                def gated_var(n):
                    for ch in range(NC):
                        last = dve.bn_aggr(mvo[:, ch, :], sto[:, ch, :])
                    last.then_inc(varo, 1)
                    dve.wait_ge(varo, n + 1)
                    dve.tensor_scalar(veo[:, :], mvo[:, :, 1], EPS, None, ALU.add).then_inc(ve_o, 1)

                def start():
                    dve.memset(S[0][:, :, :], 0.0)
                    ln_stats(dve, ln, 1, 0, 1)
                    dve.wait_ge(ln["stat"], 2)
                    ln_var(dve, ln, 1)
                    h_high(0)
                    dve.wait_ge(mm["t1"], 2)
                    ln_apply(dve, ln, 1)
                    for pair in range(2):
                        q_silu(0, 0, pair)
                    for pair in range(2):
                        f_signed(0, 0, pair)
                    q_odd(0, 0)
                    g1_low(0)
                    h_high(1)

                def body(half, par, has_next, has_next2, has_prev):
                    n = 2 * half + par
                    prev_b = (n - 1) // BPB if has_prev else 0
                    dve.wait_ge(mm["lvl"], NL * n + 1)
                    wait(dve, sto_s, 2 * n)
                    wait(dve, mm["o"], 2 * n)
                    wait(dve, merged_act, 2 * n)
                    dve.tensor_tensor(out=A[:, :, :], in0=lvl2[:, :].rearrange("p (g t) -> p g t", g=G),
                                      in1=ident[:, :].unsqueeze(1).to_broadcast([P, G, P]), op=ALU.mult).then_inc(merged, 1)
                    if has_prev:
                        gated_var(n - 1)
                    for idx, m in enumerate(LEVELS, 1):
                        level_update(n, par, m, idx, has_next2)
                        if m <= 16:
                            level_merge(n, m, idx)
                        if m == 1 and has_prev:
                            ogt_low(n - 1, 0)
                            ogt_low(n - 1, 1)
                        if has_next and m in (2, 4):
                            q_silu(n + 1, 1 - par, m // 4)
                        if has_next and m in (8, 16):
                            f_signed(n + 1, 1 - par, m // 16)
                        if has_next and m == 16:
                            q_odd(n + 1, 1 - par)
                        if has_next2 and m == 16:
                            ln_stats(dve, ln, n + 2, half + 1, par)
                        if has_next2 and m == 32:
                            ln_var(dve, ln, n + 2)
                    if has_next2:
                        dve.wait_ge(mm["t1"], 2 * (n + 2))
                        ln_apply(dve, ln, n + 2)
                    if has_next:
                        g1_low(n + 1)
                    if has_prev:
                        wo_scale(n - 1, 0, prev_b)
                    def gated(ch):
                        dve.wait_ge(mm["o"], 2 * n + ch + 1)
                        dve.wait_ge(gate_sb, 2 * n + ch + 1)
                        bk = bank[2]
                        dve.tensor_tensor(out=og[par][:, ch, :], in0=bk[:, :], in1=og[par][:, ch, :], op=ALU.mult).then_inc(og_sb, 1)

                    def gated_stats(ch):
                        dve.wait_ge(og_sb, 2 * n + ch + 1)
                        dve.bn_stats(sto[:, ch, :], og[par][:, ch, :]).then_inc(sto_s, 1)

                    gated(0)
                    dve.wait_ge(mm["ds"], 2 * n + 1)
                    dve.wait_ge(level, NU * (n + 1))
                    wait(dve, s_flag, n)
                    tot = Tot[:, G * P - 2 * G:G * P - G].rearrange("p (h c) -> p h c", c=NC)
                    for h in range(H):
                        last = dve.scalar_tensor_tensor(out=S[1][:, h, :], in0=S[0][:, h, :], scalar=tot[:, h, 0:1],
                                                        in1=bank[3][:, h * P:(h + 1) * P], op0=ALU.mult, op1=ALU.add)
                    last.then_inc(s_mid, 1)
                    dve.wait_ge(mm["ds"], 2 * n + 2)
                    dve.wait_ge(s_mid, n + 1)
                    for h in range(H):
                        last = dve.scalar_tensor_tensor(out=S[0][:, h, :], in0=S[1][:, h, :], scalar=tot[:, h, 1:2],
                                                        in1=bank[4][:, h * P:(h + 1) * P], op0=ALU.mult, op1=ALU.add)
                    last.then_inc(s_new, 1)
                    dve.wait_ge(s_new, n + 1)
                    dve.tensor_scalar(S[0][:, :, :], S[0][:, :, :], flags[:, bass.ds(n + 1, 1)], None, ALU.mult).then_inc(s_flag, 1)
                    gated_stats(0)
                    if has_next2:
                        h_high(n + 2)
                    if has_prev:
                        wo_scale(n - 1, 1, prev_b)
                    gated(1)
                    gated_stats(1)

                run(dve, start, body)
                dve.wait_ge(sto_s, 2 * NB)
                gated_var(NB - 1)
                for ch in range(NC):
                    ogt_low(NB - 1, ch)
                for ch in range(NC):
                    wo_scale(NB - 1, ch, B - 1)

            @block.tensor
            def _(pe):
                def product(dst, lhs, rhs, steps):
                    terms = [(a, b, s) for s in range(steps) for a, b in ((0, 0), (0, 1), (1, 0))]
                    for t, (a, b, s) in enumerate(terms):
                        last = pe.matmul(dst, lhs(a, s), rhs(b, s), start=(t == 0), stop=(t == len(terms) - 1))
                    return last

                def t1(n):
                    pe.wait_ge(ln["xn_ready"], n + 1)
                    for k in range(KT):
                        for ch in range(NC):
                            col = (k % 2) * TB + ch * P
                            last = pe.transpose(bank[5 - 5 * (k // 2)][:, col:col + P], xn[:, ch, k * P:(k + 1) * P], ident[:, :])
                        if k % 2:
                            last.then_inc(mm["t1"], 1)

                def rows_of(name, pair, first, key):
                    for o in range(2):
                        h = 2 * pair + o
                        last = product(bank[first + pair][:, o * TB:(o + 1) * TB],
                                       lambda a, s: W[name][a][:, s, h * P:(h + 1) * P], lambda b, s: hT[b][:, s, :], KT)
                    last.then_inc(mm[key], 1)

                def v_rows(ch):
                    product(bank[ch][:, :], lambda a, s: hT[a][:, s, ch * P:(ch + 1) * P],
                            lambda b, s: W["v"][b][:, s, :], KT).then_inc(mm["v"], 1)

                def g1_rows():
                    product(bank[2][:, 0:TB], lambda a, s: W["g1"][a][:, s, :], lambda b, s: hT[b][:, s, :], KT).then_inc(mm["g1"], 1)

                def gate_rows(ch):
                    product(bank[ch][:, :], lambda a, s: g1[a][:, ch * P:(ch + 1) * P],
                            lambda b, s: W["g2"][b][:, s, :], 1).then_inc(mm["gate"], 1)

                def t2(n, par, ch):
                    pe.wait_ge(og_sb, 2 * n + ch + 1)
                    for k in range(KT):
                        last = pe.transpose(bank[ch][:, k * P:(k + 1) * P], og[par][:, ch, k * P:(k + 1) * P], ident[:, :])
                    last.then_inc(mm["t2"], 1)

                def wo_rows(n, ch):
                    pe.wait_ge(ogt_lo, 2 * n + ch + 1)
                    product(bank[3 - 2 * ch][:, :], lambda a, s: ogT[a][:, ch, s, :],
                            lambda b, s: W["o"][b][:, s, :], KT).then_inc(mm["wo"], 1)

                def start():
                    t1(0)
                    pe.wait_ge(h_lo, 1)
                    for pair in range(2):
                        rows_of("q", pair, 2, "q")
                    pe.wait_ge(h_full, 4)
                    for pair in range(2):
                        rows_of("k", pair, 4, "k")
                    for ch in range(NC):
                        v_rows(ch)
                    pe.wait_ge(q_sb, 1)
                    g1_rows()
                    pe.wait_ge(g1_lo, 1)
                    pe.wait_ge(v_sb, 2)
                    for ch in range(NC):
                        gate_rows(ch)
                    pe.wait_ge(k_f, 2)
                    pe.wait_ge(gate_sb, 1)
                    t1(1)

                def body(half, par, has_next, has_next2, has_prev):
                    n = 2 * half + par
                    q, k = Q[par], K[par]

                    def level_product(idx):
                        m = LEVELS[idx - 1]
                        if idx == 1:
                            pe.wait_ge(qodd, n + 1)
                            wait(pe, s_mid, n)
                        else:
                            pe.wait_ge(level, NU * n + idx - 1)
                            pe.wait_ge(merged, 6 * n + min(max(1, idx - 1), 6))
                        dst = level_bank(idx)
                        for g in range(G):
                            if m == 1:
                                last = pe.matmul(dst[:, g * 64:(g + 1) * 64], k[:, g, :], Qo[:, g, :], start=True, stop=True)
                            elif m <= 16:
                                rhs = q[:, g, :].rearrange("p (n two m) -> p n two m", two=2, m=m)[:, :, 1, :]
                                last = pe.matmul(dst[:, g * 64:(g + 1) * 64].rearrange("p (n m) -> p n m", m=m),
                                                 k[:, g, :], rhs, start=True, stop=True)
                            elif m == 32:
                                for b in range(2):
                                    last = pe.matmul(dst[64 * b:64 * b + 32, g * 64 + 32 * b:g * 64 + 32 * b + 32],
                                                     k[:, g, 64 * b:64 * b + 32], q[:, g, 64 * b + 32:64 * b + 64], start=True, stop=True)
                            else:
                                last = pe.matmul(dst[0:64, g * 64:(g + 1) * 64], k[:, g, 0:64], q[:, g, 64:128], start=True, stop=True)
                        last.then_inc(mm["lvl"], 1)

                    pe.wait_ge(q_sb, 2 * (n + 1))
                    pe.wait_ge(k_f, 2 * (n + 1))
                    wait(pe, merged_act, 2 * n)
                    for g in range(G):
                        last = pe.matmul(lvl2[:, g * P:(g + 1) * P], k[:, g, :], q[:, g, :], start=True, stop=True)
                    last.then_inc(mm["lvl"], 1)
                    level_product(1)
                    if has_prev:
                        if has_next:
                            pe.wait_ge(h_full, 4 * (n + 2))
                        t2(n - 1, 1 - par, 0)
                        wait(pe, y_sb, 2 * (n - 1))
                        t2(n - 1, 1 - par, 1)
                    if has_next:
                        pe.wait_ge(h_lo, n + 2)
                        wait(pe, og_sb, 2 * n)
                        rows_of("q", 0, 2, "q")
                    level_product(2)
                    if has_next:
                        pe.wait_ge(merged, 6 * n + 2)
                        rows_of("q", 1, 2, "q")
                    level_product(3)
                    if has_next:
                        wait(pe, s_new, n)
                        rows_of("k", 0, 4, "k")
                    level_product(4)
                    if has_next:
                        pe.wait_ge(h_full, 4 * (n + 2))
                        rows_of("k", 1, 4, "k")
                    level_product(5)
                    if has_next:
                        pe.wait_ge(gate_sb, 2 * (n + 1))
                        wait(pe, ogt_lo, 2 * n)
                        v_rows(0)
                    level_product(6)
                    if has_next:
                        v_rows(1)
                    level_product(7)
                    if has_next:
                        pe.wait_ge(q_sb, 2 * (n + 2))
                        g1_rows()
                    if has_prev:
                        wait(pe, s_mid, n)
                        wo_rows(n - 1, 0)
                    pe.wait_ge(level, NU * (n + 1))
                    if has_next:
                        pe.wait_ge(k_f, 2 * (n + 2))
                    for ch in range(NC):
                        for h in range(H):
                            last = pe.transpose(bank[4 + ch][:, h * P:(h + 1) * P], k[:, h * NC + ch, :], ident[:, :])
                        last.then_inc(mm["kt"], 1)
                    if has_next:
                        pe.wait_ge(g1_lo, n + 2)
                        for ch in range(NC):
                            pe.wait_ge(v_sb, 2 * (n + 1) + ch + 1)
                            gate_rows(ch)

                    def output(ch):
                        for h in range(H):
                            g = h * NC + ch
                            pe.matmul(bank[2][:, h * P:(h + 1) * P], q[:, g, :], S[ch][:, h, :], start=True, stop=False)
                            last = pe.matmul(bank[2][:, h * P:(h + 1) * P], A[:, g, :], V[par][:, ch, h * P:(h + 1) * P],
                                             start=False, stop=True)
                        last.then_inc(mm["o"], 1)

                    pe.wait_ge(merged_act, 2 * (n + 1))
                    wait(pe, s_flag, n)
                    pe.wait_ge(v_sb, 2 * (n + 1))
                    if has_next:
                        pe.wait_ge(g1_lo, n + 2)
                    output(0)
                    if has_prev:
                        pe.wait_ge(y_sb, 2 * (n - 1) + 1)
                    elif has_next:
                        pe.wait_ge(q_sb, 2 * (n + 2))
                    for ch in range(NC):
                        pe.wait_ge(kt_sb, 2 * n + ch + 1)
                        if ch == 1:
                            pe.wait_ge(kt_sb, 2 * n + 1)
                        for h in range(H):
                            last = pe.matmul(bank[3 + ch][:, h * P:(h + 1) * P], Kt[:, ch, h, :], V[par][:, ch, h * P:(h + 1) * P],
                                             start=True, stop=True)
                        last.then_inc(mm["ds"], 1)
                    if has_next2:
                        pe.wait_ge(kt_sb, 2 * (n + 1))
                        pe.wait_ge(gate_sb, 2 * (n + 1) + 1)
                        t1(n + 2)
                    if has_prev:
                        if has_next:
                            pe.wait_ge(gate_sb, 2 * (n + 2))
                        wo_rows(n - 1, 1)
                    pe.wait_ge(s_mid, n + 1)
                    pe.wait_ge(og_sb, 2 * n + 1)
                    output(1)

                run(pe, start, body)
                pe.wait_ge(y_sb, 2 * (NB - 1))
                for ch in range(NC):
                    t2(NB - 1, (NB - 1) % 2, ch)
                for ch in range(NC):
                    pe.wait_ge(s_mid, NB)
                    if ch == 1:
                        pe.wait_ge(ogt_lo, 2 * NB)
                    wo_rows(NB - 1, ch)


def ffn(nc, sb, sem, wait, env):
    ident, flags, mhalf = (env[n] for n in ("ident", "flags", "mhalf"))
    gab, scl, sft, x2d, of = (env[n] for n in ("gab", "scl", "sft", "x2d", "of"))
    bank8 = env["bank"] + env["lbank"]
    ffn_raw, w_in = env["ffn_raw"], env["w_in"]
    mur, muk = (env["vec"][:, (B + n) * KT:(B + n + 1) * KT] for n in (1, 2))
    KK, TT, RR, FV = bank8[0:2], bank8[2:4], bank8[4:6], bank8[6:8]
    with ExitStack() as ctx:
        W = {n: [sb(ctx, f"f{n}_{part}", [P, KT, E], F32R) for part in ("hi", "lo")] for n in "rkv"}
        ffn_raw = ffn_raw + [sb(ctx, "ffn_raw2", [P, KT, E])]
        ln = ln_state(ctx, sb, sem, "ln2")
        xs, xn = ln["xs"], ln["xn"]
        tick = sb(ctx, "ftick", [P, 1])
        ticked = sem(ctx, "fticked")
        h2 = sb(ctx, "h2", [P, KT, TB + 1])
        dd = sb(ctx, "dd", [P, KT, TB])
        xk32 = sb(ctx, "xk32", [P, KT, TB])
        xr32 = sb(ctx, "xr32", [P, KT, TB])
        xk = [sb(ctx, f"xk_{part}", [P, KT, TB], F32R) for part in ("hi", "lo")]
        xr = [sb(ctx, f"xr_{part}", [P, KT, TB], F32R) for part in ("hi", "lo")]
        rl = sb(ctx, "rl", [P, KT, TB])
        ka = [sb(ctx, f"ka_{part}", [P, KT, TB], F32R) for part in ("hi", "lo")]
        r = sb(ctx, "r", [P, NC, E])
        x_out = [sem(ctx, f"fx_out{n}") for n in range(2)]
        wt, wt_hi, wt_lo = sem(ctx, "wt"), sem(ctx, "wt_hi"), sem(ctx, "wt_lo")
        mm = {n: sem(ctx, f"fmm_{n}") for n in ("t", "k", "r", "v")}
        relu, ka_hi, h_sb, r_sig, xk_hi, xr_hi = (sem(ctx, n) for n in ("relu", "ka_hi", "h_sb", "r_sig", "xk_hi", "xr_hi"))
        halo, diff, xk_f, xr_f, xk_lo, xr_lo, sq, ka_lo, rv = (
            sem(ctx, n) for n in ("halo", "diff", "xk_f", "xr_f", "xk_lo", "xr_lo", "sq", "ka_lo", "rv"))
        r_gb, x3 = (sem(ctx, n) for n in ("r_gb", "x3"))

        def run(eng, start, body):
            start()
            body(0, 0, True, True, False)
            body(0, 1, True, True, True)
            with eng.Fori(1, NB // 2 - 1) as half:
                body(half, 0, True, True, True)
                body(half, 1, True, True, True)
            body(NB // 2 - 1, 0, True, False, True)
            body(NB // 2 - 1, 1, False, False, True)

        with nc.Block() as block:
            @block.sync
            def _(sp):
                def store(n, par):
                    wait(sp, x3, 2 * (n + 1))
                    sp.dma_start(of[rows(n), :].rearrange("(c p) e -> p c e", p=P),
                                 xs[:, slot(n), :].rearrange("p a (c e) -> p (a c) e", c=NC)).then_inc(x_out[par], 16)

                def start():
                    for n in range(2):
                        ln_load(sp, ln, x2d, n, n)

                def body(half, par, has_next, has_next2, has_prev):
                    n = 2 * half + par
                    if has_next2:
                        wait(sp, x_out[par], 16 * half)
                        sp.wait_ge(ln["stat"], n + 1)
                        ln_load(sp, ln, x2d, n + 2, par)
                    if has_prev:
                        store(n - 1, 1 - par)

                run(sp, start, body)
                store(NB - 1, (NB - 1) % 2)
                for q in range(2):
                    sp.wait_ge(x_out[q], 16 * (NB // 2))

            @block.gpsimd
            def _(pool):
                def carry(ticks):
                    wait(pool, ticked, ticks)
                    pool.tensor_tensor(out=tick[:, :], in0=mhalf[:, 0:1], in1=mhalf[:, 0:1], op=ALU.mult).then_inc(ticked, 1)

                def start():
                    ln_rstd(pool, ln, mhalf, 0)
                    ln_rstd(pool, ln, mhalf, 1)

                def body(half, par, has_next, has_next2, has_prev):
                    n = 2 * half + par
                    if has_next2:
                        ln_rstd(pool, ln, mhalf, n + 2)
                    for ch in range(NC):
                        pool.wait_ge(r_sig, 2 * n + ch + 1)
                        carry(4 * n + ch)
                        pool.tensor_tensor(out=r[:, ch, :], in0=r[:, ch, :],
                                           in1=gab[:, bass.ds(n // BPB + B, 1), :].rearrange("p a e -> p (a e)"),
                                           op=ALU.mult).then_inc(r_gb, 1)
                    for ch in range(NC):
                        pool.wait_ge(rv, 2 * n + ch + 1)
                        carry(4 * n + 2 + ch)
                        pool.tensor_tensor(out=chunk(ln, n, ch), in0=chunk(ln, n, ch), in1=r[:, ch, :], op=ALU.add).then_inc(x3, 1)

                run(pool, start, body)

            @block.scalar
            def _(act):
                def h_affine(n):
                    wait(act, halo, n + 1)
                    for k in range(KT):
                        if k % 2 == 0:
                            act.wait_ge(mm["t"], 2 * n + k // 2 + 1)
                        last = act.activation(h2[:, k, 1:TB + 1], TT[k // 2][:, (k % 2) * TB:(k % 2 + 1) * TB], ACT.Identity,
                                              scale=scl[1][:, bass.ds(n, 1), k], bias=sft[1][:, bass.ds(n, 1), k])
                    last.then_inc(h_sb, 1)

                def highs(n):
                    act.wait_ge(xk_f, n + 1)
                    wait(act, mm["k"], 2 * n)
                    act.copy(xk[0][:, :, :], xk32[:, :, :]).then_inc(xk_hi, 1)
                    act.wait_ge(xr_f, n + 1)
                    wait(act, mm["r"], 2 * n)
                    act.copy(xr[0][:, :, :], xr32[:, :, :]).then_inc(xr_hi, 1)

                def start():
                    act.dma_start(ffn_raw[2][:, :, :], env["W_v"].rearrange("(k p) n -> p k n", p=P)).then_inc(w_in, 16)
                    for u in range(3 * KT):
                        act.wait_ge(wt, u + 1)
                        act.copy(W["rkv"[u // KT]][0][:, u % KT, :], bank8[u % 8][:, :]).then_inc(wt_hi, 1)
                    h_affine(0)
                    highs(0)

                def body(half, par, has_next, has_next2, has_prev):
                    n = 2 * half + par
                    for pair in range(2):
                        act.wait_ge(mm["k"], 2 * n + pair + 1)
                        wait(act, ka_lo, 2 * n)
                        act.activation(rl[:, 2 * pair:2 * pair + 2, :].rearrange("p k t -> p (k t)"), KK[pair][:, :],
                                       ACT.Relu).then_inc(relu, 1)
                    for pair in range(2):
                        act.wait_ge(sq, 2 * n + pair + 1)
                        wait(act, mm["v"], 2 * n)
                        act.copy(ka[0][:, 2 * pair:2 * pair + 2, :], rl[:, 2 * pair:2 * pair + 2, :]).then_inc(ka_hi, 1)
                    if has_next:
                        h_affine(n + 1)
                    for ch in range(NC):
                        act.wait_ge(mm["r"], 2 * n + ch + 1)
                        wait(act, x3, 2 * n)
                        act.activation(r[:, ch, :], RR[ch][:, :], ACT.Sigmoid).then_inc(r_sig, 1)
                    if has_next:
                        highs(n + 1)

                run(act, start, body)

            @block.vector
            def _(dve):
                def shift(n):
                    dve.wait_ge(h_sb, n + 1)
                    prev = h2[:, :, 0:TB]
                    dve.tensor_tensor(out=dd[:, :, :], in0=h2[:, :, 1:TB + 1], in1=prev, op=ALU.subtract).then_inc(diff, 1)
                    dve.wait_ge(diff, n + 1)
                    for dst, mu, s in ((xk32, muk, xk_f), (xr32, mur, xr_f)):
                        for k in range(KT):
                            last = dve.scalar_tensor_tensor(out=dst[:, k, :], in0=dd[:, k, :], scalar=mu[:, k:k + 1],
                                                            in1=h2[:, k, 0:TB], op0=ALU.mult, op1=ALU.add)
                        last.then_inc(s, 1)
                    dve.wait_ge(xr_f, n + 1)
                    dve.tensor_scalar(h2[:, :, 0:1], h2[:, :, TB:TB + 1], flags[:, bass.ds(n + 1, 1)], None,
                                      ALU.mult).then_inc(halo, 1)

                def lows(n):
                    for part, full, hi_s, lo_s in ((xk, xk32, xk_hi, xk_lo), (xr, xr32, xr_hi, xr_lo)):
                        dve.wait_ge(hi_s, n + 1)
                        dve.tensor_tensor(out=part[1][:, :, :], in0=full[:, :, :], in1=part[0][:, :, :].bitcast(F32),
                                          op=ALU.subtract).then_inc(lo_s, 1)

                def start():
                    dve.memset(h2[:, :, 0:1], 0.0).then_inc(halo, 1)
                    ln_stats(dve, ln, 0, 0, 0)
                    dve.wait_ge(ln["stat"], 1)
                    ln_var(dve, ln, 0)
                    ln_apply(dve, ln, 0)
                    for u in range(3 * KT):
                        dve.wait_ge(wt_hi, u + 1)
                        w = W["rkv"[u // KT]]
                        dve.tensor_tensor(out=w[1][:, u % KT, :], in0=bank8[u % 8][:, :], in1=w[0][:, u % KT, :].bitcast(F32),
                                          op=ALU.subtract).then_inc(wt_lo, 1)
                    shift(0)
                    lows(0)
                    ln_stats(dve, ln, 1, 0, 1)
                    dve.wait_ge(ln["stat"], 2)
                    ln_var(dve, ln, 1)
                    dve.wait_ge(mm["t"], 2)
                    ln_apply(dve, ln, 1)

                def body(half, par, has_next, has_next2, has_prev):
                    n = 2 * half + par
                    for pair in range(2):
                        part = rl[:, 2 * pair:2 * pair + 2, :]
                        dve.wait_ge(relu, 2 * n + pair + 1)
                        dve.tensor_tensor(out=part, in0=part, in1=part, op=ALU.mult).then_inc(sq, 1)
                    for pair in range(2):
                        part = rl[:, 2 * pair:2 * pair + 2, :]
                        dve.wait_ge(ka_hi, 2 * n + pair + 1)
                        dve.tensor_tensor(out=ka[1][:, 2 * pair:2 * pair + 2, :], in0=part,
                                          in1=ka[0][:, 2 * pair:2 * pair + 2, :].bitcast(F32), op=ALU.subtract).then_inc(ka_lo, 1)
                    if has_next2:
                        ln_stats(dve, ln, n + 2, half + 1, par)
                    if has_next:
                        if has_next2:
                            dve.wait_ge(ln["stat"], n + 3)
                        shift(n + 1)
                        if has_next2:
                            ln_var(dve, ln, n + 2)
                        lows(n + 1)
                    if has_next2:
                        dve.wait_ge(mm["t"], 2 * (n + 2))
                        ln_apply(dve, ln, n + 2)
                    for ch in range(NC):
                        dve.wait_ge(mm["v"], 2 * n + ch + 1)
                        dve.wait_ge(r_gb, 2 * n + ch + 1)
                        dve.tensor_tensor(out=r[:, ch, :], in0=FV[ch][:, :], in1=r[:, ch, :], op=ALU.mult).then_inc(rv, 1)

                run(dve, start, body)

            @block.tensor
            def _(pe):
                def product(dst, lhs, rhs, steps):
                    terms = [(a, b, s) for s in range(steps) for a, b in ((0, 0), (0, 1), (1, 0))]
                    for t, (a, b, s) in enumerate(terms):
                        last = pe.matmul(dst, lhs(a, s), rhs(b, s), start=(t == 0), stop=(t == len(terms) - 1))
                    return last

                def transposes(n):
                    pe.wait_ge(ln["xn_ready"], n + 1)
                    wait(pe, h_sb, n)
                    for k in range(KT):
                        for ch in range(NC):
                            col = (k % 2) * TB + ch * P
                            last = pe.transpose(TT[k // 2][:, col:col + P], xn[:, ch, k * P:(k + 1) * P], ident[:, :])
                        if k % 2:
                            last.then_inc(mm["t"], 1)

                def start():
                    pe.wait_ge(w_in, 48)
                    for u in range(3 * KT):
                        wait(pe, wt_lo, u - 7)
                        for d in range(KT):
                            last = pe.transpose(bank8[u % 8][:, d * P:(d + 1) * P],
                                                ffn_raw[u // KT][:, d, (u % KT) * P:(u % KT + 1) * P], ident[:, :])
                        last.then_inc(wt, 1)
                    pe.wait_ge(wt_lo, 3 * KT)
                    transposes(0)

                def body(half, par, has_next, has_next2, has_prev):
                    n = 2 * half + par
                    pe.wait_ge(xk_lo, n + 1)
                    for d in range(KT):
                        if d % 2 == 0:
                            wait(pe, relu, 2 * (n - 1) + d // 2 + 1)
                        last = product(KK[d // 2][:, (d % 2) * TB:(d % 2 + 1) * TB],
                                       lambda a, s: W["k"][a][:, s, d * P:(d + 1) * P], lambda b, s: xk[b][:, s, :], KT)
                        if d % 2:
                            last.then_inc(mm["k"], 1)
                    if has_next:
                        transposes(n + 1)
                    pe.wait_ge(xr_lo, n + 1)
                    for ch in range(NC):
                        wait(pe, r_sig, 2 * (n - 1) + ch + 1)
                        product(RR[ch][:, :], lambda a, s: xr[a][:, s, ch * P:(ch + 1) * P],
                                lambda b, s: W["r"][b][:, s, :], KT).then_inc(mm["r"], 1)
                    pe.wait_ge(ka_lo, 2 * (n + 1))
                    for ch in range(NC):
                        wait(pe, rv, 2 * (n - 1) + ch + 1)
                        product(FV[ch][:, :], lambda a, s: ka[a][:, s, ch * P:(ch + 1) * P],
                                lambda b, s: W["v"][b][:, s, :], KT).then_inc(mm["v"], 1)

                run(pe, start, body)


_INS = ['L0_attn_x', 'L0_attn_wq', 'L0_attn_wk', 'L0_attn_wv', 'L0_attn_wo', 'L0_attn_wg1', 'L0_attn_wg2', 'L0_attn_norm_w',
        'L0_ffn_W_r', 'L0_ffn_W_k', 'L0_ffn_W_v', 'L0_ffn_mu_r', 'L0_ffn_mu_k', 'L0_c', 'L0_wmod']


def kernel(**inputs):
    import numpy as _np
    import concourse.bacc as _bacc
    from concourse import mybir as _mybir
    from concourse.bass_utils import run_bass_kernel_spmd as _run

    nc = _bacc.Bacc("TRN2", target_bir_lowering=False, num_devices=1)
    arrays, args = {}, []
    for name in _INS:
        a = _np.ascontiguousarray(inputs[name])
        arrays[f"in_{name}"] = a
        args.append(nc.dram_tensor(f"in_{name}", a.shape, _mybir.dt.from_np(a.dtype), kind="ExternalInput").ap())
    args.append(nc.dram_tensor("out_0", (B, T, E), _mybir.dt.float32, kind="ExternalOutput").ap())
    adaln_kernel(nc, *args)
    r = _run(nc, [arrays], core_ids=[0])
    return r.results[0]["out_0"]
```

```python
import concourse.bass as bass
from concourse import mybir
from contextlib import ExitStack

F32 = mybir.dt.float32
F32R = mybir.dt.float32r
I32 = mybir.dt.int32
ALU = mybir.AluOpType
ACT = mybir.ActivationFunctionType

P = 128
B, T, E = 2, 4096, 512
H = 4
KT = E // P
TB = 256
NC = TB // P
NB = B * T // TB
BPB = NB // B
G = H * NC
LEVELS = [1, 2, 4, 8, 16, 32, 64]
NL = len(LEVELS) + 1
NM = 8
NU = len(LEVELS)
EPS = 1e-5
FLOOR = 0.25
QSCALE = float(2 * P) ** -0.5
XS = 4


def adaln_kernel(nc, x, wq, wk, wv, wo, wg1, wg2, norm_w, W_r, W_k, W_v, mu_r, mu_k, c, wmod, out):
    xf = x.rearrange("b t e -> (b t) e")
    of = out.rearrange("b t e -> (b t) e")
    x2d = nc.dram_tensor("x2_scratch", (B * T, E), F32, kind="Internal").ap()

    def sb(ctx, name, shape, dt=F32):
        return ctx.enter_context(nc.sbuf_tensor(name, shape, dt))

    def sem(ctx, name):
        return ctx.enter_context(nc.semaphore(name))

    def wait(eng, s, value):
        if not isinstance(value, int) or value > 0:
            eng.wait_ge(s, value)

    with ExitStack() as top:
        bank = [top.enter_context(nc.psum_tensor(f"bank{n}", [P, 512], F32)) for n in range(6)]
        lvl2 = top.enter_context(nc.psum_tensor("lvl2", [P, 1024], F32))
        lbank = [lvl2[:, 0:512], lvl2[:, 512:1024]]

        ident = sb(top, "ident", [P, P])
        flags = sb(top, "flags", [P, NB + 1])
        mhalf = sb(top, "mhalf", [P, NC])
        scl = [sb(top, f"scl{n}", [P, NB, KT]) for n in range(2)]
        sft = [sb(top, f"sft{n}", [P, NB, KT]) for n in range(2)]
        gab = sb(top, "gab", [P, 2 * B, E])
        vec = sb(top, "vec", [P, (B + 3) * KT])
        ffn_raw = [sb(top, f"ffn_raw{n}", [P, KT, E]) for n in range(2)]
        w_in = sem(top, "w_in")
        x2_out = [sem(top, f"x2_out{n}") for n in range(2)]
        xs = sb(top, "xs", [P, XS, NC * E])
        xn = sb(top, "xn", [P, NC, E])
        ln1, ln2 = (ln_state(top, sb, sem, f"ln{n}", xs, xn) for n in (1, 2))

        attn = ExitStack()
        W = {}
        for name, kt, n in (("q", KT, E), ("k", KT, E), ("v", KT, E), ("o", KT, E), ("g1", KT, P), ("g2", 1, E)):
            W[name] = [sb(attn, f"w{name}_{part}", [P, kt, n], F32R) for part in ("hi", "lo")]
        masks = sb(attn, "masks", [P, 5, 64], I32)
        setup(nc, sb, sem, wait, locals())
        attend(nc, sb, sem, wait, locals())
        attn.close()
        ffn(nc, sb, sem, wait, locals())


def ln_state(ctx, sb, sem, name, xs, xn):
    return {
        "xs": xs, "xn": xn,
        "st": sb(ctx, f"{name}_st", [P, NC, 6]), "mv": sb(ctx, f"{name}_mv", [P, NC, 2]),
        "ve": sb(ctx, f"{name}_ve", [P, NC]), "rs": sb(ctx, f"{name}_rs", [P, NC]),
        "x_in": [sem(ctx, f"{name}_x_in{n}") for n in range(2)],
        "stat": sem(ctx, f"{name}_stat"), "var": sem(ctx, f"{name}_var"), "ve_ready": sem(ctx, f"{name}_ve_ready"),
        "rstd": sem(ctx, f"{name}_rstd"), "xn_ready": sem(ctx, f"{name}_xn_ready"),
    }


def slot(n):
    return bass.ds(n % XS, 1)


def rows(n):
    return bass.ds(n * TB, TB)


def chunk(ln, n, ch):
    return ln["xs"][:, slot(n), ch * E:(ch + 1) * E].rearrange("p a e -> p (a e)")


def ln_load(sp, ln, src, n, par):
    sp.dma_start(ln["xs"][:, slot(n), :].rearrange("p a (c e) -> p (a c) e", c=NC),
                 src[rows(n), :].rearrange("(c p) e -> p c e", p=P)).then_inc(ln["x_in"][par], 16)


def ln_stats(dve, ln, n, half, par):
    dve.wait_ge(ln["x_in"][par], 16 * (half + 1))
    for ch in range(NC):
        last = dve.bn_stats(ln["st"][:, ch, :], chunk(ln, n, ch))
    last.then_inc(ln["stat"], 1)


def ln_var(dve, ln, n):
    for ch in range(NC):
        last = dve.bn_aggr(ln["mv"][:, ch, :], ln["st"][:, ch, :])
    last.then_inc(ln["var"], 1)
    dve.wait_ge(ln["var"], n + 1)
    dve.tensor_scalar(ln["ve"][:, :], ln["mv"][:, :, 1], EPS, None, ALU.add).then_inc(ln["ve_ready"], 1)


def ln_rstd(pool, ln, mhalf, n):
    pool.wait_ge(ln["ve_ready"], n + 1)
    pool.tensor_tensor(out=ln["rs"][:, :], in0=ln["ve"][:, :], in1=mhalf[:, :], op=ALU.pow).then_inc(ln["rstd"], 1)


def ln_apply(dve, ln, n):
    dve.wait_ge(ln["rstd"], n + 1)
    for ch in range(NC):
        last = dve.tensor_scalar(ln["xn"][:, ch, :], chunk(ln, n, ch), ln["mv"][:, ch, 0:1], ln["rs"][:, ch:ch + 1],
                                 ALU.subtract, ALU.mult)
    last.then_inc(ln["xn_ready"], 1)


def setup(nc, sb, sem, wait, env):
    bank, lvl2, ident, flags, mhalf, masks = (env[n] for n in ("bank", "lvl2", "ident", "flags", "mhalf", "masks"))
    scl, sft, gab, W, ln = (env[n] for n in ("scl", "sft", "gab", "W", "ln1"))
    wmod, c = env["wmod"], env["c"]
    GATES = (2, 5)
    COLS = (1, 0, 4, 3)
    ORDER = (1, 0, 2, 5, 4, 3)
    with ExitStack() as ctx:
        mod_raw = [sb(ctx, f"mod_raw{n}", [P, KT, E]) for n in range(3)] + env["ffn_raw"]
        mod_raw.append(mod_raw[0])
        raw = {n: sb(ctx, f"raw_{n}", [P, KT, E]) for n in "qkvo"}
        raw["g1"] = sb(ctx, "raw_g1", [P, KT, P])
        raw["g2"] = sb(ctx, "raw_g2", [P, 1, E])
        vrows = sb(ctx, "vrows", [(B + 3) * KT, P])
        cT, nw = env["vec"][:, 0:B * KT], env["vec"][:, B * KT:(B + 1) * KT]
        csig = sb(ctx, "csig", [P, B * KT])
        csil = sb(ctx, "csil", [P, B, KT])
        mean_m = sb(ctx, "mean_m", [P, P])
        mean_sb = sb(ctx, "mean_sb", [P, 1, E])
        sel = sb(ctx, "sel", [B, B, P])
        mrow = sb(ctx, "mrow", [B, 6, E])
        gmag = sb(ctx, "gmag", [B, 2, E])
        gsgn = sb(ctx, "gsgn", [B, 2, E])
        mcol = sb(ctx, "mcol", [P, 4, KT, B])
        maskf = sb(ctx, "maskf", [P, 5, 64])

        small_in, vec_turned, vec_sb = (sem(ctx, n) for n in ("small_in", "vec_turned", "vec_sb"))
        mod_in = [sem(ctx, f"mod_in{n}") for n in range(6)]
        raw_in = {n: sem(ctx, f"raw_in_{n}") for n in ("q", "k", "v", "o", "g1", "g2")}
        sig_ready, silu_ready, mod_ready, row_sb, cols_ready, gate_rows, gates_spread = (
            sem(ctx, n) for n in ("sig_ready", "silu_ready", "mod_ready", "row_sb", "cols_ready", "gate_rows", "gates_spread"))
        const_set, step_pool = sem(ctx, "const_set"), sem(ctx, "step_pool")
        mcopy, mag, hi_done, wo_scaled, mean_ready, mean_copied, wo_centred = (
            sem(ctx, n) for n in ("mcopy", "mag", "hi_done", "wo_scaled", "mean_ready", "mean_copied", "wo_centred"))
        order = ["q", "k", "o", "v", "g1", "g2"]

        def vector_load(eng, n, src):
            eng.dma_start(vrows[(B + n) * KT:(B + n + 1) * KT, :], src.rearrange("(k p) -> k p", p=P)).then_inc(small_in, 16)

        with nc.Block() as block:
            @block.sync
            def _(sp):
                sp.dma_start(vrows[0:B * KT, :], c.rearrange("b (k p) -> (b k) p", p=P)).then_inc(small_in, 16)
                vector_load(sp, 1, env["mu_r"])
                for n, v in enumerate(ORDER):
                    if n == 5:
                        sp.wait_ge(mod_ready, 1)
                    sp.dma_start(mod_raw[n][:, :, :], wmod[:, v * E:(v + 1) * E].rearrange("(k p) n -> p k n", p=P)
                                 ).then_inc(mod_in[v], 16)
                    if n == 1:
                        ln_load(sp, ln, env["xf"], 0, 0)
                ln_load(sp, ln, env["xf"], 1, 1)

            @block.scalar
            def _(act):
                vector_load(act, 0, env["norm_w"])
                vector_load(act, 2, env["mu_k"])
                for n in order:
                    act.dma_start(raw[n][:, :, :], env["w" + n].rearrange("(k p) n -> p k n", p=P)).then_inc(raw_in[n], 16)
                act.wait_ge(vec_sb, 1)
                act.activation(csig[:, :], cT, ACT.Sigmoid).then_inc(sig_ready, 1)

                def mod_row(n):
                    act.wait_ge(mod_ready, n + 1)
                    act.copy(mrow[:, ORDER[n], :], bank[n][0:B, :]).then_inc(row_sb, 1)

                def high(name):
                    if name == "o":
                        act.wait_ge(wo_centred, 1)
                    else:
                        act.wait_ge(raw_in[name], 16)
                    act.copy(W[name][0][:, :, :], raw[name][:, :, :]).then_inc(hi_done, 1)
                high("q")
                mod_row(0)
                mod_row(1)
                high("k")
                act.wait_ge(mean_ready, 1)
                act.copy(mean_sb[:, 0, :], lvl2[:, 512:1024]).then_inc(mean_copied, 1)
                mod_row(2)
                mod_row(3)
                high("v")
                high("g1")
                high("g2")
                mod_row(4)
                high("o")

                def spread(n):
                    act.wait_ge(gates_spread, n + 1)
                    act.copy(gab[:, n, :], bank[n][:, :])
                spread(0)
                spread(1)
                mod_row(5)
                spread(2)
                spread(3)

            @block.gpsimd
            def _(pool):
                pool.memset(ident[:, :], 0.0).then_inc(step_pool, 1)
                pool.memset(maskf[:, :, :], 1.0).then_inc(step_pool, 1)
                pool.memset(flags[:, :], 1.0).then_inc(step_pool, 1)
                pool.memset(sel[:, :, :], 1.0).then_inc(step_pool, 1)
                pool.memset(mhalf[:, :], -0.5).then_inc(step_pool, 1)
                pool.memset(mean_m[:, :], 1.0 / E).then_inc(const_set, 1)
                pool.wait_ge(step_pool, 5)
                pool.affine_select(out=ident[:, :], in_=ident[:, :], compare_op=ALU.not_equal, fill=1.0,
                                   base=0, pattern=[[-1, P]], channel_multiplier=1).then_inc(const_set, 1)
                pool.affine_select(out=sel[:, :, :], in_=sel[:, :, :], compare_op=ALU.is_equal, fill=0.0,
                                   base=0, pattern=[[-1, B], [0, P]], channel_multiplier=1).then_inc(const_set, 1)
                for b in range(B):
                    pool.memset(flags[:, b * BPB:b * BPB + 1], 0.0)
                ln_rstd(pool, ln, mhalf, 0)
                for n, m in enumerate(LEVELS[:5]):
                    nb = 64 // m
                    view = maskf[:, n, :].rearrange("p (n m) -> p n m", m=m)
                    pool.affine_select(out=view, in_=view, compare_op=ALU.is_ge, fill=0.0, base=0,
                                       pattern=[[-2 * m, nb], [0, m]], channel_multiplier=1).then_inc(step_pool, 1)
                    pool.wait_ge(step_pool, 6 + 2 * n)
                    pool.affine_select(out=view, in_=view, compare_op=ALU.is_ge, fill=0.0, base=m - 1,
                                       pattern=[[2 * m, nb], [0, m]], channel_multiplier=-1).then_inc(step_pool, 1)

            @block.vector
            def _(dve):
                dve.wait_ge(vec_turned, 1)
                dve.tensor_copy(env["vec"][:, :], bank[5][:, 0:(B + 3) * KT]).then_inc(vec_sb, 1)
                dve.wait_ge(sig_ready, 1)
                dve.tensor_tensor(out=csil[:, :, :].rearrange("p b k -> p (b k)"), in0=cT, in1=csig[:, :],
                                  op=ALU.mult).then_inc(silu_ready, 1)
                def low(name, n):
                    dve.wait_ge(hi_done, n)
                    hi, lo = W[name]
                    dve.tensor_tensor(out=lo[:, :, :], in0=raw[name][:, :, :], in1=hi[:, :, :].bitcast(F32), op=ALU.subtract)

                def cols(n):
                    dve.wait_ge(cols_ready, n + 1)
                    half = mcol[:, 2 * n:2 * n + 2, :, :]
                    dve.tensor_copy(half.rearrange("p v k b -> p (v k b)"), lvl2[:, n * 2 * KT * B:(n + 1) * 2 * KT * B]).then_inc(mcopy, 1)
                    dve.wait_ge(mcopy, n + 1)
                    for b in range(B):
                        blocks = slice(b * BPB, (b + 1) * BPB)
                        dve.tensor_scalar(scl[n][:, blocks, :], mcol[:, 2 * n:2 * n + 1, :, b].to_broadcast([P, BPB, KT]),
                                          1.0, None, ALU.add)
                        dve.tensor_copy(sft[n][:, blocks, :], mcol[:, 2 * n + 1:2 * n + 2, :, b].to_broadcast([P, BPB, KT]))

                low("q", 1)
                dve.wait_ge(raw_in["o"], 16)
                for k in range(KT):
                    last = dve.tensor_scalar(raw["o"][:, k, :], raw["o"][:, k, :], nw[:, k:k + 1], None, ALU.mult)
                last.then_inc(wo_scaled, 1)
                cols(0)
                ln_stats(dve, ln, 0, 0, 0)
                dve.wait_ge(ln["stat"], 1)
                ln_var(dve, ln, 0)
                low("k", 2)
                ln_apply(dve, ln, 0)
                dve.wait_ge(mean_copied, 1)
                dve.tensor_tensor(out=raw["o"][:, :, :], in0=raw["o"][:, :, :],
                                  in1=mean_sb[:, :, :].to_broadcast([P, KT, E]), op=ALU.subtract).then_inc(wo_centred, 1)
                dve.wait_ge(row_sb, 4)
                for n, v in enumerate(GATES):
                    dve.scalar_tensor_tensor(out=gmag[:, n, :], in0=mrow[:, v, :], scalar=-1.0, in1=mrow[:, v, :],
                                             op0=ALU.mult, op1=ALU.max)
                    last = dve.tensor_scalar(gsgn[:, n, :], mrow[:, v, :], 0.0, 2.0, ALU.is_ge, ALU.mult)
                last.then_inc(mag, 1)
                dve.wait_ge(mag, 1)
                dve.tensor_scalar(gmag[:, :, :], gmag[:, :, :], FLOOR, None, ALU.max).then_inc(mag, 1)
                dve.wait_ge(mag, 2)
                dve.scalar_tensor_tensor(out=gmag[:, :, :], in0=gsgn[:, :, :], scalar=-1.0, in1=gmag[:, :, :],
                                         op0=ALU.add, op1=ALU.mult).then_inc(gate_rows, 1)
                for n, name in enumerate(("v", "g1", "g2", "o"), 3):
                    low(name, n)
                cols(1)
                dve.wait_ge(step_pool, 5 + 2 * 5)
                dve.tensor_copy(masks[:, :, :], maskf[:, :, :])

            @block.tensor
            def _(pe):
                pe.wait_ge(const_set, 3)
                pe.wait_ge(small_in, 64)
                n = (B + 3) * KT
                pe.transpose(bank[5][:, 0:n], vrows[:, :], ident[0:n, 0:n]).then_inc(vec_turned, 1)
                pe.wait_ge(silu_ready, 1)

                def mod_rows(n):
                    v = ORDER[n]
                    pe.wait_ge(mod_in[v], 16)
                    for k in range(KT):
                        last = pe.matmul(bank[n][0:B, :], csil[:, :, k], mod_raw[n][:, k, :], start=(k == 0), stop=(k == KT - 1))
                    last.then_inc(mod_ready, 1)

                def mod_cols(n):
                    pe.wait_ge(row_sb, 2 if n == 0 else 6)
                    wait(pe, mcopy, n)
                    for q in range(2):
                        for t in range(KT):
                            col = ((2 * n + q) * KT + t) * B
                            last = pe.transpose(lvl2[:, col:col + B], mrow[:, COLS[2 * n + q], t * P:(t + 1) * P], ident[0:B, 0:B])
                    last.then_inc(cols_ready, 1)

                def spread(n):
                    pe.wait_ge(row_sb, 4)
                    for b in range(B):
                        pe.matmul(bank[n * B + b][:, :], sel[:, b, :], gmag[:, n, :], start=True, stop=True).then_inc(gates_spread, 1)

                mod_rows(0)
                mod_rows(1)
                mod_cols(0)
                pe.wait_ge(wo_scaled, 1)
                for k in range(KT):
                    last = pe.matmul(lvl2[:, 512:1024], mean_m[:, :], raw["o"][:, k, :], start=(k == 0), stop=(k == KT - 1))
                last.then_inc(mean_ready, 1)
                for n in range(2, 5):
                    mod_rows(n)
                pe.wait_ge(gate_rows, 1)
                spread(0)
                mod_rows(5)
                spread(1)
                mod_cols(1)


def attend(nc, sb, sem, wait, env):
    bank, lvl2, lbank, ident, flags, mhalf, masks = (env[n] for n in ("bank", "lvl2", "lbank", "ident", "flags", "mhalf", "masks"))
    W, gab, scl, sft, xf, x2d = (env[n] for n in ("W", "gab", "scl", "sft", "xf", "x2d"))
    ffn_raw, w_in, ln = env["ffn_raw"], env["w_in"], env["ln1"]
    ln2, x_out, xs, xn = (env[n] for n in ("ln2", "x2_out", "xs", "xn"))
    with ExitStack() as ctx:
        tick = sb(ctx, "tick", [P, 1])
        ticked = sem(ctx, "ticked")
        hF = sb(ctx, "hF", [P, KT, TB])
        hT = [sb(ctx, f"hT_{part}", [P, KT, TB], F32R) for part in ("hi", "lo")]
        Qx = [sb(ctx, f"Q{n}", [P, G, P + P // 2]) for n in range(2)]
        Q, Qo = [t[:, :, 0:P] for t in Qx], [t[:, :, P:P + P // 2] for t in Qx]
        K = [sb(ctx, f"K{n}", [P, G, P]) for n in range(2)]
        f = sb(ctx, "f", [P, G, P])
        V = [sb(ctx, f"V{n}", [P, NC, E]) for n in range(2)]
        og = [sb(ctx, f"og{n}", [P, NC, E]) for n in range(2)]
        g1 = [sb(ctx, f"g1_{part}", [P, TB], F32R) for part in ("hi", "lo")]
        eq = sb(ctx, "eq", [P, E])
        Tot = sb(ctx, "Tot", [P, G * P])
        A = sb(ctx, "A", [P, G, P])
        Kt = sb(ctx, "Kt", [P, NC, H, P])
        S = [sb(ctx, f"S{n}", [P, H, P]) for n in range(NC)]
        ogT = [sb(ctx, f"ogT_{part}", [P, NC, KT, P], F32R) for part in ("hi", "lo")]
        y = sb(ctx, "y", [P, NC, E])
        sto = sb(ctx, "sto", [P, NC, 6])
        mvo = sb(ctx, "mvo", [P, NC, 2])
        veo = sb(ctx, "veo", [P, NC])
        rso = sb(ctx, "rso", [P, NC])

        mm = {n: sem(ctx, f"mm_{n}") for n in ("t1", "q", "k", "v", "g1", "gate", "lvl", "kt", "o", "ds", "t2", "wo")}
        h_full, q_sig, k_f, v_sb, g1_hi, gate_sb, kt_sb, ogt_hi, merged_act = (
            sem(ctx, n) for n in ("h_full", "q_sig", "k_f", "v_sb", "g1_hi", "gate_sb", "kt_sb", "ogt_hi", "merged_act"))
        h_hi, q_sb, qodd, f_eq, f_sb, level, merged, g1_lo, ogt_lo, s_mid, s_new, og_sb, sto_s, varo, ve_o, y_sb, s_flag = (
            sem(ctx, n) for n in ("h_hi", "q_sb", "qodd", "f_eq", "f_sb", "level", "merged", "g1_lo", "ogt_lo",
                                  "s_mid", "s_new", "og_sb", "sto_s", "varo", "ve_o", "y_sb", "s_flag"))
        rstdo, h_lo, x2_sb = (sem(ctx, n) for n in ("rstdo", "h_lo", "x2_sb"))

        def run(eng, start, body):
            start()
            body(0, 0, True, True, False)
            body(0, 1, True, True, True)
            with eng.Fori(1, NB // 2 - 1) as half:
                body(half, 0, True, True, True)
                body(half, 1, True, True, True)
            body(NB // 2 - 1, 0, True, False, True)
            body(NB // 2 - 1, 1, False, False, True)

        def level_bank(idx):
            return lbank[idx % 2]

        NEAR = [(slice(0, 4), lvl2[:, :].rearrange("p (b c) -> p b c", b=2)[:, :, 0:3 * P]),
                (slice(4, 6), bank[3][:, :].rearrange("p (b c) -> p b c", b=1)[:, :, 0:3 * P]),
                (slice(6, 8), bank[4][:, :].rearrange("p (b c) -> p b c", b=1)[:, :, 0:3 * P])]

        with nc.Block() as block:
            @block.sync
            def _(sp):
                def store(n, par):
                    wait(sp, x2_sb, 2 * (n + 1))
                    sp.dma_start(x2d[rows(n), :].rearrange("(c p) e -> p c e", p=P),
                                 xs[:, slot(n), :].rearrange("p a (c e) -> p (a c) e", c=NC)).then_inc(x_out[par], 16)

                def body(half, par, has_next, has_next2, has_prev):
                    n = 2 * half + par
                    if has_next2:
                        wait(sp, x_out[par], 16 * half)
                        sp.wait_ge(ln["stat"], n + 1)
                        ln_load(sp, ln, xf, n + 2, par)
                    if not has_next:
                        for q in range(2):
                            sp.wait_ge(x_out[q], 16 * (NB // 2 - 1))
                            ln_load(sp, ln2, x2d, q, q)
                    if has_prev:
                        store(n - 1, 1 - par)

                run(sp, lambda: None, body)
                store(NB - 1, (NB - 1) % 2)

            @block.gpsimd
            def _(pool):
                def carry(ticks):
                    wait(pool, ticked, ticks)
                    pool.tensor_tensor(out=tick[:, :], in0=mhalf[:, 0:1], in1=mhalf[:, 0:1], op=ALU.mult).then_inc(ticked, 1)

                def rstd_o(n):
                    pool.wait_ge(ve_o, n + 1)
                    pool.tensor_tensor(out=rso[:, :], in0=veo[:, :], in1=mhalf[:, :], op=ALU.pow).then_inc(rstdo, 1)

                def h_low(n):
                    wait(pool, h_hi, n + 1)
                    pool.tensor_tensor(out=hT[1][:, :, :], in0=hF[:, :, :], in1=hT[0][:, :, :].bitcast(F32),
                                       op=ALU.subtract).then_inc(h_lo, 1)

                def add(n, ch):
                    wait(pool, y_sb, 2 * n + ch + 1)
                    carry(2 * n + ch)
                    dst = xs[:, slot(n), ch * E:(ch + 1) * E].rearrange("p a e -> p (a e)")
                    pool.tensor_tensor(out=dst, in0=dst, in1=y[:, ch, :], op=ALU.add).then_inc(x2_sb, 1)

                def start():
                    h_low(0)
                    ln_rstd(pool, ln, mhalf, 1)
                    h_low(1)

                def body(half, par, has_next, has_next2, has_prev):
                    n = 2 * half + par
                    if has_prev:
                        rstd_o(n - 1)
                    if has_next2:
                        ln_rstd(pool, ln, mhalf, n + 2)
                    if has_prev:
                        add(n - 1, 0)
                    if has_next2:
                        h_low(n + 2)
                    if has_prev:
                        add(n - 1, 1)

                run(pool, start, body)
                rstd_o(NB - 1)
                ln_rstd(pool, ln2, mhalf, 0)
                add(NB - 1, 0)
                add(NB - 1, 1)

            @block.scalar
            def _(act):
                def h_affine(n):
                    wait(act, h_lo, n)
                    for k in range(KT):
                        if k % 2 == 0:
                            act.wait_ge(mm["t1"], 2 * n + k // 2 + 1)
                        src = bank[5 - 5 * (k // 2)][:, (k % 2) * TB:(k % 2 + 1) * TB]
                        act.activation(hF[:, k, :], src, ACT.Identity, scale=scl[0][:, bass.ds(n, 1), k],
                                       bias=sft[0][:, bass.ds(n, 1), k]).then_inc(h_full, 1)

                def q_gate(n, par, pair):
                    act.wait_ge(mm["q"], 2 * n + pair + 1)
                    act.activation(Q[par][:, 4 * pair:4 * pair + 4, :], bank[2 + pair][:, :].rearrange("p (g t) -> p g t", t=P),
                                   ACT.Sigmoid).then_inc(q_sig, 1)

                def k_and_f(n, par, pair):
                    act.wait_ge(mm["k"], 2 * n + pair + 1)
                    act.activation(K[par][:, 4 * pair:4 * pair + 4, :].rearrange("p g t -> p (g t)"), bank[4 + pair][:, :], ACT.Sigmoid)
                    act.activation(f[:, 4 * pair:4 * pair + 4, :].rearrange("p g t -> p (g t)"), bank[4 + pair][:, :],
                                   ACT.Sigmoid, scale=-1.0).then_inc(k_f, 1)

                def v_copy(n, par, ch):
                    act.wait_ge(mm["v"], 2 * n + ch + 1)
                    act.copy(V[par][:, ch, :], bank[ch][:, :]).then_inc(v_sb, 1)

                def g1_high(n):
                    act.wait_ge(mm["g1"], n + 1)
                    act.copy(g1[0][:, :], bank[2][:, 0:TB]).then_inc(g1_hi, 1)

                def gate(n, par, ch):
                    wait(act, sto_s, 2 * (n - 1))
                    act.wait_ge(mm["gate"], 2 * n + ch + 1)
                    act.activation(og[par][:, ch, :], bank[ch][:, :], ACT.Sigmoid).then_inc(gate_sb, 1)

                def start():
                    for n, src in enumerate((env["W_r"], env["W_k"])):
                        act.dma_start(ffn_raw[n][:, :, :], src.rearrange("(k p) n -> p k n", p=P)).then_inc(w_in, 16)
                    h_affine(0)
                    for pair in range(2):
                        q_gate(0, 0, pair)
                    for pair in range(2):
                        k_and_f(0, 0, pair)
                    for ch in range(NC):
                        v_copy(0, 0, ch)
                    g1_high(0)
                    for ch in range(NC):
                        gate(0, 0, ch)
                    h_affine(1)

                def body(half, par, has_next, has_next2, has_prev):
                    n = 2 * half + par
                    if has_prev:
                        for ch in range(NC):
                            act.wait_ge(mm["t2"], 2 * (n - 1) + ch + 1)
                            act.copy(ogT[0][:, ch, :, :].rearrange("p k t -> p (k t)"), bank[ch][:, :]).then_inc(ogt_hi, 1)
                    if has_next:
                        for pair in range(2):
                            q_gate(n + 1, 1 - par, pair)
                        for pair in range(2):
                            k_and_f(n + 1, 1 - par, pair)
                        v_copy(n + 1, 1 - par, 0)
                    act.wait_ge(mm["lvl"], NL * n + 7)
                    act.wait_ge(merged, NM * (n + 1))
                    src = level_bank(6).rearrange("p (g t) -> p g t", g=G)
                    for q in range(2):
                        last = act.copy(A[64 * q:64 * q + 32, :, 64 * q + 32:64 * q + 64],
                                        src[64 * q:64 * q + 32, :, 32 * q:32 * q + 32])
                    last.then_inc(merged_act, 1)
                    if has_next:
                        v_copy(n + 1, 1 - par, 1)
                    act.wait_ge(mm["lvl"], NL * n + 8)
                    act.copy(A[0:64, :, 64:128], level_bank(7).rearrange("p (g t) -> p g t", g=G)[0:64, :, :]).then_inc(merged_act, 1)
                    if has_next:
                        g1_high(n + 1)
                    for ch in range(NC):
                        act.wait_ge(mm["kt"], 2 * n + ch + 1)
                        act.copy(Kt[:, ch, :, :].rearrange("p h t -> p (h t)"), bank[4 + ch][:, :]).then_inc(kt_sb, 1)
                    if has_next:
                        for ch in range(NC):
                            gate(n + 1, 1 - par, ch)
                    if has_next2:
                        h_affine(n + 2)

                run(act, start, body)
                for ch in range(NC):
                    act.wait_ge(mm["t2"], 2 * (NB - 1) + ch + 1)
                    act.copy(ogT[0][:, ch, :, :].rearrange("p k t -> p (k t)"), bank[ch][:, :]).then_inc(ogt_hi, 1)

            @block.vector
            def _(dve):
                def h_high(n):
                    dve.wait_ge(h_full, 4 * (n + 1))
                    dve.tensor_copy(hT[0][:, :, :], hF[:, :, :]).then_inc(h_hi, 1)

                def q_silu(n, par, pair):
                    dve.wait_ge(q_sig, 2 * n + pair + 1)
                    dst = Q[par][:, 4 * pair:4 * pair + 4, :]
                    dve.scalar_tensor_tensor(out=dst, in0=bank[2 + pair][:, :].rearrange("p (g t) -> p g t", t=P), scalar=QSCALE, in1=dst,
                                             op0=ALU.mult, op1=ALU.mult).then_inc(q_sb, 1)

                def f_signed(n, par, pair):
                    dve.wait_ge(k_f, 2 * n + pair + 1)
                    dst = f[:, 4 * pair:4 * pair + 4, :].rearrange("p g t -> p (g t)")
                    wait(dve, f_sb, 2 * n + pair)
                    dve.tensor_scalar(eq[:, :], dst, 0.5, 2.0, ALU.is_equal, ALU.mult).then_inc(f_eq, 1)
                    dve.wait_ge(f_eq, 2 * n + pair + 1)
                    dve.scalar_tensor_tensor(out=dst, in0=eq[:, :], scalar=-1.0, in1=dst,
                                             op0=ALU.add, op1=ALU.mult).then_inc(f_sb, 1)

                def q_odd(n, par):
                    dve.wait_ge(f_sb, 2 * (n + 1))
                    dve.wait_ge(q_sb, 2 * (n + 1))
                    dve.tensor_tensor(out=Qo[par], in0=Q[par][:, :, 1::2], in1=f[:, :, 1::2], op=ALU.mult).then_inc(qodd, 1)

                def g1_low(n):
                    dve.wait_ge(g1_hi, n + 1)
                    dve.tensor_tensor(out=g1[1][:, :], in0=bank[2][:, 0:TB], in1=g1[0][:, :].bitcast(F32),
                                      op=ALU.subtract).then_inc(g1_lo, 1)

                def ogt_low(n, ch):
                    dve.wait_ge(ogt_hi, 2 * n + ch + 1)
                    dve.tensor_tensor(out=ogT[1][:, ch, :, :].rearrange("p k t -> p (k t)"), in0=bank[ch][:, :],
                                      in1=ogT[0][:, ch, :, :].rearrange("p k t -> p (k t)").bitcast(F32),
                                      op=ALU.subtract).then_inc(ogt_lo, 1)

                def wo_scale(n, ch, b):
                    dve.wait_ge(mm["wo"], 2 * n + ch + 1)
                    dve.wait_ge(rstdo, n + 1)
                    wait(dve, x2_sb, 2 * (n - 1) + ch + 1)
                    dve.scalar_tensor_tensor(out=y[:, ch, :], in0=bank[3 - 2 * ch][:, :], scalar=rso[:, ch:ch + 1],
                                             in1=gab[:, bass.ds(b, 1), :].rearrange("p a e -> p (a e)"),
                                             op0=ALU.mult, op1=ALU.mult).then_inc(y_sb, 1)

                def tots(par, m):
                    cnt = G * P // m
                    off = G * P - 2 * cnt
                    t = f[:, :, :].rearrange("p g t -> p (g t)") if m == 1 else Tot[:, off:off + cnt]
                    return t.rearrange("p (n two) -> p n two", two=2)

                def level_update(n, par, m, idx, has_next2):
                    nb = G * P // (2 * m)
                    t = tots(par, m)
                    if m == 1:
                        dve.wait_ge(mm["lvl"], NL * n + 2)
                        dve.wait_ge(qodd, n + 1)
                        dve.wait_ge(merged, NM * n + 1)
                        tq, tk = Q[par].rearrange("p g (n two) -> p g n two", two=2), K[par][:, :, 0::2]
                        fe = f[:, :, 0::2]
                        dve.tensor_tensor(out=tq[:, :, :, 1], in0=Qo[par], in1=fe, op=ALU.mult)
                        dve.tensor_tensor(out=tq[:, :, :, 0], in0=tq[:, :, :, 0], in1=fe, op=ALU.mult)
                        dve.tensor_tensor(out=tk, in0=tk, in1=f[:, :, 1::2], op=ALU.mult).then_inc(level, 1)
                        first_merge(0).then_inc(merged, 1)
                        diagonal(1)
                        diagonal(2).then_inc(merged, 1)
                        dve.wait_ge(merged, NM * n + 3)
                        dve.tensor_tensor(out=Tot[:, 0:G * P // 2].rearrange("p (g n) -> p g n", g=G), in0=fe,
                                          in1=f[:, :, 1::2], op=ALU.mult)
                        first_merge(1)
                        first_merge(2).then_inc(merged, 1)
                        return
                    cnt2 = G * P // (2 * m)
                    off2 = G * P - 2 * cnt2
                    dve.wait_ge(mm["lvl"], NL * n + idx + 1)
                    dve.wait_ge(level, NU * n + idx - 1)
                    if idx <= 5:
                        dve.wait_ge(merged, NM * n + idx + 2)
                    if m == 64 and has_next2:
                        dve.wait_ge(ln["stat"], n + 3)
                    dve.tensor_tensor(out=Tot[:, off2:off2 + cnt2], in0=t[:, :, 0], in1=t[:, :, 1], op=ALU.mult)
                    q = Q[par].rearrange("p g (n two m) -> p g n two m", two=2, m=m)[:, :, :, 1, :]
                    tq = t[:, :, 0:1].rearrange("p (g n) one -> p g n one", g=G).to_broadcast([P, G, nb // G, m])
                    k = K[par][:, :, :].rearrange("p g t -> p (g t)").rearrange("p (n two m) -> p n two m", two=2, m=m)[:, :, 0, :]
                    dve.tensor_tensor(out=q, in0=q, in1=tq, op=ALU.mult)
                    dve.tensor_tensor(out=k, in0=k, in1=t[:, :, 1:2].to_broadcast([P, nb, m]), op=ALU.mult).then_inc(level, 1)

                def level_merge(n, m, idx):
                    nb = 64 // m
                    dst = A[:, :, :].rearrange("p g (n two m) -> p g n two m", two=2, m=m)[:, :, :, 1, :]
                    src = level_bank(idx).rearrange("p (g n m) -> p g n m", g=G, m=m)
                    msk = masks[:, idx - 1, :].rearrange("p (n m) -> p n m", m=m).unsqueeze(1).to_broadcast([P, G, nb, m])
                    dve.copy_predicated(dst, msk, src).then_inc(merged, 1)

                def diagonal(part):
                    groups, src = NEAR[part]
                    nb = src.shape[1]
                    return dve.tensor_tensor(out=A[:, groups, :].rearrange("p (b g) t -> p b g t", b=nb),
                                             in0=src.rearrange("p b (g t) -> p b g t", g=2)[:, :, :, 0:P],
                                             in1=ident[:, :].unsqueeze(1).unsqueeze(1).to_broadcast([P, nb, 2, P]), op=ALU.mult)

                def first_merge(part):
                    groups, src = NEAR[part]
                    nb = src.shape[1]
                    return dve.copy_predicated(A[:, groups, :].rearrange("p (b g) (n two) -> p b g n two", b=nb, two=2)[:, :, :, :, 1],
                                               masks[:, 0, :].unsqueeze(1).unsqueeze(1).to_broadcast([P, nb, 2, P // 2]),
                                               src.rearrange("p b (g t) -> p b g t", g=2)[:, :, :, P:P + P // 2])

                def gated_var(n):
                    for ch in range(NC):
                        last = dve.bn_aggr(mvo[:, ch, :], sto[:, ch, :])
                    last.then_inc(varo, 1)
                    dve.wait_ge(varo, n + 1)
                    dve.tensor_scalar(veo[:, :], mvo[:, :, 1], EPS, None, ALU.add).then_inc(ve_o, 1)

                def start():
                    dve.memset(S[0][:, :, :], 0.0)
                    dve.memset(lvl2[:, :], 0.0)
                    ln_stats(dve, ln, 1, 0, 1)
                    dve.wait_ge(ln["stat"], 2)
                    ln_var(dve, ln, 1)
                    h_high(0)
                    dve.wait_ge(mm["t1"], 2)
                    ln_apply(dve, ln, 1)
                    for pair in range(2):
                        q_silu(0, 0, pair)
                    for pair in range(2):
                        f_signed(0, 0, pair)
                    q_odd(0, 0)
                    g1_low(0)
                    h_high(1)

                def body(half, par, has_next, has_next2, has_prev):
                    n = 2 * half + par
                    prev_b = (n - 1) // BPB if has_prev else 0
                    dve.wait_ge(mm["lvl"], NL * n + 1)
                    wait(dve, sto_s, 2 * n)
                    wait(dve, mm["o"], 2 * n)
                    wait(dve, merged_act, 2 * n)
                    diagonal(0).then_inc(merged, 1)
                    if has_prev:
                        gated_var(n - 1)
                    for idx, m in enumerate(LEVELS, 1):
                        level_update(n, par, m, idx, has_next2)
                        if m == 1 and has_prev:
                            ogt_low(n - 1, 0)
                            ogt_low(n - 1, 1)
                        if 1 < m <= 16:
                            level_merge(n, m, idx)
                        if has_next and m in (2, 4):
                            q_silu(n + 1, 1 - par, m // 4)
                        if has_next and m in (8, 16):
                            f_signed(n + 1, 1 - par, m // 16)
                        if has_next and m == 16:
                            q_odd(n + 1, 1 - par)
                        if has_next2 and m == 32:
                            ln_stats(dve, ln, n + 2, half + 1, par)
                        if has_next2 and m == 64:
                            ln_var(dve, ln, n + 2)
                    if has_next2:
                        dve.wait_ge(mm["t1"], 2 * (n + 2))
                        ln_apply(dve, ln, n + 2)
                    if has_next:
                        g1_low(n + 1)
                    if has_prev:
                        wo_scale(n - 1, 0, prev_b)
                    def gated(ch):
                        dve.wait_ge(mm["o"], 2 * n + ch + 1)
                        dve.wait_ge(gate_sb, 2 * n + ch + 1)
                        dve.tensor_tensor(out=og[par][:, ch, :], in0=bank[2][:, :], in1=og[par][:, ch, :], op=ALU.mult).then_inc(og_sb, 1)

                    def gated_stats(ch):
                        dve.wait_ge(og_sb, 2 * n + ch + 1)
                        dve.bn_stats(sto[:, ch, :], og[par][:, ch, :]).then_inc(sto_s, 1)

                    gated(0)
                    dve.wait_ge(mm["ds"], 2 * n + 1)
                    dve.wait_ge(level, NU * (n + 1))
                    wait(dve, s_flag, n)
                    tot = Tot[:, G * P - 2 * G:G * P - G].rearrange("p (h c) -> p h c", c=NC)
                    for h in range(H):
                        last = dve.scalar_tensor_tensor(out=S[1][:, h, :], in0=S[0][:, h, :], scalar=tot[:, h, 0:1],
                                                        in1=bank[3][:, h * P:(h + 1) * P], op0=ALU.mult, op1=ALU.add)
                    last.then_inc(s_mid, 1)
                    dve.wait_ge(mm["ds"], 2 * n + 2)
                    dve.wait_ge(s_mid, n + 1)
                    for h in range(H):
                        last = dve.scalar_tensor_tensor(out=S[0][:, h, :], in0=S[1][:, h, :], scalar=tot[:, h, 1:2],
                                                        in1=bank[4][:, h * P:(h + 1) * P], op0=ALU.mult, op1=ALU.add)
                    last.then_inc(s_new, 1)
                    dve.wait_ge(s_new, n + 1)
                    dve.tensor_scalar(S[0][:, :, :], S[0][:, :, :], flags[:, bass.ds(n + 1, 1)], None, ALU.mult).then_inc(s_flag, 1)
                    gated_stats(0)
                    if has_next2:
                        h_high(n + 2)
                    if has_prev:
                        wo_scale(n - 1, 1, prev_b)
                    gated(1)
                    gated_stats(1)

                run(dve, start, body)
                dve.wait_ge(sto_s, 2 * NB)
                gated_var(NB - 1)
                for ch in range(NC):
                    ogt_low(NB - 1, ch)
                ln_stats(dve, ln2, 0, 0, 0)
                dve.wait_ge(ln2["stat"], 1)
                ln_var(dve, ln2, 0)
                dve.wait_ge(mm["t1"], 2 * NB)
                ln_apply(dve, ln2, 0)
                for ch in range(NC):
                    wo_scale(NB - 1, ch, B - 1)

            @block.tensor
            def _(pe):
                def product(dst, lhs, rhs, steps):
                    terms = [(a, b, s) for s in range(steps) for a, b in ((0, 0), (0, 1), (1, 0))]
                    for t, (a, b, s) in enumerate(terms):
                        last = pe.matmul(dst, lhs(a, s), rhs(b, s), start=(t == 0), stop=(t == len(terms) - 1))
                    return last

                def t1(n):
                    pe.wait_ge(ln["xn_ready"], n + 1)
                    for k in range(KT):
                        for ch in range(NC):
                            col = (k % 2) * TB + ch * P
                            last = pe.transpose(bank[5 - 5 * (k // 2)][:, col:col + P], xn[:, ch, k * P:(k + 1) * P], ident[:, :])
                        if k % 2:
                            last.then_inc(mm["t1"], 1)

                def rows_of(name, pair, first, key):
                    for o in range(2):
                        h = 2 * pair + o
                        last = product(bank[first + pair][:, o * TB:(o + 1) * TB],
                                       lambda a, s: W[name][a][:, s, h * P:(h + 1) * P], lambda b, s: hT[b][:, s, :], KT)
                    last.then_inc(mm[key], 1)

                def v_rows(ch):
                    product(bank[ch][:, :], lambda a, s: hT[a][:, s, ch * P:(ch + 1) * P],
                            lambda b, s: W["v"][b][:, s, :], KT).then_inc(mm["v"], 1)

                def g1_rows():
                    product(bank[2][:, 0:TB], lambda a, s: W["g1"][a][:, s, :], lambda b, s: hT[b][:, s, :], KT).then_inc(mm["g1"], 1)

                def gate_rows(ch):
                    product(bank[ch][:, :], lambda a, s: g1[a][:, ch * P:(ch + 1) * P],
                            lambda b, s: W["g2"][b][:, s, :], 1).then_inc(mm["gate"], 1)

                def t2(n, par, ch):
                    pe.wait_ge(og_sb, 2 * n + ch + 1)
                    for k in range(KT):
                        last = pe.transpose(bank[ch][:, k * P:(k + 1) * P], og[par][:, ch, k * P:(k + 1) * P], ident[:, :])
                    last.then_inc(mm["t2"], 1)

                def wo_rows(n, ch):
                    pe.wait_ge(ogt_lo, 2 * n + ch + 1)
                    product(bank[3 - 2 * ch][:, :], lambda a, s: ogT[a][:, ch, s, :],
                            lambda b, s: W["o"][b][:, s, :], KT).then_inc(mm["wo"], 1)

                def start():
                    t1(0)
                    pe.wait_ge(h_lo, 1)
                    for pair in range(2):
                        rows_of("q", pair, 2, "q")
                    pe.wait_ge(h_full, 4)
                    for pair in range(2):
                        rows_of("k", pair, 4, "k")
                    for ch in range(NC):
                        v_rows(ch)
                    pe.wait_ge(q_sb, 1)
                    g1_rows()
                    pe.wait_ge(g1_lo, 1)
                    pe.wait_ge(v_sb, 2)
                    for ch in range(NC):
                        gate_rows(ch)
                    pe.wait_ge(k_f, 2)
                    pe.wait_ge(gate_sb, 1)
                    t1(1)

                def body(half, par, has_next, has_next2, has_prev):
                    n = 2 * half + par
                    q, k = Q[par], K[par]

                    def level_product(idx):
                        m = LEVELS[idx - 1]
                        pe.wait_ge(level, NU * n + idx - 1)
                        pe.wait_ge(merged, NM * n + (2 if idx <= 3 else idx + 1))
                        dst = level_bank(idx)
                        for g in range(G):
                            if m <= 16:
                                for b in range(2):
                                    part = dst[64 * b:64 * b + 64, g * 64 + 32 * b:g * 64 + 32 * b + 32]
                                    tokens = slice(64 * b, 64 * b + 64)
                                    rhs = q[:, g, tokens].rearrange("p (n two m) -> p n two m", two=2, m=m)[:, :, 1, :]
                                    last = pe.matmul(part.rearrange("p (n m) -> p n m", m=m), k[:, g, tokens], rhs,
                                                     start=True, stop=True)
                            elif m == 32:
                                for b in range(2):
                                    last = pe.matmul(dst[64 * b:64 * b + 32, g * 64 + 32 * b:g * 64 + 32 * b + 32],
                                                     k[:, g, 64 * b:64 * b + 32], q[:, g, 64 * b + 32:64 * b + 64], start=True, stop=True)
                            else:
                                last = pe.matmul(dst[0:64, g * 64:(g + 1) * 64], k[:, g, 0:64], q[:, g, 64:128], start=True, stop=True)
                        last.then_inc(mm["lvl"], 1)

                    pe.wait_ge(q_sb, 2 * (n + 1))
                    pe.wait_ge(k_f, 2 * (n + 1))
                    pe.wait_ge(qodd, n + 1)
                    wait(pe, merged_act, 2 * n)
                    wait(pe, s_new, n)
                    for part, (groups, dst) in enumerate(NEAR):
                        for g in range(groups.start, groups.stop):
                            o = g - groups.start
                            last = pe.matmul(dst[:, o // 2, 3 * P // 2 * (o % 2):3 * P // 2 * (o % 2 + 1)], k[:, g, :],
                                             Qx[par][:, g, :], start=True, stop=True)
                        if part != 1:
                            last.then_inc(mm["lvl"], 1)
                    if has_prev:
                        if has_next:
                            pe.wait_ge(h_full, 4 * (n + 2))
                        t2(n - 1, 1 - par, 0)
                        wait(pe, y_sb, 2 * (n - 1))
                        t2(n - 1, 1 - par, 1)
                    if has_next:
                        pe.wait_ge(h_lo, n + 2)
                        wait(pe, og_sb, 2 * n)
                        rows_of("q", 0, 2, "q")
                    level_product(2)
                    if has_next:
                        pe.wait_ge(merged, NM * n + 4)
                        rows_of("q", 1, 2, "q")
                    else:
                        pe.wait_ge(merged, NM * n + 4)
                        wo_rows(n - 1, 0)
                    level_product(3)
                    if has_next:
                        rows_of("k", 0, 4, "k")
                    else:
                        wo_rows(n - 1, 1)
                    level_product(4)
                    if has_next:
                        pe.wait_ge(h_full, 4 * (n + 2))
                        rows_of("k", 1, 4, "k")
                    level_product(5)
                    if has_next:
                        pe.wait_ge(gate_sb, 2 * (n + 1))
                        wait(pe, ogt_lo, 2 * n)
                        v_rows(0)
                    level_product(6)
                    if has_next:
                        v_rows(1)
                    level_product(7)
                    if has_next:
                        pe.wait_ge(q_sb, 2 * (n + 2))
                        g1_rows()
                    if has_prev and has_next:
                        wait(pe, s_mid, n)
                        wo_rows(n - 1, 0)
                    pe.wait_ge(level, NU * (n + 1))
                    if has_next:
                        pe.wait_ge(k_f, 2 * (n + 2))
                    for ch in range(NC):
                        for h in range(H):
                            last = pe.transpose(bank[4 + ch][:, h * P:(h + 1) * P], k[:, h * NC + ch, :], ident[:, :])
                        last.then_inc(mm["kt"], 1)
                    if has_next:
                        pe.wait_ge(g1_lo, n + 2)
                        for ch in range(NC):
                            pe.wait_ge(v_sb, 2 * (n + 1) + ch + 1)
                            gate_rows(ch)

                    def output(ch):
                        for h in range(H):
                            g = h * NC + ch
                            pe.matmul(bank[2][:, h * P:(h + 1) * P], q[:, g, :], S[ch][:, h, :], start=True, stop=False)
                            last = pe.matmul(bank[2][:, h * P:(h + 1) * P], A[:, g, :], V[par][:, ch, h * P:(h + 1) * P],
                                             start=False, stop=True)
                        last.then_inc(mm["o"], 1)

                    pe.wait_ge(merged_act, 2 * (n + 1))
                    wait(pe, s_flag, n)
                    pe.wait_ge(v_sb, 2 * (n + 1))
                    if has_next:
                        pe.wait_ge(g1_lo, n + 2)
                    output(0)
                    if has_prev:
                        pe.wait_ge(y_sb, 2 * (n - 1) + 1)
                    elif has_next:
                        pe.wait_ge(q_sb, 2 * (n + 2))
                    for ch in range(NC):
                        pe.wait_ge(kt_sb, 2 * n + ch + 1)
                        if ch == 1:
                            pe.wait_ge(kt_sb, 2 * n + 1)
                        for h in range(H):
                            last = pe.matmul(bank[3 + ch][:, h * P:(h + 1) * P], Kt[:, ch, h, :], V[par][:, ch, h * P:(h + 1) * P],
                                             start=True, stop=True)
                        last.then_inc(mm["ds"], 1)
                    if has_next2:
                        pe.wait_ge(kt_sb, 2 * (n + 1))
                        pe.wait_ge(gate_sb, 2 * (n + 1) + 1)
                        t1(n + 2)
                    if has_prev and has_next:
                        pe.wait_ge(gate_sb, 2 * (n + 2))
                        wo_rows(n - 1, 1)
                    pe.wait_ge(s_mid, n + 1)
                    pe.wait_ge(og_sb, 2 * n + 1)
                    output(1)

                run(pe, start, body)
                pe.wait_ge(y_sb, 2 * (NB - 1))
                for ch in range(NC):
                    t2(NB - 1, (NB - 1) % 2, ch)
                for ch in range(NC):
                    pe.wait_ge(s_mid, NB)
                    if ch == 1:
                        pe.wait_ge(ogt_lo, 2 * NB)
                    wo_rows(NB - 1, ch)


def ffn(nc, sb, sem, wait, env):
    ident, flags, mhalf = (env[n] for n in ("ident", "flags", "mhalf"))
    gab, scl, sft, x2d, of = (env[n] for n in ("gab", "scl", "sft", "x2d", "of"))
    bank8 = env["bank"] + env["lbank"]
    ffn_raw, w_in = env["ffn_raw"], env["w_in"]
    mur, muk = (env["vec"][:, (B + n) * KT:(B + n + 1) * KT] for n in (1, 2))
    KK, TT, RR, FV = bank8[0:2], bank8[2:4], bank8[4:6], bank8[6:8]
    with ExitStack() as ctx:
        W = {n: [sb(ctx, f"f{n}_{part}", [P, KT, E], F32R) for part in ("hi", "lo")] for n in "rkv"}
        raw = {"r": ffn_raw[0], "k": ffn_raw[1], "v": sb(ctx, "v_raw", [P, KT, E])}
        v_in = sem(ctx, "v_in")
        TURNS = [(name, u) for name in "krv" for u in range(KT)]
        TURN_BANK = [bank8[n] for n in (0, 1, 6, 7, 4, 5, 6, 7, 6, 7, 6, 7)]
        ln, x2_out, xs, xn = (env[n] for n in ("ln2", "x2_out", "xs", "xn"))
        tick = sb(ctx, "ftick", [P, 1])
        ticked = sem(ctx, "fticked")
        h2 = sb(ctx, "h2", [P, KT, TB + 1])
        dd = sb(ctx, "dd", [P, KT, TB])
        xk32 = sb(ctx, "xk32", [P, KT, TB])
        xr32 = sb(ctx, "xr32", [P, KT, TB])
        xk = [sb(ctx, f"xk_{part}", [P, KT, TB], F32R) for part in ("hi", "lo")]
        xr = [sb(ctx, f"xr_{part}", [P, KT, TB], F32R) for part in ("hi", "lo")]
        rl = sb(ctx, "rl", [P, KT, TB])
        ka = [sb(ctx, f"ka_{part}", [P, KT, TB], F32R) for part in ("hi", "lo")]
        r = sb(ctx, "r", [P, NC, E])
        x_out = [sem(ctx, f"fx_out{n}") for n in range(2)]
        wt, wt_hi, wt_lo = sem(ctx, "wt"), sem(ctx, "wt_hi"), sem(ctx, "wt_lo")
        mm = {n: sem(ctx, f"fmm_{n}") for n in ("t", "k", "r", "v")}
        relu, ka_hi, h_sb, r_sig, xk_hi, xr_hi = (sem(ctx, n) for n in ("relu", "ka_hi", "h_sb", "r_sig", "xk_hi", "xr_hi"))
        halo, diff, xk_f, xr_f, xk_lo, xr_lo, sq, ka_lo, rv = (
            sem(ctx, n) for n in ("halo", "diff", "xk_f", "xr_f", "xk_lo", "xr_lo", "sq", "ka_lo", "rv"))
        r_gb, x3 = (sem(ctx, n) for n in ("r_gb", "x3"))

        def run(eng, start, body):
            start()
            body(0, 0, True, True, False)
            body(0, 1, True, True, True)
            with eng.Fori(1, NB // 2 - 1) as half:
                body(half, 0, True, True, True)
                body(half, 1, True, True, True)
            body(NB // 2 - 1, 0, True, False, True)
            body(NB // 2 - 1, 1, False, False, True)

        with nc.Block() as block:
            @block.sync
            def _(sp):
                def store(n, par):
                    wait(sp, x3, 2 * (n + 1))
                    sp.dma_start(of[rows(n), :].rearrange("(c p) e -> p c e", p=P),
                                 xs[:, slot(n), :].rearrange("p a (c e) -> p (a c) e", c=NC)).then_inc(x_out[par], 16)

                def start():
                    for q in range(2):
                        sp.wait_ge(x2_out[q], 16 * (NB // 2))

                def body(half, par, has_next, has_next2, has_prev):
                    n = 2 * half + par
                    if has_next2:
                        wait(sp, x_out[par], 16 * half)
                        sp.wait_ge(ln["stat"], n + 1)
                        ln_load(sp, ln, x2d, n + 2, par)
                    if has_prev:
                        store(n - 1, 1 - par)

                run(sp, start, body)
                store(NB - 1, (NB - 1) % 2)
                for q in range(2):
                    sp.wait_ge(x_out[q], 16 * (NB // 2))

            @block.gpsimd
            def _(pool):
                def carry(ticks):
                    wait(pool, ticked, ticks)
                    pool.tensor_tensor(out=tick[:, :], in0=mhalf[:, 0:1], in1=mhalf[:, 0:1], op=ALU.mult).then_inc(ticked, 1)

                def start():
                    ln_rstd(pool, ln, mhalf, 1)

                def body(half, par, has_next, has_next2, has_prev):
                    n = 2 * half + par
                    if has_next2:
                        ln_rstd(pool, ln, mhalf, n + 2)
                    for ch in range(NC):
                        pool.wait_ge(r_sig, 2 * n + ch + 1)
                        carry(4 * n + ch)
                        pool.tensor_tensor(out=r[:, ch, :], in0=r[:, ch, :],
                                           in1=gab[:, bass.ds(n // BPB + B, 1), :].rearrange("p a e -> p (a e)"),
                                           op=ALU.mult).then_inc(r_gb, 1)
                    for ch in range(NC):
                        pool.wait_ge(rv, 2 * n + ch + 1)
                        carry(4 * n + 2 + ch)
                        pool.tensor_tensor(out=chunk(ln, n, ch), in0=chunk(ln, n, ch), in1=r[:, ch, :], op=ALU.add).then_inc(x3, 1)

                run(pool, start, body)

            @block.scalar
            def _(act):
                def h_affine(n):
                    wait(act, halo, n + 1)
                    for k in range(KT):
                        if k % 2 == 0:
                            act.wait_ge(mm["t"], 2 * n + k // 2 + 1)
                        last = act.activation(h2[:, k, 1:TB + 1], TT[k // 2][:, (k % 2) * TB:(k % 2 + 1) * TB], ACT.Identity,
                                              scale=scl[1][:, bass.ds(n, 1), k], bias=sft[1][:, bass.ds(n, 1), k])
                    last.then_inc(h_sb, 1)

                def high(n, name):
                    ready, used, part, full, done = ((xk_f, "k", xk, xk32, xk_hi) if name == "k" else
                                                     (xr_f, "r", xr, xr32, xr_hi))
                    act.wait_ge(ready, n + 1)
                    wait(act, mm[used], 2 * n)
                    act.copy(part[0][:, :, :], full[:, :, :]).then_inc(done, 1)

                def weights_high(turns):
                    for t in turns:
                        name, u = TURNS[t]
                        act.wait_ge(wt, t + 1)
                        act.copy(W[name][0][:, u, :], TURN_BANK[t][:, :]).then_inc(wt_hi, 1)

                def start():
                    act.dma_start(raw["v"][:, :, :], env["W_v"].rearrange("(k p) n -> p k n", p=P)).then_inc(v_in, 16)
                    h_affine(0)
                    weights_high(range(0, 4))
                    high(0, "k")
                    weights_high(range(4, 8))
                    high(0, "r")

                def body(half, par, has_next, has_next2, has_prev):
                    n = 2 * half + par
                    for pair in range(2):
                        act.wait_ge(mm["k"], 2 * n + pair + 1)
                        wait(act, ka_lo, 2 * n)
                        act.activation(rl[:, 2 * pair:2 * pair + 2, :].rearrange("p k t -> p (k t)"), KK[pair][:, :],
                                       ACT.Relu).then_inc(relu, 1)
                    if not has_prev:
                        weights_high(range(8, 10))
                    for pair in range(2):
                        act.wait_ge(sq, 2 * n + pair + 1)
                        wait(act, mm["v"], 2 * n)
                        act.copy(ka[0][:, 2 * pair:2 * pair + 2, :], rl[:, 2 * pair:2 * pair + 2, :]).then_inc(ka_hi, 1)
                    if has_next:
                        h_affine(n + 1)
                    if not has_prev:
                        weights_high(range(10, 12))
                    for ch in range(NC):
                        act.wait_ge(mm["r"], 2 * n + ch + 1)
                        wait(act, x3, 2 * n)
                        act.activation(r[:, ch, :], RR[ch][:, :], ACT.Sigmoid).then_inc(r_sig, 1)
                    if has_next:
                        high(n + 1, "k")
                        high(n + 1, "r")

                run(act, start, body)

            @block.vector
            def _(dve):
                def shift(n, name):
                    if name == "k":
                        dve.wait_ge(h_sb, n + 1)
                        dve.tensor_tensor(out=dd[:, :, :], in0=h2[:, :, 1:TB + 1], in1=h2[:, :, 0:TB], op=ALU.subtract).then_inc(diff, 1)
                        dve.wait_ge(diff, n + 1)
                    dst, mu, s = (xk32, muk, xk_f) if name == "k" else (xr32, mur, xr_f)
                    for k in range(KT):
                        last = dve.scalar_tensor_tensor(out=dst[:, k, :], in0=dd[:, k, :], scalar=mu[:, k:k + 1],
                                                        in1=h2[:, k, 0:TB], op0=ALU.mult, op1=ALU.add)
                    last.then_inc(s, 1)
                    if name == "r":
                        dve.wait_ge(xr_f, n + 1)
                        dve.tensor_scalar(h2[:, :, 0:1], h2[:, :, TB:TB + 1], flags[:, bass.ds(n + 1, 1)], None,
                                          ALU.mult).then_inc(halo, 1)

                def low(n, name):
                    part, full, hi_s, lo_s = (xk, xk32, xk_hi, xk_lo) if name == "k" else (xr, xr32, xr_hi, xr_lo)
                    dve.wait_ge(hi_s, n + 1)
                    dve.tensor_tensor(out=part[1][:, :, :], in0=full[:, :, :], in1=part[0][:, :, :].bitcast(F32),
                                      op=ALU.subtract).then_inc(lo_s, 1)

                def weights_low(turns):
                    for t in turns:
                        name, u = TURNS[t]
                        hi, lo = W[name]
                        dve.wait_ge(wt_hi, t + 1)
                        dve.tensor_tensor(out=lo[:, u, :], in0=TURN_BANK[t][:, :], in1=hi[:, u, :].bitcast(F32),
                                          op=ALU.subtract).then_inc(wt_lo, 1)

                def start():
                    dve.memset(h2[:, :, 0:1], 0.0).then_inc(halo, 1)
                    shift(0, "k")
                    weights_low(range(0, 4))
                    low(0, "k")
                    shift(0, "r")
                    weights_low(range(4, 8))
                    low(0, "r")
                    ln_stats(dve, ln, 1, 0, 1)
                    dve.wait_ge(ln["stat"], 2)
                    ln_var(dve, ln, 1)
                    dve.wait_ge(mm["t"], 2)
                    ln_apply(dve, ln, 1)

                def body(half, par, has_next, has_next2, has_prev):
                    n = 2 * half + par
                    for pair in range(2):
                        part = rl[:, 2 * pair:2 * pair + 2, :]
                        dve.wait_ge(relu, 2 * n + pair + 1)
                        dve.tensor_tensor(out=part, in0=part, in1=part, op=ALU.mult).then_inc(sq, 1)
                    if not has_prev:
                        weights_low(range(8, 10))
                    for pair in range(2):
                        part = rl[:, 2 * pair:2 * pair + 2, :]
                        dve.wait_ge(ka_hi, 2 * n + pair + 1)
                        dve.tensor_tensor(out=ka[1][:, 2 * pair:2 * pair + 2, :], in0=part,
                                          in1=ka[0][:, 2 * pair:2 * pair + 2, :].bitcast(F32), op=ALU.subtract).then_inc(ka_lo, 1)
                    if not has_prev:
                        weights_low(range(10, 12))
                    if has_next2:
                        ln_stats(dve, ln, n + 2, half + 1, par)
                    if has_next:
                        if has_next2:
                            dve.wait_ge(ln["stat"], n + 3)
                        shift(n + 1, "k")
                        shift(n + 1, "r")
                        if has_next2:
                            ln_var(dve, ln, n + 2)
                        low(n + 1, "k")
                        low(n + 1, "r")
                    if has_next2:
                        dve.wait_ge(mm["t"], 2 * (n + 2))
                        ln_apply(dve, ln, n + 2)
                    for ch in range(NC):
                        dve.wait_ge(mm["v"], 2 * n + ch + 1)
                        dve.wait_ge(r_gb, 2 * n + ch + 1)
                        dve.tensor_tensor(out=r[:, ch, :], in0=FV[ch][:, :], in1=r[:, ch, :], op=ALU.mult).then_inc(rv, 1)

                run(dve, start, body)

            @block.tensor
            def _(pe):
                def product(dst, lhs, rhs, steps):
                    terms = [(a, b, s) for s in range(steps) for a, b in ((0, 0), (0, 1), (1, 0))]
                    for t, (a, b, s) in enumerate(terms):
                        last = pe.matmul(dst, lhs(a, s), rhs(b, s), start=(t == 0), stop=(t == len(terms) - 1))
                    return last

                def transposes(n):
                    pe.wait_ge(ln["xn_ready"], n + 1)
                    wait(pe, h_sb, n)
                    for k in range(KT):
                        for ch in range(NC):
                            col = (k % 2) * TB + ch * P
                            last = pe.transpose(TT[k // 2][:, col:col + P], xn[:, ch, k * P:(k + 1) * P], ident[:, :])
                        if k % 2:
                            last.then_inc(mm["t"], 1)

                def turn(turns):
                    for t in turns:
                        name, u = TURNS[t]
                        if t >= 6:
                            pe.wait_ge(wt_lo, {6: 3, 7: 4, 8: 7, 9: 8, 10: 9, 11: 10}[t])
                        for d in range(KT):
                            last = pe.transpose(TURN_BANK[t][:, d * P:(d + 1) * P], raw[name][:, d, u * P:(u + 1) * P], ident[:, :])
                        last.then_inc(wt, 1)

                def start():
                    transposes(0)
                    pe.wait_ge(w_in, 32)
                    turn(range(0, 8))
                    pe.wait_ge(wt_lo, 4)

                def body(half, par, has_next, has_next2, has_prev):
                    n = 2 * half + par
                    pe.wait_ge(xk_lo, n + 1)
                    for d in range(KT):
                        if d % 2 == 0:
                            wait(pe, relu, 2 * (n - 1) + d // 2 + 1)
                        last = product(KK[d // 2][:, (d % 2) * TB:(d % 2 + 1) * TB],
                                       lambda a, s: W["k"][a][:, s, d * P:(d + 1) * P], lambda b, s: xk[b][:, s, :], KT)
                        if d % 2:
                            last.then_inc(mm["k"], 1)
                    if not has_prev:
                        pe.wait_ge(v_in, 16)
                        turn(range(8, 10))
                    if has_next:
                        transposes(n + 1)
                    if not has_prev:
                        turn(range(10, 12))
                    pe.wait_ge(xr_lo, n + 1)
                    for ch in range(NC):
                        wait(pe, r_sig, 2 * (n - 1) + ch + 1)
                        product(RR[ch][:, :], lambda a, s: xr[a][:, s, ch * P:(ch + 1) * P],
                                lambda b, s: W["r"][b][:, s, :], KT).then_inc(mm["r"], 1)
                    pe.wait_ge(ka_lo, 2 * (n + 1))
                    if not has_prev:
                        pe.wait_ge(wt_lo, 3 * KT)
                    for ch in range(NC):
                        wait(pe, rv, 2 * (n - 1) + ch + 1)
                        product(FV[ch][:, :], lambda a, s: ka[a][:, s, ch * P:(ch + 1) * P],
                                lambda b, s: W["v"][b][:, s, :], KT).then_inc(mm["v"], 1)

                run(pe, start, body)


_INS = ['L0_attn_x', 'L0_attn_wq', 'L0_attn_wk', 'L0_attn_wv', 'L0_attn_wo', 'L0_attn_wg1', 'L0_attn_wg2', 'L0_attn_norm_w',
        'L0_ffn_W_r', 'L0_ffn_W_k', 'L0_ffn_W_v', 'L0_ffn_mu_r', 'L0_ffn_mu_k', 'L0_c', 'L0_wmod']


def kernel(**inputs):
    import numpy as _np
    import concourse.bacc as _bacc
    from concourse import mybir as _mybir
    from concourse.bass_utils import run_bass_kernel_spmd as _run

    nc = _bacc.Bacc("TRN2", target_bir_lowering=False, num_devices=1)
    arrays, args = {}, []
    for name in _INS:
        a = _np.ascontiguousarray(inputs[name])
        arrays[f"in_{name}"] = a
        args.append(nc.dram_tensor(f"in_{name}", a.shape, _mybir.dt.from_np(a.dtype), kind="ExternalInput").ap())
    args.append(nc.dram_tensor("out_0", (B, T, E), _mybir.dt.float32, kind="ExternalOutput").ap())
    adaln_kernel(nc, *args)
    r = _run(nc, [arrays], core_ids=[0])
    return r.results[0]["out_0"]
```
